# Optimizing a Trainium2 kernel written in Bass

```python
import numpy as np
import jax
import jax.numpy as jnp

def _softmax(x, axis=-1):
    return jax.nn.softmax(x, axis=axis)

def _gelu(x):
    return jax.nn.gelu(x, approximate=True)

def _silu(x):
    return jax.nn.silu(x)

def _sigmoid(x):
    return jax.nn.sigmoid(x)

def _layernorm(x, axis=-1, eps=1e-05):
    m = jnp.mean(x, axis=axis, keepdims=True)
    v = jnp.var(x, axis=axis, keepdims=True)
    return (x - m) / jnp.sqrt(v + eps)

def _scatter_add(tgt, idx, src, axis=0):
    return tgt.at[idx].add(src)

def _segment_sum(src, seg, n):
    return jax.ops.segment_sum(src, seg, n)
kernel_name = 'mk_gnn_ffn_d1_gnn_r8_b33e7b'

def setup_inputs(seed: int=0):
    np.random.seed(seed)
    _w = jnp.asarray

    def _rec_inputs():
        import jax
        import jax.numpy as jnp
        _gk = jax.random.key(seed)
        x = -0.0002117 + 1 * jax.random.normal(jax.random.fold_in(_gk, 1), (12500, 256), jnp.float32)
        src = jax.random.randint(jax.random.fold_in(_gk, 2), (200000,), 0, 12500, jnp.int32)
        dst = jax.random.randint(jax.random.fold_in(_gk, 3), (200000,), 0, 12500, jnp.int32)
        _o = jnp.argsort(dst, stable=True)
        src = src[_o]
        dst = dst[_o]
        return (x, src, dst)
    x, src, dst = _rec_inputs()

    def _L0_gnn_setup():
        import jax, jax.numpy as jnp
        import numpy as np
        N = 12500
        E = 200000
        IN = 256
        H = 4
        C = 64
        key = jax.random.key(seed)
        k1, k2, k3, k4, k5, k6 = jax.random.split(key, 6)
        x = jax.random.normal(k1, (N, IN), dtype=jnp.float32)
        edge_index = jax.random.randint(k2, (2, E), 0, N, dtype=jnp.int64)
        W = jax.random.normal(k3, (IN, H * C), dtype=jnp.float32) * (1.0 / np.sqrt(IN))
        att_src = jax.random.normal(k4, (H, C), dtype=jnp.float32) * 0.1
        att_dst = jax.random.normal(k5, (H, C), dtype=jnp.float32) * 0.1
        bias = jax.random.normal(k6, (H * C,), dtype=jnp.float32) * 0.01
        return {'x': x, 'edge_index': edge_index, 'W': W, 'att_src': att_src, 'att_dst': att_dst, 'bias': bias}
    _L0_gnn_all = _L0_gnn_setup()
    _L0_gnn_in = {k: v for k, v in _L0_gnn_all.items() if k in ('W', 'att_src', 'att_dst', 'bias')}
    del _L0_gnn_all

    def _L0_ffn_setup():
        import jax, jax.numpy as jnp
        import numpy as np
        B, S, D = (8, 512, 256)
        H = 4 * D
        CAPACITY = 0.5
        key = jax.random.key(seed)
        ks = jax.random.split(key, 6)
        x = jax.random.normal(ks[0], (B, S, D), dtype=jnp.float32)
        attention_mask = jnp.zeros((B, 1, 1, S), dtype=jnp.float32)
        wr = jax.random.normal(ks[1], (D, 1), dtype=jnp.float32) * 0.02
        br = jnp.zeros((1,), dtype=jnp.float32)
        w1 = jax.random.normal(ks[2], (D, H), dtype=jnp.float32) * 0.02
        b1 = jnp.zeros((H,), dtype=jnp.float32)
        w2 = jax.random.normal(ks[3], (H, D), dtype=jnp.float32) * 0.02
        b2 = jnp.zeros((D,), dtype=jnp.float32)
        return {'x': x, 'attention_mask': attention_mask, 'wr': wr, 'br': br, 'w1': w1, 'b1': b1, 'w2': w2, 'b2': b2}
    _L0_ffn_all = _L0_ffn_setup()
    _L0_ffn_in = {k: v for k, v in _L0_ffn_all.items() if k in ('attention_mask', 'wr', 'br', 'w1', 'b1', 'w2', 'b2')}
    del _L0_ffn_all
    return {'x': x, 'src': src, 'dst': dst, 'L0_gnn_W': _L0_gnn_in['W'], 'L0_gnn_att_src': _L0_gnn_in['att_src'], 'L0_gnn_att_dst': _L0_gnn_in['att_dst'], 'L0_gnn_bias': _L0_gnn_in['bias'], 'L0_ffn_attention_mask': _L0_ffn_in['attention_mask'], 'L0_ffn_wr': _L0_ffn_in['wr'], 'L0_ffn_br': _L0_ffn_in['br'], 'L0_ffn_w1': _L0_ffn_in['w1'], 'L0_ffn_b1': _L0_ffn_in['b1'], 'L0_ffn_w2': _L0_ffn_in['w2'], 'L0_ffn_b2': _L0_ffn_in['b2']}

def reference(x, src, dst, L0_gnn_W, L0_gnn_att_src, L0_gnn_att_dst, L0_gnn_bias, L0_ffn_attention_mask, L0_ffn_wr, L0_ffn_br, L0_ffn_w1, L0_ffn_b1, L0_ffn_w2, L0_ffn_b2):
    import jax
    import jax.numpy as jnp

    def _L0_gnn_ref(x, edge_index, W, att_src, att_dst, bias):
        import jax, jax.numpy as jnp
        import numpy as np
        N = 12500
        E = 200000
        IN = 256
        H = 4
        C = 64
        n = x.shape[0]
        loops = jnp.arange(n, dtype=edge_index.dtype)
        src = jnp.concatenate([edge_index[0], loops])
        dst = jnp.concatenate([edge_index[1], loops])
        xp = (x @ W).reshape(n, H, C)
        a_src = jnp.einsum('nhc,hc->nh', xp, att_src)
        a_dst = jnp.einsum('nhc,hc->nh', xp, att_dst)
        alpha = jax.nn.leaky_relu(a_src[src] + a_dst[dst], negative_slope=0.2)
        amax = jax.ops.segment_max(alpha, dst, num_segments=n)
        amax = jnp.where(jnp.isfinite(amax), amax, 0.0)
        ex = jnp.exp(alpha - amax[dst])
        denom = jax.ops.segment_sum(ex, dst, num_segments=n)
        w = ex / denom[dst]
        msg = xp[src] * w[..., None]
        agg = jax.ops.segment_sum(msg, dst, num_segments=n)
        out = agg.reshape(n, H * C) + bias
        return jax.nn.elu(out)

    def _L0_ffn_ref(x, attention_mask, wr, br, w1, b1, w2, b2):
        import jax, jax.numpy as jnp
        import numpy as np
        B, S, D = (8, 512, 256)
        H = 4 * D
        CAPACITY = 0.5
        b, s, d = x.shape
        weights = (jnp.einsum('bsd,do->bso', x, wr) + br)[..., 0]
        k = max(1, int(CAPACITY * s))
        kk = k - 1 if k > 1 else 1
        _, idx = jax.lax.top_k(weights, k)
        sel_idx = idx[:, :kk]
        sel = jnp.take_along_axis(x, sel_idx[:, :, None], axis=1)
        h = jax.nn.gelu(jnp.einsum('bkd,dh->bkh', sel, w1) + b1)
        y = jnp.einsum('bkh,hd->bkd', h, w2) + b2
        w_sel = jnp.take_along_axis(weights, sel_idx, axis=1)
        y = y * w_sel[..., None]
        batch_idx = jnp.arange(b)[:, None]
        processed = jnp.zeros_like(x).at[batch_idx, sel_idx].set(y)
        return processed + x
    edge_index = jnp.stack([src, dst])
    x = x + _L0_gnn_ref(_layernorm(x, axis=-1), edge_index, L0_gnn_W, L0_gnn_att_src, L0_gnn_att_dst, L0_gnn_bias)
    x = x + _L0_ffn_ref(_layernorm(x, axis=-1)[None], L0_ffn_attention_mask, L0_ffn_wr, L0_ffn_br, L0_ffn_w1, L0_ffn_b1, L0_ffn_w2, L0_ffn_b2)[0]
    return x

_drawn_inputs = setup_inputs


def setup_inputs(seed=0):
    import zlib

    import numpy as np

    out = dict(_drawn_inputs(seed))
    spreads = {'L0_ffn_b1': (0.0, 0.8), 'L0_ffn_b2': (0.0, 0.724)}
    factors = {'L0_gnn_bias': 6.141, 'L0_ffn_wr': 3.815, 'L0_ffn_w1': 4.547, 'L0_ffn_w2': 4.25}
    for name, (base, spread) in spreads.items():
        noise = np.random.default_rng([zlib.crc32(name.encode()), seed]).standard_normal(out[name].shape)
        drawn = base * np.exp(spread * noise) if base else spread * noise
        out[name] = jnp.asarray(drawn.astype(out[name].dtype))
    for name, factor in factors.items():
        out[name] = (out[name] * factor).astype(out[name].dtype)
    return out
```

```python
from contextlib import ExitStack

import concourse.bass as bass
from concourse import mybir

F32 = mybir.dt.float32
BF16 = mybir.dt.bfloat16
I32 = mybir.dt.int32
I16 = mybir.dt.int16
ALU = mybir.AluOpType
ACT = mybir.ActivationFunctionType
AXX = mybir.AxisListType.X

P = 128
EPS = 1e-5
SLOPE = 0.2
BLOCK = 32
SPREAD = 40.0


def sizes(n, e):
    nw = -(-n // P)
    tiles = -(-e // n) + 1
    ep = -(-(e + P * (tiles + 1)) // (P * BLOCK)) * P * BLOCK
    return nw, tiles, ep


def build(nc, x, src, dst, W, att_src, att_dst, gbias, wr, br, w1, b1, w2, b2, out, N, E):
    D = W.shape[0]
    H, C = att_src.shape
    F = w1.shape[1]
    NW, TILES, EP = sizes(N, E)
    BATCH = 7
    PAIRS = NW // 2
    TURNS = NW // BATCH // 2
    K = max(1, int(0.5 * N)) - 1
    ROW = D + H
    DC, FC = D // P, F // P
    NB = NW // BATCH
    VK = 2 * H * 3
    EPP = EP // P
    BPP = EPP // BLOCK
    NBLK = EP // BLOCK
    FLAT = TILES * P
    FB = FLAT // BLOCK
    PB = P // BLOCK
    ROUNDS = 2 * 8 + 2
    FREED = 6
    IN_BANK = 512 // P
    assert NW % 2 == 0 and NW % (2 * BATCH) == 0 and DC == 2 and TILES * VK <= 512
    PIECES = []
    at = 0
    for size in (1, 2, 2, 3, 3, 3, 3, 3, 3, 3):
        if at < TILES:
            PIECES.append((at, min(size, TILES - at)))
            at += size
    NP = len(PIECES)
    piece_of = {t: n for n, (a, m) in enumerate(PIECES) for t in range(a, a + m)}

    with ExitStack() as ctx:
        def sb(name, shape, dt=F32):
            return ctx.enter_context(nc.sbuf_tensor(name, shape, dt))

        def ps(name, shape):
            return ctx.enter_context(nc.psum_tensor(name, shape, F32))

        def sem(name):
            return ctx.enter_context(nc.semaphore(name))

        def sem2(name):
            return [sem(f"{name}{b}") for b in range(2)]

        table = nc.dram_tensor("node_rows", (NW * P, ROW), F32).ap()
        y_dram = nc.dram_tensor("ffn_rows", (NW * P, D), F32).ap()
        dst16_dram = nc.dram_tensor("dst16", (EP,), I16).ap()
        blk_dram = nc.dram_tensor("block_range", (2, NBLK), F32).ap()
        win_dram = nc.dram_tensor("window_table", (NW, 5), I32).ap()

        ident = sb("ident", [P, P])
        ones = sb("ones", [P, P])
        below = sb("below", [P, P])
        iota_d = sb("iota_d", [P, P])
        node_id = sb("node_id", [P, NW])
        base_id = sb("base_id", [P, NW])
        w1s = sb("w1s", [P, DC, F])
        w2s = sb("w2s", [P, FC, D])
        b1s = sb("b1s", [P, FC])
        b2s = sb("b2s", [P, D])
        gbs = sb("gbs", [P, D])
        wrs = sb("wrs", [P, D])
        brs = sb("brs", [P, 1])
        base = sb("base", [P, NW, D])
        parts = sb("parts", [P, NW, 2 * H, 3], BF16)
        exself = sb("exself", [P, NW, H])
        wt = sb("wt", [P, NW])
        win = sb("win", [1, 5 * NW], I32)
        rows = sb("rows", [P, 2, TILES, ROW])
        srci = sb("srci", [P, 2, TILES], I32)
        dsti = sb("dsti", [P, 2, TILES], I32)
        dbc = sb("dbc", [P, 2, FLAT], I16)
        oht = dbc[:, :, :].bitcast(BF16)
        oh = sb("oh", [P, 2, TILES, P])
        dloc = sb("dloc", [P, TILES])
        edge_dm = sb("edge_dm", [P, TILES, 2 * H])
        zz = sb("zz", [P, TILES, 2, H])
        zl = sb("zl", [P, TILES, 2, H])
        diff = sb("diff", [P, TILES, H])
        selfr = sb("selfr", [P, 2, ROW])
        rden = sb("rden", [P, H])
        zag = sb("zag", [P, D])
        zmin = sb("zmin", [P, D])
        zexp = sb("zexp", [P, D])
        xn = sb("xn", [P, D])
        junk = zexp
        xnT = sb("xnT", [P, DC, P])
        hT = sb("hT", [P, FC, P])
        yb = sb("yb", [P, 2, D])
        st6 = sb("st6", [P, 6])
        mv = sb("mv", [P, 2])
        lnv = sb("lnv", [P, 1])
        rs0 = sb("rs0", [P, 1])
        rs1 = sb("rs1", [P, 1])
        rstd = sb("rstd", [P, 1])
        vareps = sb("vareps", [P, 1])
        sq = sb("sq", [P, 1])
        half = sb("half", [P, 1])
        wcol = sb("wcol", [P, 2])
        xsrc = sb("xsrc", [P, 1], I32)
        xdst = sb("xdst", [P, 1], I32)
        xdbc = sb("xdbc", [P, P], I16)
        xrow = sb("xrow", [P, ROW])
        xoh = sb("xoh", [P, P])
        xoht = sb("xoht", [P, P], BF16)
        xloc = sb("xloc", [P, 1])
        xdm = sb("xdm", [P, 2 * H])
        xzz = sb("xzz", [P, 2, H])
        xzl = sb("xzl", [P, 2, H])
        xdiff = sb("xdiff", [P, H])

        xmax = sb("xmax", [P, H])

        BD = BATCH * D
        WIDE = ROW + H
        rows_flat = rows[:, :, :, :].rearrange("p a t c -> p (a t c)")
        base_flat = base[:, :, :].rearrange("p w c -> p (w c)")
        oh_flat = oh[:, :, :, :].rearrange("p a t c -> p (a t c)")

        def batch(flat, at, width):
            return flat[:, at:at + BATCH * width].rearrange("p (g c) -> p g c", g=BATCH)

        xb = [batch(rows_flat, b * BD, D) for b in range(2)]
        nb = [batch(rows_flat, (2 + b) * BD, D) for b in range(2)]
        yin = [batch(rows_flat, k * BD, D) for k in range(4)]
        lo_b = base_flat[0:NW, 0:NBLK]
        hi_b = base_flat[0:NW, NBLK:2 * NBLK]
        pos = base_flat[0:NW, 2 * NBLK:3 * NBLK]
        po = [batch(base_flat, 3 * NBLK + b * BATCH * WIDE, WIDE) for b in range(2)]
        assert 3 * NBLK + 2 * BATCH * WIDE <= NW * D and 4 * BD + 2 * NW * 2 * H <= 2 * TILES * ROW
        asd, dm = (rows_flat[:, 4 * BD + k * NW * 2 * H:4 * BD + (k + 1) * NW * 2 * H].rearrange("p (w v) -> p w v", w=NW) for k in range(2))
        left = rows_flat[:, 0:NW * 2 * H].rearrange("p (w v) -> p w v", w=NW)
        sz, sm = (rows_flat[:, (2 + k) * NW * H:(3 + k) * NW * H].rearrange("p (w v) -> p w v", w=NW) for k in range(2))
        wext = hT[:, :, :].rearrange("p m q -> p (m q)")[:, 0:DC * WIDE].rearrange("p (c n) -> p c n", c=DC)
        xpen = oh_flat[:, 0:P]
        xmask = oh_flat[:, P:(1 + H) * P].rearrange("p (h e) -> p h e", h=H)
        key, sgn, khi, klo, tie, above, col, rank, coef, valid, *marks = (oh_flat[:, k * NW:(k + 1) * NW] for k in range(13))
        key, sgn = key.bitcast(I32), sgn.bitcast(I32)
        dst_all = oh_flat[:, 0:EPP].bitcast(I32)
        dst16 = dbc[:, 0, 0:EPP]
        bmin = oh_flat[:, EPP:EPP + BPP]
        bmax = oh_flat[:, EPP + BPP:EPP + 2 * BPP]
        xnT2 = dbc[:, 1, 0:4 * D].bitcast(F32).rearrange("p (a c q) -> p a c q", a=2, c=DC)
        att_b = [zag[:, :], zmin[:, :]]
        st_b = sb("st_b", [P, BATCH, 6])
        mv_b = sb("mv_b", [P, 2, BATCH, 2])
        rs_b = sb("rs_b", [P, 2, BATCH])
        minus_half = sb("minus_half", [P, BATCH])
        gmax = sb("gmax", [P, 2 * H])
        gall = sb("gall", [P, 2 * H])
        spread = sb("spread", [P, H])
        widest = sb("widest", [P, 1])
        exact = sb("exact", [P, 1], I32)
        wv = sb("wv", [P, 8])
        wi = sb("wi", [P, 5], I32)
        count_f = sb("count_f", [P, 2])
        i1 = sb("i1", [P, 2], I32)
        i2 = sb("i2", [P, 2], I32)
        thr = sb("thr", [P, 3])
        cnt = sb("cnt", [P, 3])
        got = sb("got", [P, 3])
        nge = sb("nge", [P, 1])
        cur = sb("cur", [P, 1])
        kth = sb("kth", [P, 1])

        lk_ps = ps("lk_ps", [P, 512])
        ag_ps = [ps(f"ag_ps{b}", [P, 512]) for b in range(2)]
        tr_ps = ps("tr_ps", [P, 512])
        h_ps = ps("h_ps", [P, 1024])
        y_ps = ps("y_ps", [P, 512])
        xl_ps = ps("xl_ps", [P, 512])
        tr2 = [t[:, 0:D].rearrange("p (c q) -> p c q", c=DC) for t in (tr_ps, xl_ps)]

        def sems(names):
            return [sem(n) for n in names.split()]

        dst_ld, att_ld, w_ld, d16_st, blk_st, blk_ld, win_st, win_ld = sems(
            "dst_ld att_ld w_ld d16_st blk_st blk_ld win_st win_ld")
        x_ld, tab_st = sem2("x_ld"), sem2("tab_st")
        (pool_const, d16_ok, blk_ok, wext_ok, stat_ok, aggr_ok, vareps_b, rstd_b, norm_ok, trb_ok, trc_ok, xp_ok, xpc_ok, asd_ok,
         mask_ok, desc_ok, count_ok, before_ok, win_ok, gmax_ok, gall_ok, exact_ok, sdiff_ok, exself_ok, parts_ok,
         pre) = sems(
            "pool_const d16_ok blk_ok wext_ok stat_ok aggr_ok vareps_b rstd_b norm_ok trb_ok trc_ok xp_ok xpc_ok asd_ok "
            "mask_ok desc_ok count_ok before_ok win_ok gmax_ok gall_ok exact_ok sdiff_ok exself_ok parts_ok pre")
        ld_src, ld_dst, ld_dbc, ld_self, ld_x, gath, y_st = (
            sem2(n) for n in ("ld_src", "ld_dst", "ld_dbc", "ld_self", "ld_x", "gath", "y_st"))
        (oht_ok, loc_ok, oh_ok, lk_ok, dm_ok, zs_ok, zm_ok, zl_ok, diff_ok, ex_ok, scaled, tile_done, agg_ok, selfx_ok,
         self_ok, rden_ok, zn_ok, zb_ok, zmin_ok, zexp_ok, xa_ok, x1_ok, st_ok, mv_ok, ln_ok, rs0_ok, ve_ok, sq_ok,
         half_ok, rstd_ok, xn_ok, base_ok, wcol_ok, wt_ok, tr_ok, xnT_ok, h_ok, hT_ok, y_ok, yb_ok) = sems(
            "oht_ok loc_ok oh_ok lk_ok dm_ok zs_ok zm_ok zl_ok diff_ok ex_ok scaled tile_done agg_ok selfx_ok "
            "self_ok rden_ok zn_ok zb_ok zmin_ok zexp_ok xa_ok x1_ok st_ok mv_ok ln_ok rs0_ok ve_ok sq_ok "
            "half_ok rstd_ok xn_ok base_ok wcol_ok wt_ok tr_ok xnT_ok h_ok hT_ok y_ok yb_ok")
        (x_src, x_dst, x_dbc, x_row, x_oht, x_loc, x_oh, x_lk, x_dm, x_zs, x_zm, x_zl, x_diff, x_ex, x_exc, x_sc,
         x_done) = sems(
            "x_src x_dst x_dbc x_row x_oht x_loc x_oh x_lk x_dm x_zs x_zm x_zl x_diff x_ex x_exc x_sc x_done")
        m_src, m_dst, m_row, m_loc, m_oh, m_pen, m_mask, m_tr, m_max, m_done = sems(
            "m_src m_dst m_row m_loc m_oh m_pen m_mask m_tr m_max m_done")
        step_ok, cnt_ok, tot_ok, tie_ok, rank_ok, out_ok, out_st = sems(
            "step_ok cnt_ok tot_ok tie_ok rank_ok out_ok out_st")
        y_ld = [sem(f"y_ld{k}") for k in range(4)]

        def bc(v, n):
            return v.rearrange("(a n) -> a n", a=1).broadcast_to([P, n])

        def nodes(t, first, count):
            return t[bass.ds(first * P, count * P), :].rearrange("(g p) c -> p g c", p=P)

        def two_by_two(eng, turns, body, last_peeled=False):
            for b in range(2):
                body(b, 0, b)
            with eng.Fori(1, turns - last_peeled) as i:
                for b in range(2):
                    body(2 * i + b, i, b)
            if last_peeled:
                for b in range(2):
                    body(2 * (turns - 1) + b, turns - 1, b)

        def known(n, least):
            return not isinstance(n, int) or n >= least

        def wait_apart(eng, *waits):
            waits = [(semaphore, value if isinstance(value, int) else eng.to_reg(value)) for semaphore, value in waits]
            eng.wait_ge(pool_const, 12)
            for semaphore, value in waits:
                eng.wait_ge(semaphore, value)

        def entry(eng, w, k, most):
            return eng.value_load(win[0:1, bass.ds(5 * w + k, 1)], min_val=0, max_val=most)

        def for_extra(eng, w, body):
            n = entry(eng, w, 1, EP // P)
            before = entry(eng, w, 2, NW * EP // P)
            with eng.If(n > 0):
                with eng.Fori(0, n) as j:
                    body(j, before + j)

        def in_edges(at):
            return nc.s_assert_within(at, 0, EP - P, skip_runtime_bounds_check_because="a window's tiles begin before its last edge")

        def if_exact(eng, body):
            flag = eng.value_load(exact[0:1, 0:1], min_val=0, max_val=1)
            with eng.If(flag > 0):
                with eng.Fori(0, NW) as w:
                    n = entry(eng, w, 3, EP // P)
                    before = entry(eng, w, 4, NW * EP // P)
                    with eng.If(n > 0):
                        with eng.Fori(0, n) as j:
                            body(w, j, before + j)

        block = ctx.enter_context(nc.Block())

        @block.sync
        def _(sp):
            sp.dma_start(dst_all, dst.rearrange("(p e) -> p e", p=P)).then_inc(dst_ld, 16)
            for b in range(2):
                sp.dma_start(xb[b], nodes(x, b * BATCH, BATCH)).then_inc(x_ld[b], 16)
            sp.dma_start(wext[:, :, 0:D], W.rearrange("(c p) n -> p c n", p=P)).then_inc(att_ld, 16)
            sp.dma_start(att_b[0], bc(att_src.rearrange("h c -> (h c)"), D)).then_inc(att_ld, 16)
            sp.dma_start(att_b[1], bc(att_dst.rearrange("h c -> (h c)"), D)).then_inc(att_ld, 16)
            sp.dma_start(w1s[:, :, :], w1.rearrange("(c p) n -> p c n", p=P)).then_inc(w_ld, 16)
            sp.dma_start(w2s[:, :, :], w2.rearrange("(c p) n -> p c n", p=P)).then_inc(w_ld, 16)
            with nc.allow_non_contiguous_dma("a bias by column of the hidden layer"):
                sp.dma_start(b1s[:, :], b1.rearrange("(c p) -> p c", p=P)).then_inc(w_ld, 16)
            sp.dma_start(b2s[:, :], bc(b2, D)).then_inc(w_ld, 16)
            sp.dma_start(gbs[:, :], bc(gbias, D)).then_inc(w_ld, 16)
            sp.dma_start(wrs[:, :], bc(wr.rearrange("d o -> (d o)"), D)).then_inc(w_ld, 16)
            sp.dma_start(brs[:, :], bc(br, 1)).then_inc(w_ld, 16)
            sp.wait_ge(d16_ok, 1)
            sp.dma_start(dst16_dram.rearrange("(p e) -> p e", p=P), dst16).then_inc(d16_st, 16)
            sp.wait_ge(blk_ok, 2)
            sp.dma_start(blk_dram[0, :].rearrange("(p n) -> p n", p=P), bmin).then_inc(blk_st, 16)
            sp.dma_start(blk_dram[1, :].rearrange("(p n) -> p n", p=P), bmax).then_inc(blk_st, 16)
            sp.wait_ge(blk_st, 32)
            sp.dma_start(lo_b, blk_dram[0:1, :].broadcast_to([NW, NBLK])).then_inc(blk_ld, 16)
            sp.dma_start(hi_b, blk_dram[1:2, :].broadcast_to([NW, NBLK])).then_inc(blk_ld, 16)

            def store_rows(g, b):
                wait_apart(sp, (xpc_ok, BATCH * (g + 1)))
                sp.dma_start(nodes(table, g * BATCH, BATCH), po[b][:, :, 0:ROW]).then_inc(tab_st[b], 16)

            def batch_io(g, i, b):
                if known(g, 1):
                    store_rows(g - 1, 1 - b)
                if not isinstance(g, int) or g + 2 < NB:
                    wait_apart(sp, (norm_ok, g + 1))
                    sp.dma_start(xb[b], nodes(x, (g + 2) * BATCH, BATCH)).then_inc(x_ld[b], 16)

            two_by_two(sp, TURNS, batch_io, last_peeled=True)
            store_rows(NB - 1, 1)
            sp.wait_ge(win_ok, 1)
            sp.dma_start(win_dram, wi[0:NW, :]).then_inc(win_st, 16)
            sp.wait_ge(win_st, 16)
            sp.dma_start(win[:, :], win_dram.rearrange("(a w) c -> a (w c)", a=1)).then_inc(win_ld, 16)
            sp.wait_ge(win_ld, 16)
            sp.wait_ge(d16_st, 16)
            for b in range(2):
                sp.wait_ge(tab_st[b], 16 * TURNS)
            sp.wait_ge(exact_ok, 1)

            def exact_loads(w, j, k):
                first = in_edges(entry(sp, w, 0, EP - FLAT) + j * P)
                wait_apart(sp, (m_done, k + 1))
                with nc.allow_non_contiguous_dma("an edge to a partition"):
                    sp.dma_start(xsrc[:, :], src[bass.ds(first, P)].rearrange("(p t) -> p t", t=1)).then_inc(m_src, 16)
                    sp.dma_start(xdst[:, :], dst[bass.ds(first, P)].rearrange("(p t) -> p t", t=1)).then_inc(m_dst, 16)

            if_exact(sp, exact_loads)

            def window(w, i, b):
                first = entry(sp, w, 0, EP - FLAT)
                if known(w, 2):
                    wait_apart(sp, (gath[b], 16 * TILES * i), (oh_ok, w - 1), (agg_ok, w - 1), (lk_ok, w - 1))
                sp.dma_start(srci[:, b, :], src[bass.ds(first, FLAT)].rearrange("(p t) -> p t", t=TILES)).then_inc(ld_src[b], 16)
                sp.dma_start(dbc[:, b, :], dst16_dram[bass.ds(first, FLAT)].rearrange("(a e) -> a e", a=1).broadcast_to([P, FLAT])).then_inc(ld_dbc[b], 16)
                sp.dma_start(dsti[:, b, :], dst[bass.ds(first, FLAT)].rearrange("(p t) -> p t", t=TILES)).then_inc(ld_dst[b], 16)
                sp.dma_start(selfr[:, b, :], table[bass.ds(w * P, P), :]).then_inc(ld_self[b], 16)
                sp.dma_start(base[:, bass.ds(w, 1), :].rearrange("p w c -> p (w c)"), x[bass.ds(w * P, P), :]).then_inc(ld_x[b], 16)

                def extra_loads(j, k):
                    at = in_edges(first + FLAT + j * P)
                    wait_apart(sp, (x_done, k + 1))
                    with nc.allow_non_contiguous_dma("an edge to a partition"):
                        sp.dma_start(xsrc[:, :], src[bass.ds(at, P)].rearrange("(p t) -> p t", t=1)).then_inc(x_src, 16)
                        sp.dma_start(xdst[:, :], dst[bass.ds(at, P)].rearrange("(p t) -> p t", t=1)).then_inc(x_dst, 16)
                    sp.dma_start(xdbc[:, :], dst16_dram[bass.ds(at, P)].rearrange("(a e) -> a e", a=1).broadcast_to([P, P])).then_inc(x_dbc, 16)

                for_extra(sp, w, extra_loads)

            two_by_two(sp, PAIRS, window)
            sp.wait_ge(agg_ok, NW)
            for b in range(2):
                sp.wait_ge(y_st[b], 16 * PAIRS)
            for g in range(NB + 4):
                if g >= 4:
                    sp.wait_ge(out_ok, g - 3)
                    sp.dma_start(nodes(out, (g - 4) * BATCH, BATCH), base[:, (g - 4) * BATCH:(g - 3) * BATCH, :]).then_inc(out_st, 16)
                if g < NB:
                    sp.dma_start(yin[g % 4], nodes(y_dram, g * BATCH, BATCH)).then_inc(y_ld[g % 4], 16)
            sp.wait_ge(out_st, 16 * NB)

        @block.gpsimd
        def _(pool):
            nc.gpsimd.memset(ident[:, :], 0.0).then_inc(pool_const, 1)
            nc.gpsimd.memset(below[:, :], 1.0).then_inc(pool_const, 1)
            nc.gpsimd.memset(ones[:, :], 1.0).then_inc(pool_const, 1)
            nc.gpsimd.memset(minus_half[:, :], -0.5).then_inc(pool_const, 1)
            pool.wait_ge(pool_const, 4)
            nc.gpsimd.affine_select(out=ident[:, :], in_=ident[:, :], compare_op=ALU.not_equal, fill=1.0, base=0,
                                    pattern=[[-1, P]], channel_multiplier=1).then_inc(pool_const, 1)
            nc.gpsimd.affine_select(out=below[:, :], in_=below[:, :], compare_op=ALU.is_gt, fill=0.0, base=0,
                                    pattern=[[1, P]], channel_multiplier=-1).then_inc(pool_const, 1)

            def count(dst_ap, pattern, base_, by_partition):
                nc.gpsimd.iota(dst_ap, pattern=pattern, base=base_, channel_multiplier=by_partition,
                               allow_small_or_imprecise_dtypes=True).then_inc(pool_const, 1)

            count(iota_d[:, :], [[1, P]], 0, 0)
            count(node_id[:, :], [[P, NW]], 0, 1)
            count(base_id[:, :], [[P, NW]], 0, 0)
            count(wv[0:NW, 0:1], [[0, 1]], 0, P)
            count(wv[0:NW, 1:2], [[0, 1]], P - 1, P)
            count(pos, [[1, NBLK]], 1, 0)

            def rstd_batch(g, i, b):
                wait_apart(pool, (aggr_ok, g + 1), *([(norm_ok, g - 1)] if known(g, 2) else []))
                nc.gpsimd.tensor_scalar(rs_b[:, b, :], mv_b[:, b, :, 1], EPS, None, ALU.add).then_inc(vareps_b, 1)
                wait_apart(pool, (vareps_b, g + 1))
                nc.gpsimd.tensor_tensor(rs_b[:, b, :], rs_b[:, b, :], minus_half[:, :], ALU.pow).then_inc(rstd_b, 1)

            two_by_two(pool, TURNS, rstd_batch)
            pool.wait_ge(mask_ok, 1)
            nc.gpsimd.iota(hi_b, pattern=[[-1, NBLK]], base=NBLK, channel_multiplier=0,
                           allow_small_or_imprecise_dtypes=True).then_inc(desc_ok, 1)
            pool.wait_ge(gmax_ok, 2)
            nc.gpsimd.partition_all_reduce(gall[:, :], gmax[:, :], P, bass.bass_isa.ReduceOp.max).then_inc(gall_ok, 1)
            for b in range(2):
                pool.wait_ge(tab_st[b], 16 * TURNS)
            pool.wait_ge(win_ld, 16)
            pool.wait_ge(exact_ok, 1)

            def exact_gather(w, j, k):
                wait_apart(pool, (m_src, 16 * k + 16))
                pool.indirect_dma_start(out=xrow[:, :], out_offset=None, in_=table,
                                        in_offset=bass.IndirectOffsetOnAxis(ap=xsrc[:, 0:1], axis=0)).then_inc(m_row, 16)

            if_exact(pool, exact_gather)
            pool.wait_ge(sdiff_ok, 1)

            def window(w, i, b):
                pool.wait_ge(ld_src[b], 16 * (i + 1))
                for t in range(TILES):
                    if known(w, 2) and t % FREED == 0:
                        wait_apart(pool, (tile_done, (w - 2) * TILES + min(t + FREED, TILES)))
                    pool.indirect_dma_start(out=rows[:, b, t, :], out_offset=None, in_=table,
                                            in_offset=bass.IndirectOffsetOnAxis(ap=srci[:, b, t:t + 1], axis=0)).then_inc(gath[b], 16)

                def extra_gather(j, k):
                    wait_apart(pool, (x_src, 16 * k + 16))
                    pool.indirect_dma_start(out=xrow[:, :], out_offset=None, in_=table,
                                            in_offset=bass.IndirectOffsetOnAxis(ap=xsrc[:, 0:1], axis=0)).then_inc(x_row, 16)

                for_extra(pool, w, extra_gather)

            two_by_two(pool, PAIRS, window)

        @block.scalar
        def _(act):
            def row_copy(n, g, t, b):
                act.wait_ge(xp_ok, n + 1)
                if t == 0 and known(g, 2):
                    act.wait_ge(tab_st[b], 8 * (g - b))
                    act.wait_ge(asd_ok, g - 1)
                nc.scalar.copy(po[b][:, t, :], ag_ps[(b + t) % 2][:, 0:WIDE]).then_inc(xpc_ok, 1)

            def batch_copies(g, i, b):
                for t in range(BATCH):
                    n = BATCH * g + t
                    act.wait_ge(trb_ok, n + 1)
                    if known(n, 2):
                        act.wait_ge(xp_ok, n - 1)
                    nc.scalar.copy(xnT2[:, (b + t) % 2], tr2[(b + t) % 2]).then_inc(trc_ok, 1)
                    if t >= 1:
                        row_copy(n - 1, g, t - 1, b)
                row_copy(BATCH * g + BATCH - 1, g, BATCH - 1, b)

            two_by_two(act, TURNS, batch_copies)
            act.wait_ge(sdiff_ok, 1)
            nc.scalar.activation(exself[:, :, :], exself[:, :, :], ACT.Exp).then_inc(exself_ok, 1)
            act.wait_ge(win_ld, 16)
            act.wait_ge(w_ld, 16 * 7)

            def turn(w):
                act.wait_ge(tr_ok, w + 1)
                if known(w, 1):
                    act.wait_ge(h_ok, FC * w)
                nc.scalar.copy(xnT[:, :, :], tr2[0]).then_inc(xnT_ok, 1)

            def gelu(w):
                if known(w, 1):
                    act.wait_ge(y_ok, w)
                for m in range(FC):
                    if m % IN_BANK == 0:
                        act.wait_ge(h_ok, FC * w + m + IN_BANK)
                    nc.scalar.activation(hT[:, m, :], h_ps[:, m * P:(m + 1) * P], ACT.Gelu_apprx_tanh, bias=b1s[:, m:m + 1]).then_inc(hT_ok, 1)

            def store(w, b):
                act.wait_ge(yb_ok, w + 1)
                act.dma_start(y_dram[bass.ds(w * P, P), :], yb[:, b, :]).then_inc(y_st[b], 16)

            def window(w, i, b):
                act.wait_ge(diff_ok, w + 1)
                nc.scalar.activation(rows[:, b, :, D:ROW], diff[:, :, :], ACT.Exp).then_inc(ex_ok, 1)
                if known(w, 1):
                    turn(w - 1)

                def extra_exp(j, k):
                    act.wait_ge(x_diff, k + 1)
                    nc.scalar.activation(xrow[:, D:ROW], xdiff[:, :], ACT.Exp).then_inc(x_ex, 1)

                for_extra(act, w, extra_exp)
                act.wait_ge(zmin_ok, w + 1)
                nc.scalar.activation(zexp[:, :], zmin[:, :], ACT.Exp).then_inc(zexp_ok, 1)
                act.wait_ge(ve_ok, w + 1)
                nc.scalar.activation(lnv[:, :], vareps[:, :], ACT.Ln).then_inc(ln_ok, 1)
                act.wait_ge(ln_ok, w + 1)
                nc.scalar.activation(rs0[:, :], lnv[:, :], ACT.Exp, scale=-0.5).then_inc(rs0_ok, 1)
                if known(w, 1):
                    gelu(w - 1)
                if known(w, 2):
                    store(w - 2, b)

            two_by_two(act, PAIRS, window)
            turn(NW - 1)
            gelu(NW - 1)
            store(NW - 2, 0)
            store(NW - 1, 1)

        @block.tensor
        def _(pe):
            pe.sem_inc(x_done, 1)
            pe.sem_inc(m_done, 1)
            pe.wait_ge(pool_const, 6)
            pe.wait_ge(wext_ok, 1)

            def project(n, t, b):
                pe.wait_ge(trc_ok, n + 1)
                if known(n, 2):
                    pe.wait_ge(xpc_ok, n - 1)
                for c in range(DC):
                    last = nc.tensor.matmul(ag_ps[(b + t) % 2][:, 0:WIDE], xnT2[:, (b + t) % 2, c, :], wext[:, c, :],
                                            start=(c == 0), stop=(c == DC - 1))
                last.then_inc(xp_ok, 1)

            def batch_products(g, i, b):
                pe.wait_ge(norm_ok, g + 1)
                for t in range(BATCH):
                    n = BATCH * g + t
                    if known(n, 2):
                        pe.wait_ge(trc_ok, n - 1)
                    for c in range(DC):
                        last = nc.tensor.transpose(tr2[(b + t) % 2][:, c, :], nb[b][:, t, c * P:(c + 1) * P], ident[:, :])
                    last.then_inc(trb_ok, 1)
                    if t >= 1:
                        project(n - 1, t - 1, b)
                project(BATCH * g + BATCH - 1, BATCH - 1, b)

            two_by_two(pe, TURNS, batch_products)
            pe.wait_ge(count_ok, 1)
            nc.tensor.matmul(y_ps[0:NW, 0:2], below[0:NW, 0:NW], count_f[0:NW, :], start=True, stop=True).then_inc(before_ok, 1)
            pe.wait_ge(win_ld, 16)
            pe.wait_ge(exact_ok, 1)

            def exact_turn(w, j, k):
                pe.wait_ge(m_mask, k + 1)
                for h in range(H):
                    last = nc.tensor.transpose(xl_ps[:, h * P:(h + 1) * P], xmask[:, h, :], ident[:, :])
                last.then_inc(m_tr, 1)

            if_exact(pe, exact_turn)
            pe.wait_ge(parts_ok, 3)
            pe.wait_ge(w_ld, 16 * 7)

            def node_parts(w):
                return parts[:, bass.ds(w, 1), :, :].rearrange("p w v k -> p (w v k)")

            def look_up(w, b):
                pe.wait_ge(oht_ok, w + 1)
                if known(w, 1):
                    pe.wait_ge(dm_ok, w)
                by_tile = oht[:, b, :].rearrange("p (e t) -> p t e", t=TILES)
                for t in range(TILES):
                    last = nc.tensor.matmul(lk_ps[:, VK * t:VK * (t + 1)], by_tile[:, t, :], node_parts(w), start=True, stop=True)
                last.then_inc(lk_ok, 1)

            def turn(w):
                pe.wait_ge(xn_ok, w + 1)
                if known(w, 1):
                    pe.wait_ge(xnT_ok, w)
                for c in range(DC):
                    last = nc.tensor.transpose(tr2[0][:, c, :], xn[:, c * P:(c + 1) * P], ident[:, :])
                last.then_inc(tr_ok, 1)

            def ffn(w):
                pe.wait_ge(xnT_ok, w + 1)
                if known(w, 1):
                    pe.wait_ge(hT_ok, FC * w)
                for m in range(FC):
                    for c in range(DC):
                        last = nc.tensor.matmul(h_ps[:, m * P:(m + 1) * P], w1s[:, c, m * P:(m + 1) * P], xnT[:, c, :],
                                                start=(c == 0), stop=(c == DC - 1))
                    last.then_inc(h_ok, 1)
                if known(w, 1):
                    pe.wait_ge(yb_ok, w)
                for m in range(FC):
                    pe.wait_ge(hT_ok, FC * w + m + 1)
                    last = nc.tensor.matmul(y_ps[:, 0:D], hT[:, m, :], w2s[:, m, :], start=(m == 0), stop=(m == FC - 1))
                last.then_inc(y_ok, 1)

            def window(w, i, b):
                pe.wait_ge(oh_ok, w + 1)
                if known(w, 2):
                    pe.wait_ge(zn_ok, w - 1)
                for t in range(TILES):
                    pe.wait_ge(scaled, w * NP + piece_of[t] + 1)
                    nc.tensor.matmul(ag_ps[b][:, 0:ROW], oh[:, b, t, :], rows[:, b, t, :], start=(t == 0), stop=False).then_inc(tile_done, 1)
                    if t == TILES // 2 and known(w, 1):
                        turn(w - 1)

                def extra_products(j, k):
                    pe.wait_ge(x_oht, k + 1)
                    nc.tensor.matmul(xl_ps[:, 0:VK], xoht[:, :], node_parts(w), start=True, stop=True).then_inc(x_lk, 1)
                    pe.wait_ge(x_sc, k + 1)
                    nc.tensor.matmul(ag_ps[b][:, 0:ROW], xoh[:, :], xrow[:, :], start=False, stop=False).then_inc(x_done, 1)

                for_extra(pe, w, extra_products)
                pe.wait_ge(self_ok, w + 1)
                nc.tensor.matmul(ag_ps[b][:, 0:ROW], ident[:, :], selfr[:, b, :], start=False, stop=True).then_inc(agg_ok, 1)
                if not isinstance(w, int) or w + 1 < NW:
                    look_up(w + 1, 1 - b)
                if known(w, 1):
                    ffn(w - 1)

            look_up(0, 0)
            two_by_two(pe, PAIRS, window, last_peeled=True)
            turn(NW - 1)
            ffn(NW - 1)
            for r in range(ROUNDS):
                pe.wait_ge(cnt_ok, r + 1)
                nc.tensor.matmul(lk_ps[:, 0:3], ones[:, :], cnt[:, :], start=True, stop=True).then_inc(tot_ok, 1)
            pe.wait_ge(tie_ok, 1)
            nc.tensor.matmul(lk_ps[:, 0:NW], below[:, :], tie, start=True, stop=True)
            nc.tensor.matmul(xl_ps[:, 0:NW], ones[:, :], tie, start=True, stop=True).then_inc(rank_ok, 1)

        @block.vector
        def _(dve):
            taken = [0]

            def then(ins):
                taken[0] += 1
                ins.then_inc(pre, 1)
                dve.wait_ge(pre, taken[0])

            dve.wait_ge(dst_ld, 16)
            nc.vector.tensor_copy(dst16, dst_all).then_inc(d16_ok, 1)
            by_block = dst_all.rearrange("p (n e) -> p n e", e=BLOCK)
            nc.vector.tensor_reduce(bmin, by_block, AXX, ALU.min).then_inc(blk_ok, 1)
            nc.vector.tensor_reduce(bmax, by_block, AXX, ALU.max).then_inc(blk_ok, 1)
            dve.wait_ge(att_ld, 16 * 3)
            for k in range(2):
                for c in range(DC):
                    then(nc.vector.tensor_tensor(junk[:, :], wext[:, c, 0:D], att_b[k], ALU.mult))
                    ins = nc.vector.tensor_reduce(wext[:, c, ROW - H + k * H:ROW + k * H], junk[:, :].rearrange("p (h c) -> p h c", h=H), AXX, ALU.add)
                    if (k, c) == (1, DC - 1):
                        ins.then_inc(wext_ok, 1)
                    else:
                        then(ins)

            def norm(g, b):
                dve.wait_ge(rstd_b, g + 1)
                if known(g, 2):
                    dve.wait_ge(trb_ok, BATCH * (g - 1))
                for t in range(BATCH):
                    last = nc.vector.tensor_scalar(nb[b][:, t, :], xb[b][:, t, :], mv_b[:, b, t, 0:1], rs_b[:, b, t:t + 1], ALU.subtract, ALU.mult)
                last.then_inc(norm_ok, 1)

            def keep_asd(g, b):
                dve.wait_ge(xpc_ok, BATCH * (g + 1))
                nc.vector.tensor_copy(asd[:, bass.ds(g * BATCH, BATCH), :], po[b][:, :, D:WIDE]).then_inc(asd_ok, 1)

            def batch_stats(g, i, b):
                wait_apart(dve, (x_ld[b], 16 * (i + 1)), *([(aggr_ok, g)] if known(g, 1) else []))
                for t in range(BATCH):
                    last = nc.vector.bn_stats(st_b[:, t, :], xb[b][:, t, :])
                last.then_inc(stat_ok, 1)
                wait_apart(dve, (stat_ok, g + 1))
                for t in range(BATCH):
                    last = nc.vector.bn_aggr(mv_b[:, b, t, :], st_b[:, t, :])
                last.then_inc(aggr_ok, 1)
                if known(g, 1):
                    norm(g - 1, 1 - b)
                if known(g, 2):
                    keep_asd(g - 2, b)
                if isinstance(g, int) and g == 1:
                    dve.wait_ge(pool_const, 12)
                    dve.wait_ge(blk_ld, 32)
                    then(nc.vector.tensor_scalar(lo_b, lo_b, wv[0:NW, 1:2], None, ALU.is_le))
                    nc.vector.scalar_tensor_tensor(out=lo_b, in0=hi_b, scalar=wv[0:NW, 0:1], in1=lo_b, op0=ALU.is_ge, op1=ALU.mult).then_inc(mask_ok, 1)

            two_by_two(dve, TURNS, batch_stats)
            norm(NB - 1, 1)
            keep_asd(NB - 2, 0)
            dve.wait_ge(mask_ok, 1)
            then(nc.vector.tensor_tensor_reduce(pos, lo_b, pos, 1.0, 0.0, ALU.mult, ALU.max, wv[0:NW, 3:4]))
            dve.wait_ge(desc_ok, 1)
            then(nc.vector.tensor_tensor_reduce(hi_b, lo_b, hi_b, 1.0, 0.0, ALU.mult, ALU.max, wv[0:NW, 2:3]))
            then(nc.vector.tensor_scalar(wv[0:NW, 4:5], wv[0:NW, 2:3], -1.0, float(NBLK), ALU.mult, ALU.add))
            then(nc.vector.tensor_scalar(wv[0:NW, 5:6], wv[0:NW, 4:5], float(NBLK - FB), float(BLOCK), ALU.min, ALU.mult))
            then(nc.vector.tensor_copy(wi[0:NW, 0:1], wv[0:NW, 5:6]))
            then(nc.vector.scalar_tensor_tensor(out=wv[0:NW, 6:7], in0=wv[0:NW, 3:4], scalar=float(PB - 1 - NBLK), in1=wv[0:NW, 2:3], op0=ALU.add, op1=ALU.add))
            then(nc.vector.tensor_scalar(i1[0:NW, 0:1], wv[0:NW, 6:7], float(-FB), None, ALU.add))
            then(nc.vector.tensor_copy(i1[0:NW, 1:2], wv[0:NW, 6:7]))
            then(nc.vector.tensor_scalar(i2[0:NW, :], i1[0:NW, :], PB.bit_length() - 1, None, ALU.arith_shift_right))
            then(nc.vector.tensor_scalar(count_f[0:NW, :], i2[0:NW, :], 0.0, None, ALU.max))
            then(nc.vector.tensor_copy(wi[0:NW, 1:2], count_f[0:NW, 0:1]))
            nc.vector.tensor_copy(wi[0:NW, 3:4], count_f[0:NW, 1:2]).then_inc(count_ok, 1)
            dve.wait_ge(before_ok, 1)
            then(nc.vector.tensor_copy(wi[0:NW, 2:3], y_ps[0:NW, 0:1]))
            nc.vector.tensor_copy(wi[0:NW, 4:5], y_ps[0:NW, 1:2]).then_inc(win_ok, 1)
            keep_asd(NB - 1, 1)
            dve.wait_ge(asd_ok, NB)
            by_head = asd[:, :, 0:H].rearrange("p w h -> p h w")
            nc.vector.tensor_reduce(gmax[:, 0:H], by_head, AXX, ALU.max).then_inc(gmax_ok, 1)
            then(nc.vector.tensor_reduce(spread[:, :], by_head, AXX, ALU.min))
            nc.vector.tensor_scalar(gmax[:, H:2 * H], spread[:, :], -1.0, None, ALU.mult).then_inc(gmax_ok, 1)
            dve.wait_ge(gall_ok, 1)
            then(nc.vector.tensor_tensor(spread[:, :], gall[:, 0:H], gall[:, H:2 * H], ALU.add))
            then(nc.vector.tensor_reduce(widest[:, :], spread[:, :], AXX, ALU.max))
            then(nc.vector.tensor_copy(dm[:, :, 0:H], asd[:, :, H:2 * H]))
            then(nc.vector.tensor_copy(dm[:, :, H:2 * H], gall[:, 0:H].unsqueeze(1).broadcast_to([P, NW, H])))
            nc.vector.tensor_scalar(exact[:, :], widest[:, :], SPREAD, None, ALU.is_gt).then_inc(exact_ok, 1)
            dve.wait_ge(exact_ok, 1)
            dve.wait_ge(win_ld, 16)
            flag = dve.value_load(exact[0:1, 0:1], min_val=0, max_val=1)
            with dve.If(flag > 0):
                nc.vector.tensor_copy(dm[:, :, H:2 * H], asd[:, :, 0:H]).then_inc(m_max, 1)
                dve.wait_ge(m_max, 1)

            def exact_max(w, j, k):
                dve.wait_ge(m_dst, 16 * k + 16)
                nc.vector.tensor_scalar(xloc[:, :], xdst[:, :], base_id[:, bass.ds(w, 1)], None, ALU.subtract).then_inc(m_loc, 1)
                dve.wait_ge(m_loc, k + 1)
                nc.vector.tensor_scalar(xoh[:, :], iota_d[:, :], xloc[:, 0:1], None, ALU.is_equal).then_inc(m_oh, 1)
                dve.wait_ge(m_oh, k + 1)
                nc.vector.tensor_scalar(xpen, xoh[:, :], 1.0, 1e38, ALU.subtract, ALU.mult).then_inc(m_pen, 1)
                dve.wait_ge(m_pen, k + 1)
                dve.wait_ge(m_row, 16 * k + 16)
                nc.vector.tensor_tensor(xmask[:, :, :], xpen.unsqueeze(1).broadcast_to([P, H, P]),
                                        xrow[:, D:ROW].unsqueeze(2).broadcast_to([P, H, P]), ALU.add).then_inc(m_mask, 1)
                dve.wait_ge(m_tr, k + 1)
                nc.vector.tensor_reduce(xmax[:, :], xl_ps[:, :].rearrange("p (h e) -> p h e", h=H), AXX, ALU.max).then_inc(m_max, 1)
                dve.wait_ge(m_max, k + 2)
                mx = dm[:, bass.ds(w, 1), H:2 * H].rearrange("p w h -> p (w h)")
                nc.vector.tensor_tensor(mx, mx, xmax[:, :], ALU.max).then_inc(m_done, 1)
                dve.wait_ge(m_done, k + 2)

            if_exact(dve, exact_max)
            nc.vector.tensor_copy(parts[:, :, :, 0], dm[:, :, :]).then_inc(parts_ok, 1)
            dve.wait_ge(parts_ok, 1)
            then(nc.vector.tensor_tensor(left[:, :, :], dm[:, :, :], parts[:, :, :, 0], ALU.subtract))
            nc.vector.tensor_copy(parts[:, :, :, 1], left[:, :, :]).then_inc(parts_ok, 1)
            dve.wait_ge(parts_ok, 2)
            then(nc.vector.tensor_tensor(left[:, :, :], left[:, :, :], parts[:, :, :, 1], ALU.subtract))
            nc.vector.tensor_copy(parts[:, :, :, 2], left[:, :, :]).then_inc(parts_ok, 1)

            def flat(a):
                return a.rearrange("p w h -> p (w h)")

            then(nc.vector.tensor_tensor(sz[:, :, :], asd[:, :, 0:H], dm[:, :, 0:H], ALU.add))
            then(nc.vector.tensor_tensor(sm[:, :, :], dm[:, :, H:2 * H], dm[:, :, 0:H], ALU.add))
            then(nc.vector.scalar_tensor_tensor(out=flat(sz[:, :, :]), in0=flat(sz[:, :, :]), scalar=SLOPE, in1=flat(sz[:, :, :]), op0=ALU.mult, op1=ALU.max))
            then(nc.vector.scalar_tensor_tensor(out=flat(sm[:, :, :]), in0=flat(sm[:, :, :]), scalar=SLOPE, in1=flat(sm[:, :, :]), op0=ALU.mult, op1=ALU.max))
            nc.vector.tensor_tensor(exself[:, :, :], sz[:, :, :], sm[:, :, :], ALU.subtract).then_inc(sdiff_ok, 1)
            dve.wait_ge(exself_ok, 1)
            dve.wait_ge(w_ld, 16 * 7)
            dve.wait_ge(parts_ok, 3)

            def one_hots(w, i, b):
                dve.wait_ge(ld_dbc[b], 16 * (i + 1))
                nc.vector.tensor_scalar(oht[:, b, :], dbc[:, b, :], node_id[:, bass.ds(w, 1)], None, ALU.is_equal).then_inc(oht_ok, 1)
                dve.wait_ge(ld_dst[b], 16 * (i + 1))
                nc.vector.tensor_scalar(dloc[:, :], dsti[:, b, :], base_id[:, bass.ds(w, 1)], None, ALU.subtract).then_inc(loc_ok, 1)
                dve.wait_ge(loc_ok, w + 1)
                nc.vector.tensor_tensor(oh[:, b, :, :], iota_d[:, :].unsqueeze(1).broadcast_to([P, TILES, P]),
                                        dloc[:, :].unsqueeze(2).broadcast_to([P, TILES, P]), ALU.is_equal).then_inc(oh_ok, 1)

            def exponents(w, i, b):
                dve.wait_ge(lk_ok, w + 1)
                nc.vector.tensor_reduce(edge_dm[:, :, :].rearrange("p t v -> p (t v)"), lk_ps[:, 0:TILES * VK].rearrange("p (v k) -> p v k", k=3), AXX, ALU.add).then_inc(dm_ok, 1)
                dve.wait_ge(dm_ok, w + 1)
                nc.vector.tensor_tensor(zz[:, :, 1, :], edge_dm[:, :, H:2 * H], edge_dm[:, :, 0:H], ALU.add).then_inc(zm_ok, 1)
                dve.wait_ge(gath[b], 16 * TILES * (i + 1))
                nc.vector.tensor_tensor(zz[:, :, 0, :], rows[:, b, :, D:ROW], edge_dm[:, :, 0:H], ALU.add).then_inc(zs_ok, 1)
                dve.wait_ge(zm_ok, w + 1)
                dve.wait_ge(zs_ok, w + 1)
                za = zz[:, :, :, :].rearrange("p t k h -> p (t k h)")
                nc.vector.scalar_tensor_tensor(out=zl[:, :, :, :].rearrange("p t k h -> p (t k h)"), in0=za, scalar=SLOPE, in1=za, op0=ALU.mult, op1=ALU.max).then_inc(zl_ok, 1)
                dve.wait_ge(zl_ok, w + 1)
                nc.vector.tensor_tensor(diff[:, :, :], zl[:, :, 0, :], zl[:, :, 1, :], ALU.subtract).then_inc(diff_ok, 1)

            def weigh(w, i, b):
                dve.wait_ge(ex_ok, w + 1)
                for a, m in PIECES:
                    v = rows[:, b, a:a + m, 0:D].rearrange("p t (h c) -> p t h c", h=H)
                    e = rows[:, b, a:a + m, D:ROW].unsqueeze(3).broadcast_to([P, m, H, C])
                    nc.vector.tensor_tensor(v, v, e, ALU.mult).then_inc(scaled, 1)

            def weigh_self(w, i, b):
                dve.wait_ge(ld_self[b], 16 * (i + 1))
                e = exself[:, bass.ds(w, 1), :].rearrange("p w h -> p (w h)")
                v = selfr[:, b, 0:D].rearrange("p (h c) -> p h c", h=H)
                nc.vector.tensor_tensor(v, v, e.unsqueeze(2).broadcast_to([P, H, C]), ALU.mult).then_inc(selfx_ok, 1)
                nc.vector.tensor_copy(selfr[:, b, D:ROW], e).then_inc(self_ok, 1)

            def ffn_bias(w, i, b):
                dve.wait_ge(y_ok, w + 1)
                if known(w, 2):
                    dve.wait_ge(y_st[b], 16 * i)
                nc.vector.tensor_tensor(yb[:, b, :], y_ps[:, 0:D], b2s[:, :], ALU.add).then_inc(yb_ok, 1)

            def extra_tile(w, k):
                dve.wait_ge(x_dbc, 16 * k + 16)
                nc.vector.tensor_scalar(xoht[:, :], xdbc[:, :], node_id[:, bass.ds(w, 1)], None, ALU.is_equal).then_inc(x_oht, 1)
                dve.wait_ge(x_dst, 16 * k + 16)
                nc.vector.tensor_scalar(xloc[:, :], xdst[:, :], base_id[:, bass.ds(w, 1)], None, ALU.subtract).then_inc(x_loc, 1)
                dve.wait_ge(x_loc, k + 1)
                nc.vector.tensor_scalar(xoh[:, :], iota_d[:, :], xloc[:, 0:1], None, ALU.is_equal).then_inc(x_oh, 1)
                dve.wait_ge(x_lk, k + 1)
                nc.vector.tensor_reduce(xdm[:, :], xl_ps[:, 0:VK].rearrange("p (v k) -> p v k", k=3), AXX, ALU.add).then_inc(x_dm, 1)
                dve.wait_ge(x_dm, k + 1)
                nc.vector.tensor_tensor(xzz[:, 1, :], xdm[:, H:2 * H], xdm[:, 0:H], ALU.add).then_inc(x_zm, 1)
                dve.wait_ge(x_row, 16 * k + 16)
                nc.vector.tensor_tensor(xzz[:, 0, :], xrow[:, D:ROW], xdm[:, 0:H], ALU.add).then_inc(x_zs, 1)
                dve.wait_ge(x_zm, k + 1)
                dve.wait_ge(x_zs, k + 1)
                za = xzz[:, :, :].rearrange("p k h -> p (k h)")
                nc.vector.scalar_tensor_tensor(out=xzl[:, :, :].rearrange("p k h -> p (k h)"), in0=za, scalar=SLOPE, in1=za, op0=ALU.mult, op1=ALU.max).then_inc(x_zl, 1)
                dve.wait_ge(x_zl, k + 1)
                nc.vector.tensor_tensor(xdiff[:, :], xzl[:, 0, :], xzl[:, 1, :], ALU.subtract).then_inc(x_diff, 1)
                dve.wait_ge(x_ex, k + 1)
                dve.wait_ge(x_oh, k + 1)
                v = xrow[:, 0:D].rearrange("p (h c) -> p h c", h=H)
                nc.vector.tensor_tensor(v, v, xrow[:, D:ROW].unsqueeze(2).broadcast_to([P, H, C]), ALU.mult).then_inc(x_sc, 1)

            def residual(w, i, b):
                dve.wait_ge(agg_ok, w + 1)
                nc.vector.reciprocal(rden[:, :], ag_ps[b][:, D:ROW]).then_inc(rden_ok, 1)
                dve.wait_ge(rden_ok, w + 1)
                nc.vector.tensor_tensor(zag[:, :].rearrange("p (h c) -> p h c", h=H), ag_ps[b][:, 0:D].rearrange("p (h c) -> p h c", h=H),
                                        rden[:, :].unsqueeze(2).broadcast_to([P, H, C]), ALU.mult).then_inc(zn_ok, 1)
                dve.wait_ge(zn_ok, w + 1)
                nc.vector.tensor_tensor(zag[:, :], zag[:, :], gbs[:, :], ALU.add).then_inc(zb_ok, 1)
                dve.wait_ge(zb_ok, w + 1)
                nc.vector.tensor_scalar(zmin[:, :], zag[:, :], 0.0, None, ALU.min).then_inc(zmin_ok, 1)
                dve.wait_ge(ld_x[b], 16 * (i + 1))
                x1 = base[:, bass.ds(w, 1), :].rearrange("p w c -> p (w c)")
                nc.vector.scalar_tensor_tensor(out=zag[:, :], in0=zag[:, :], scalar=0.0, in1=x1, op0=ALU.max, op1=ALU.add).then_inc(xa_ok, 1)
                dve.wait_ge(xa_ok, w + 1)
                dve.wait_ge(zexp_ok, w + 1)
                nc.vector.scalar_tensor_tensor(out=x1, in0=zexp[:, :], scalar=-1.0, in1=zag[:, :], op0=ALU.add, op1=ALU.add).then_inc(x1_ok, 1)
                wait_apart(dve, (x1_ok, w + 1))
                nc.vector.bn_stats(st6[:, :], x1).then_inc(st_ok, 1)
                wait_apart(dve, (st_ok, w + 1))
                nc.vector.bn_aggr(mv[:, :], st6[:, :]).then_inc(mv_ok, 1)
                dve.wait_ge(mv_ok, w + 1)
                nc.vector.tensor_scalar(vareps[:, :], mv[:, 1:2], EPS, None, ALU.add).then_inc(ve_ok, 1)

            def route(w, i, b):
                dve.wait_ge(rs0_ok, w + 1)
                nc.vector.scalar_tensor_tensor(out=sq[:, :], in0=rs0[:, :], scalar=rs0[:, 0:1], in1=vareps[:, :], op0=ALU.mult, op1=ALU.mult).then_inc(sq_ok, 1)
                dve.wait_ge(sq_ok, w + 1)
                nc.vector.tensor_scalar(half[:, :], sq[:, :], -0.5, 1.5, ALU.mult, ALU.add).then_inc(half_ok, 1)
                dve.wait_ge(half_ok, w + 1)
                nc.vector.tensor_tensor(rstd[:, :], rs0[:, :], half[:, :], ALU.mult).then_inc(rstd_ok, 1)
                dve.wait_ge(rstd_ok, w + 1)
                if known(w, 1):
                    dve.wait_ge(tr_ok, w)
                x1 = base[:, bass.ds(w, 1), :].rearrange("p w c -> p (w c)")
                nc.vector.tensor_scalar(xn[:, :], x1, mv[:, 0:1], rstd[:, 0:1], ALU.subtract, ALU.mult).then_inc(xn_ok, 1)
                dve.wait_ge(xn_ok, w + 1)
                nc.vector.tensor_tensor(x1, x1, xn[:, :], ALU.add).then_inc(base_ok, 1)
                nc.vector.tensor_tensor_reduce(junk[:, :], xn[:, :], wrs[:, :], 1.0, 0.0, ALU.mult, ALU.add, wcol[:, b:b + 1]).then_inc(wcol_ok, 1)
                dve.wait_ge(wcol_ok, w + 1)
                nc.vector.tensor_copy(wt[:, bass.ds(w, 1)], wcol[:, b:b + 1]).then_inc(wt_ok, 1)

            def window(w, i, b):
                exponents(w, i, b)
                weigh(w, i, b)
                weigh_self(w, i, b)
                if known(w, 2):
                    ffn_bias(w - 2, i - 1, b)
                if not isinstance(w, int) or w + 1 < NW:
                    one_hots(w + 1, i + b, 1 - b)
                for_extra(dve, w, lambda j, k: extra_tile(w, k))
                residual(w, i, b)
                route(w, i, b)

            one_hots(0, 0, 0)
            two_by_two(dve, PAIRS, window, last_peeled=True)
            ffn_bias(NW - 2, PAIRS - 1, 0)
            dve.wait_ge(wt_ok, NW)
            dve.wait_ge(base_ok, NW)
            then(nc.vector.tensor_scalar(wt[:, :], wt[:, :], brs[:, 0:1], None, ALU.add))
            bits = wt[:, :].bitcast(I32)
            then(nc.vector.tensor_scalar(sgn, bits, 31, None, ALU.arith_shift_right))
            then(nc.vector.tensor_scalar(sgn, sgn, -2 ** 31, None, ALU.bitwise_or))
            then(nc.vector.tensor_tensor(key, bits, sgn, ALU.bitwise_xor))
            then(nc.vector.tensor_scalar(sgn, key, 16, 0xffff, ALU.logical_shift_right, ALU.bitwise_and))
            then(nc.vector.tensor_copy(khi, sgn))
            then(nc.vector.tensor_scalar(sgn, key, 0xffff, None, ALU.bitwise_and))
            then(nc.vector.tensor_copy(klo, sgn))
            then(nc.vector.tensor_scalar(valid, node_id[:, :], float(N), None, ALU.is_lt))
            then(nc.vector.scalar_tensor_tensor(out=khi, in0=khi, scalar=1.0, in1=valid, op0=ALU.add, op1=ALU.mult))
            then(nc.vector.tensor_scalar(khi, khi, -1.0, None, ALU.add))
            then(nc.vector.memset(kth[:, :], float(K)))
            then(nc.vector.memset(cnt[:, :], 0.0))
            ffn_bias(NW - 1, PAIRS - 1, 1)
            rounds = [0]

            def totals():
                rounds[0] += 1
                dve.wait_ge(tot_ok, rounds[0])

            def search(keys):
                then(nc.vector.memset(cur[:, :], 0.0))
                for place in range(7, -1, -1):
                    step = float(4 ** place)
                    then(nc.vector.tensor_scalar(thr[:, :], iota_d[:, 1:4], step, cur[:, 0:1], ALU.mult, ALU.add))
                    for j in range(3):
                        last = nc.vector.tensor_scalar(marks[j], keys, thr[:, j:j + 1], 0.0, ALU.is_ge, ALU.add, accum_out=cnt[:, j:j + 1])
                    last.then_inc(cnt_ok, 1)
                    totals()
                    then(nc.vector.tensor_scalar(got[:, :], lk_ps[:, 0:3], kth[:, 0:1], 0.0, ALU.is_ge, ALU.add, accum_out=nge[:, :]))
                    then(nc.vector.tensor_scalar(cur[:, :], nge[:, :], step, cur[:, 0:1], ALU.mult, ALU.add))

            def take_above(keys):
                then(nc.vector.tensor_scalar(above, keys, cur[:, 0:1], None, ALU.is_gt))
                nc.vector.tensor_reduce(cnt[:, 0:1], above, AXX, ALU.add).then_inc(cnt_ok, 1)
                totals()
                then(nc.vector.tensor_tensor(kth[:, :], kth[:, :], lk_ps[:, 0:1], ALU.subtract))

            search(khi)
            take_above(khi)
            then(nc.vector.tensor_tensor(coef, above, wt[:, :], ALU.mult))
            then(nc.vector.tensor_scalar(tie, khi, cur[:, 0:1], None, ALU.is_equal))
            then(nc.vector.scalar_tensor_tensor(out=klo, in0=klo, scalar=1.0, in1=tie, op0=ALU.add, op1=ALU.mult))
            then(nc.vector.tensor_scalar(klo, klo, -1.0, None, ALU.add))
            search(klo)
            take_above(klo)
            nc.vector.tensor_scalar(tie, klo, cur[:, 0:1], None, ALU.is_equal).then_inc(tie_ok, 1)
            dve.wait_ge(rank_ok, 1)
            then(nc.vector.tensor_copy(col, xl_ps[:, 0:NW]))
            then(nc.vector.tensor_tensor_scan(rank, ones[:, 0:NW], col, 0.0, ALU.mult, ALU.add))
            then(nc.vector.tensor_tensor(rank, rank, col, ALU.subtract))
            then(nc.vector.tensor_tensor(rank, rank, lk_ps[:, 0:NW], ALU.add))
            then(nc.vector.scalar_tensor_tensor(out=tie, in0=rank, scalar=kth[:, 0:1], in1=tie, op0=ALU.is_lt, op1=ALU.mult))
            then(nc.vector.tensor_tensor(tie, tie, above, ALU.add))
            then(nc.vector.tensor_tensor(tie, tie, wt[:, :], ALU.mult))
            then(nc.vector.tensor_tensor(coef, coef, tie, ALU.add))
            for g in range(NB):
                dve.wait_ge(y_ld[g % 4], 16 * (g // 4 + 1))
                for t in range(BATCH):
                    w = g * BATCH + t
                    last = nc.vector.scalar_tensor_tensor(out=base[:, w, :], in0=yin[g % 4][:, t, :], scalar=coef[:, w:w + 1], in1=base[:, w, :], op0=ALU.mult, op1=ALU.add)
                last.then_inc(out_ok, 1)


def kernel(**inputs):
    import numpy as np
    import concourse.bacc as bacc
    from concourse import mybir as my
    from concourse.bass_utils import run_bass_kernel_spmd as run

    arrays = {k: np.ascontiguousarray(v) for k, v in inputs.items() if k != "L0_ffn_attention_mask"}
    n, e = arrays["x"].shape[0], arrays["src"].shape[0]
    nw, _, ep = sizes(n, e)
    arrays["x"] = np.pad(arrays["x"], ((0, nw * P - n), (0, 0)))
    arrays["src"] = np.pad(arrays["src"], (0, ep - e))
    arrays["dst"] = np.pad(arrays["dst"], (0, ep - e), constant_values=-1)
    nc = bacc.Bacc("TRN2", target_bir_lowering=False, num_devices=1)
    ins = {k: nc.dram_tensor(f"in_{k}", a.shape, my.dt.from_np(a.dtype), kind="ExternalInput").ap() for k, a in arrays.items()}
    out = nc.dram_tensor("out", arrays["x"].shape, F32, kind="ExternalOutput").ap()
    build(nc, ins["x"], ins["src"], ins["dst"], ins["L0_gnn_W"], ins["L0_gnn_att_src"], ins["L0_gnn_att_dst"],
          ins["L0_gnn_bias"], ins["L0_ffn_wr"], ins["L0_ffn_br"], ins["L0_ffn_w1"], ins["L0_ffn_b1"],
          ins["L0_ffn_w2"], ins["L0_ffn_b2"], out, n, e)
    r = run(nc, [{f"in_{k}": a for k, a in arrays.items()}], core_ids=[0])
    return r.results[0]["out"][:n]
```

```python
from contextlib import ExitStack

import concourse.bass as bass
from concourse import mybir

F32 = mybir.dt.float32
BF16 = mybir.dt.bfloat16
I32 = mybir.dt.int32
I16 = mybir.dt.int16
ALU = mybir.AluOpType
ACT = mybir.ActivationFunctionType
AXX = mybir.AxisListType.X

P = 128
EPS = 1e-5
SLOPE = 0.2
BLOCK = 32
SPREAD = 40.0


def sizes(n, e):
    nw = -(-n // P)
    tiles = -(-e // n) + 1
    ep = -(-(e + P * (tiles + 1)) // (P * BLOCK)) * P * BLOCK
    return nw, tiles, ep


def build(nc, x, src, dst, W, att_src, att_dst, gbias, wr, br, w1, b1, w2, b2, out, N, E):
    D = W.shape[0]
    H, C = att_src.shape
    F = w1.shape[1]
    NW, TILES, EP = sizes(N, E)
    BATCH = 7
    PAIRS = NW // 2
    K = max(1, int(0.5 * N)) - 1
    ROW = D + H
    DC, FC = D // P, F // P
    NB = NW // BATCH
    DEEP = 4
    VK = 2 * H * 3
    EPP = EP // P
    BPP = EPP // BLOCK
    NBLK = EP // BLOCK
    FLAT = TILES * P
    FB = FLAT // BLOCK
    PB = P // BLOCK
    ROUNDS = 2 * 8 + 2
    FREED = 6
    CONSTS = 14
    LOADS = 5
    IN_BANK = 512 // P
    assert NW % (2 * BATCH) == 0 and (NB - 2) % DEEP == 0 and NB > DEEP and DC == 2 and TILES * VK <= 512
    PIECES = []
    at = 0
    for size in (1, 2, 2, 3, 3, 3, 3, 3, 3, 3):
        if at < TILES:
            PIECES.append((at, min(size, TILES - at)))
            at += size
    NP = len(PIECES)
    piece_of = {t: n for n, (a, m) in enumerate(PIECES) for t in range(a, a + m)}

    with ExitStack() as ctx:
        def sb(name, shape, dt=F32):
            return ctx.enter_context(nc.sbuf_tensor(name, shape, dt))

        def ps(name, shape):
            return ctx.enter_context(nc.psum_tensor(name, shape, F32))

        def sem(name):
            return ctx.enter_context(nc.semaphore(name))

        def sem2(name):
            return [sem(f"{name}{b}") for b in range(2)]

        table = nc.dram_tensor("node_rows", (NW * P, ROW), F32).ap()
        y_dram = nc.dram_tensor("ffn_rows", (NW * P, D), F32).ap()
        dst16_dram = nc.dram_tensor("dst16", (EP,), I16).ap()
        blk_dram = nc.dram_tensor("block_range", (2, NBLK), F32).ap()
        win_dram = nc.dram_tensor("window_table", (NW, 5), I32).ap()

        ident = sb("ident", [P, P])
        ones = sb("ones", [P, P])
        below = sb("below", [P, P])
        iota_d = sb("iota_d", [P, P])
        node_id = sb("node_id", [P, NW])
        base_id = sb("base_id", [P, NW])
        w1s = sb("w1s", [P, DC, F])
        w2s = sb("w2s", [P, FC, D])
        b1s = sb("b1s", [P, FC])
        gb_parts = sb("gb_parts", [P, ROW + H], BF16)
        b2_parts = sb("b2_parts", [P, D], BF16)
        ones_bf = sb("ones_bf", [P, P], BF16)
        wrs = sb("wrs", [P, D])
        brs = sb("brs", [P, 1])
        base = sb("base", [P, NW, D])
        parts = sb("parts", [P, NW, 2 * H, 3], BF16)
        exself = sb("exself", [P, NW, H])
        wt = sb("wt", [P, NW])
        win = sb("win", [1, 5 * NW], I32)
        rows = sb("rows", [P, 2, TILES, ROW])
        srci = sb("srci", [P, 2, TILES], I32)
        dsti = sb("dsti", [P, 2, TILES], I32)
        dbc = sb("dbc", [P, 2, FLAT], I16)
        oht = dbc[:, :, :].bitcast(BF16)
        oh = sb("oh", [P, 2, TILES, P])
        dloc = sb("dloc", [P, TILES])
        edge_dm = sb("edge_dm", [P, TILES, 2 * H])
        zz = sb("zz", [P, TILES, H])
        zl = sb("zl", [P, TILES, H])
        zc = sb("zc", [P, TILES, H])
        diff = sb("diff", [P, TILES, H])
        selfr = sb("selfr", [P, 2, ROW])
        rden = sb("rden", [P, H])
        zag = sb("zag", [P, D])
        zmin = sb("zmin", [P, D])
        zexp = sb("zexp", [P, D])
        xn = sb("xn", [P, D])
        junk = zexp
        xnT = sb("xnT", [P, DC, P])
        hT = sb("hT", [P, FC, P])
        yb = sb("yb", [P, 2, D])
        st6 = sb("st6", [P, 6])
        mv = sb("mv", [P, 2])
        lnv = sb("lnv", [P, 1])
        rs0 = sb("rs0", [P, 1])
        rs1 = sb("rs1", [P, 1])
        rstd = sb("rstd", [P, 1])
        vareps = sb("vareps", [P, 1])
        sq = sb("sq", [P, 1])
        half = sb("half", [P, 1])
        wcol = sb("wcol", [P, 2])
        xsrc = sb("xsrc", [P, 1], I32)
        xdst = sb("xdst", [P, 1], I32)
        xdbc = sb("xdbc", [P, P], I16)
        xrow = sb("xrow", [P, ROW])
        xoh = sb("xoh", [P, P])
        xoht = sb("xoht", [P, P], BF16)
        xloc = sb("xloc", [P, 1])
        xdm = sb("xdm", [P, 2 * H])
        xzz = sb("xzz", [P, H])
        xzl = sb("xzl", [P, H])
        xzc = sb("xzc", [P, H])
        xdiff = sb("xdiff", [P, H])

        xmax = sb("xmax", [P, H])

        BD = BATCH * D
        WIDE = ROW + H
        rows_flat = rows[:, :, :, :].rearrange("p a t c -> p (a t c)")
        base_flat = base[:, :, :].rearrange("p w c -> p (w c)")
        oh_flat = oh[:, :, :, :].rearrange("p a t c -> p (a t c)")

        def batch(flat, at, width):
            return flat[:, at:at + BATCH * width].rearrange("p (g c) -> p g c", g=BATCH)

        nb = [batch(rows_flat, b * BD, D) for b in range(2)]
        scratch = 2 * BD
        falls = rows_flat[:, scratch:scratch + EPP].bitcast(I32)
        bias_f = [rows_flat[:, scratch + EPP + k * D:scratch + EPP + (k + 1) * D] for k in range(3)]
        bias_b = rows_flat[:, scratch + EPP + 3 * D:scratch + EPP + 3 * D + 3 * D // 2].bitcast(BF16).rearrange("p (k n) -> p k n", k=3)
        lo_b = base_flat[0:NW, 0:NBLK]
        hi_b = base_flat[0:NW, NBLK:2 * NBLK]
        xb = [batch(base_flat, 2 * NBLK + q * BD, D) for q in range(DEEP)]
        po = [batch(base_flat, 2 * NBLK + DEEP * BD + b * BATCH * WIDE, WIDE) for b in range(2)]
        dst_all = oh_flat[:, 0:EPP + 1].bitcast(I32)
        kept = EPP + 1
        blo = oh_flat[:, kept:kept + BPP]
        bhi = oh_flat[:, kept + BPP:kept + 2 * BPP]
        kept += 2 * BPP
        asd, dm = (oh_flat[:, kept + k * NW * 2 * H:kept + (k + 1) * NW * 2 * H].rearrange("p (w v) -> p w v", w=NW) for k in range(2))
        kept += 4 * NW * H
        sz, sm = (oh_flat[:, kept + k * NW * H:kept + (k + 1) * NW * H].rearrange("p (w v) -> p w v", w=NW) for k in range(2))
        left = oh_flat[:, 0:2 * NW * H].rearrange("p (w v) -> p w v", w=NW)
        xpen = oh_flat[:, 2 * NW * H:2 * NW * H + P]
        xmask = oh_flat[:, 2 * NW * H + P:2 * NW * H + (1 + H) * P].rearrange("p (h e) -> p h e", h=H)
        assert kept + 2 * NW * H <= 2 * TILES * P and 2 * NW * H + (1 + H) * P <= EPP
        assert 2 * NBLK + DEEP * BD + 2 * BATCH * WIDE <= NW * D and scratch + EPP + 3 * D + 3 * D // 2 <= 2 * TILES * ROW
        spare = 2 * TILES * P - BD
        dbc_flat = dbc[:, :, :].rearrange("p a e -> p (a e)").bitcast(F32)
        w1_flat = w1s[:, :, :].rearrange("p c n -> p (c n)")
        w2_flat = w2s[:, :, :].rearrange("p m n -> p (m n)")
        yin = [batch(rows_flat, k * BD, D) for k in range(4)] + [batch(f, 0, D) for f in (w1_flat, w2_flat, dbc_flat)] + [batch(oh_flat, spare, D)]
        YIN = len(yin)
        wext = hT[:, :, :].rearrange("p m q -> p (m q)")[:, 0:DC * WIDE].rearrange("p (c n) -> p c n", c=DC)
        key, sgn, khi, klo, tie, above, col, rank, coef, valid, *marks = (oh_flat[:, k * NW:(k + 1) * NW] for k in range(13))
        assert 13 * NW <= spare
        key, sgn = key.bitcast(I32), sgn.bitcast(I32)
        dst16 = dbc[:, 0, 0:EPP]
        xnT2 = dbc[:, 1, 0:4 * D].bitcast(F32).rearrange("p (a c q) -> p a c q", a=2, c=DC)
        att_b = [zag[:, :], zmin[:, :]]
        wext_mul = [zexp, xn, yb[:, 0, :], yb[:, 1, :]]
        broken = sb("broken", [P, 1])
        broken_all = sb("broken_all", [P, 1])
        st_b = sb("st_b", [P, BATCH, 6])
        mv_b = sb("mv_b", [P, 2, BATCH, 2])
        rs_b = sb("rs_b", [P, 2, BATCH])
        minus_half = sb("minus_half", [P, BATCH])
        gmax = sb("gmax", [P, 2 * H])
        gall = sb("gall", [P, 2 * H])
        spread = sb("spread", [P, H])
        widest = sb("widest", [P, 1])
        exact = sb("exact", [P, 1], I32)
        wv = sb("wv", [P, 8])
        wi = sb("wi", [P, 5], I32)
        count_f = sb("count_f", [P, 2])
        i1 = sb("i1", [P, 2], I32)
        i2 = sb("i2", [P, 2], I32)
        thr = sb("thr", [P, 3])
        cnt = sb("cnt", [P, 3])
        got = sb("got", [P, 3])
        nge = sb("nge", [P, 1])
        cur = sb("cur", [P, 1])
        kth = sb("kth", [P, 1])

        lk_ps = ps("lk_ps", [P, 512])
        ag_ps = [ps(f"ag_ps{b}", [P, 512]) for b in range(2)]
        tr_ps = ps("tr_ps", [P, 512])
        h_ps = ps("h_ps", [P, 1024])
        y_ps = ps("y_ps", [P, 512])
        xl_ps = ps("xl_ps", [P, 512])
        tr2 = [t[:, 0:D].rearrange("p (c q) -> p c q", c=DC) for t in (tr_ps, xl_ps)]

        def sems(names):
            return [sem(n) for n in names.split()]

        dst_ld, att_ld, gb_ld, b2_ld, w_ld, d16_st, blk_st, blk_ld, win_st, win_ld = sems(
            "dst_ld att_ld gb_ld b2_ld w_ld d16_st blk_st blk_ld win_st win_ld")
        x_ld, tab_st = [sem(f"x_ld{q}") for q in range(DEEP)], sem2("tab_st")
        (pool_const, d16_ok, blk_ok, falls_ok, fall_ok, broken_ok, gb_ok, b2_ok, bias_step, wext_mul_ok, wext_ok, stat_ok, aggr_ok, vareps_b, rstd_b, norm_ok, trb_ok, trc_ok, xp_ok, xpc_ok, asd_ok,
         count_ok, before_ok, win_ok, gmax_ok, gall_ok, exact_ok, sdiff_ok, exself_ok, parts_ok,
         pre) = sems(
            "pool_const d16_ok blk_ok falls_ok fall_ok broken_ok gb_ok b2_ok bias_step wext_mul_ok wext_ok stat_ok aggr_ok vareps_b rstd_b norm_ok trb_ok trc_ok xp_ok xpc_ok asd_ok "
            "count_ok before_ok win_ok gmax_ok gall_ok exact_ok sdiff_ok exself_ok parts_ok pre")
        ld_src, ld_dst, ld_dbc, ld_self, ld_x, gath, y_st = (
            sem2(n) for n in ("ld_src", "ld_dst", "ld_dbc", "ld_self", "ld_x", "gath", "y_st"))
        (oht_ok, loc_ok, oh_ok, lk_ok, dm_ok, zs_ok, zm_ok, zl_ok, diff_ok, ex_ok, scaled, tile_done, agg_ok, selfx_ok,
         self_ok, rden_ok, zn_ok, zmin_ok, zexp_ok, xa_ok, x1_ok, st_ok, mv_ok, ln_ok, rs0_ok, ve_ok, sq_ok,
         half_ok, rstd_ok, xn_ok, base_ok, wcol_ok, wt_ok, tr_ok, xnT_ok, h_ok, hT_ok, y_ok, yb_ok) = sems(
            "oht_ok loc_ok oh_ok lk_ok dm_ok zs_ok zm_ok zl_ok diff_ok ex_ok scaled tile_done agg_ok selfx_ok "
            "self_ok rden_ok zn_ok zmin_ok zexp_ok xa_ok x1_ok st_ok mv_ok ln_ok rs0_ok ve_ok sq_ok "
            "half_ok rstd_ok xn_ok base_ok wcol_ok wt_ok tr_ok xnT_ok h_ok hT_ok y_ok yb_ok")
        (x_src, x_dst, x_dbc, x_row, x_oht, x_loc, x_oh, x_lk, x_dm, x_zs, x_zm, x_zl, x_diff, x_ex, x_exc, x_sc,
         x_done) = sems(
            "x_src x_dst x_dbc x_row x_oht x_loc x_oh x_lk x_dm x_zs x_zm x_zl x_diff x_ex x_exc x_sc x_done")
        m_src, m_dst, m_row, m_loc, m_oh, m_pen, m_mask, m_tr, m_max, m_done = sems(
            "m_src m_dst m_row m_loc m_oh m_pen m_mask m_tr m_max m_done")
        step_ok, cnt_ok, tot_ok, tie_ok, rank_ok, out_ok, out_st = sems(
            "step_ok cnt_ok tot_ok tie_ok rank_ok out_ok out_st")
        y_ld = [sem(f"y_ld{k}") for k in range(YIN)]

        def bc(v, n):
            return v.rearrange("(a n) -> a n", a=1).broadcast_to([P, n])

        def nodes(t, first, count):
            return t[bass.ds(first * P, count * P), :].rearrange("(g p) c -> p g c", p=P)

        def two_by_two(eng, turns, body, last_peeled=False):
            for b in range(2):
                body(b, 0, b)
            with eng.Fori(1, turns - last_peeled) as i:
                for b in range(2):
                    body(2 * i + b, i, b)
            if last_peeled:
                for b in range(2):
                    body(2 * (turns - 1) + b, turns - 1, b)

        def batches(eng, body, last_peeled=False):
            for b in range(2):
                body(b, 0, b, 0, b)
            turns = (NB - 2) // DEEP - last_peeled
            if turns:
                with eng.Fori(0, turns) as i:
                    for k in range(DEEP):
                        body(DEEP * i + 2 + k, 2 * i + 1 + k // 2, k % 2, i + (2 + k) // DEEP, (2 + k) % DEEP)
            if last_peeled:
                for g in range(NB - DEEP, NB):
                    body(g, g // 2, g % 2, g // DEEP, g % DEEP)

        def known(n, least):
            return not isinstance(n, int) or n >= least

        def wait_apart(eng, *waits):
            waits = [(semaphore, value if isinstance(value, int) else eng.to_reg(value)) for semaphore, value in waits]
            eng.wait_ge(pool_const, CONSTS)
            for semaphore, value in waits:
                eng.wait_ge(semaphore, value)

        def entry(eng, w, k, most):
            return eng.value_load(win[0:1, bass.ds(5 * w + k, 1)], min_val=0, max_val=most)

        def for_extra(eng, w, body):
            n = entry(eng, w, 1, EP // P)
            before = entry(eng, w, 2, NW * EP // P)
            with eng.If(n > 0):
                with eng.Fori(0, n) as j:
                    body(j, before + j)

        def in_edges(at):
            return nc.s_assert_within(at, 0, EP - P, skip_runtime_bounds_check_because="a window's tiles begin before its last edge")

        def if_exact(eng, body):
            flag = eng.value_load(exact[0:1, 0:1], min_val=0, max_val=1)
            with eng.If(flag > 0):
                with eng.Fori(0, NW) as w:
                    n = entry(eng, w, 3, EP // P)
                    before = entry(eng, w, 4, NW * EP // P)
                    with eng.If(n > 0):
                        with eng.Fori(0, n) as j:
                            body(w, j, before + j)

        block = ctx.enter_context(nc.Block())

        @block.sync
        def _(sp):
            def load_x(g, q):
                sp.dma_start(xb[q], nodes(x, g * BATCH, BATCH)).then_inc(x_ld[q], 16)

            load_x(0, 0)
            sp.dma_start(wext[:, :, 0:D], W.rearrange("(c p) n -> p c n", p=P)).then_inc(att_ld, 16)
            sp.dma_start(att_b[0], bc(att_src.rearrange("h c -> (h c)"), D)).then_inc(att_ld, 16)
            sp.dma_start(att_b[1], bc(att_dst.rearrange("h c -> (h c)"), D)).then_inc(att_ld, 16)
            for q in range(1, DEEP):
                load_x(q, q)

            def store_rows(g, b):
                wait_apart(sp, (xpc_ok, BATCH * (g + 1)))
                sp.dma_start(nodes(table, g * BATCH, BATCH), po[b][:, :, 0:ROW]).then_inc(tab_st[b], 16)

            def batch_io(g, t, b, r, q):
                if not isinstance(g, int) or g + DEEP < NB:
                    wait_apart(sp, (norm_ok, g + 1))
                    load_x(g + DEEP, q)
                if known(g, 1):
                    store_rows(g - 1, 1 - b)
                if isinstance(g, int) and g == 1:
                    sp.wait_ge(blk_ok, 2)
                    sp.dma_start(blk_dram[0, :].rearrange("(p n) -> p n", p=P), blo).then_inc(blk_st, 16)
                    sp.dma_start(blk_dram[1, :].rearrange("(p n) -> p n", p=P), bhi).then_inc(blk_st, 16)
                    sp.wait_ge(blk_st, 32)
                    sp.dma_start(lo_b, blk_dram[0:1, :].broadcast_to([NW, NBLK])).then_inc(blk_ld, 16)
                    sp.dma_start(hi_b, blk_dram[1:2, :].broadcast_to([NW, NBLK])).then_inc(blk_ld, 16)
                    sp.wait_ge(d16_ok, 1)
                    sp.dma_start(dst16_dram.rearrange("(p e) -> p e", p=P), dst16).then_inc(d16_st, 16)

            batches(sp, batch_io, last_peeled=True)
            store_rows(NB - 1, 1)
            sp.wait_ge(win_ld, 16)
            sp.wait_ge(d16_st, 16)
            for b in range(2):
                sp.wait_ge(tab_st[b], 16 * (NB // 2))
            sp.wait_ge(exact_ok, 1)

            def exact_loads(w, j, k):
                first = in_edges(entry(sp, w, 0, EP - FLAT) + j * P)
                wait_apart(sp, (m_done, k + 1))
                with nc.allow_non_contiguous_dma("an edge to a partition"):
                    sp.dma_start(xsrc[:, :], src[bass.ds(first, P)].rearrange("(p t) -> p t", t=1)).then_inc(m_src, 16)
                    sp.dma_start(xdst[:, :], dst[bass.ds(first, P)].rearrange("(p t) -> p t", t=1)).then_inc(m_dst, 16)

            if_exact(sp, exact_loads)

            def load_sources(w, b):
                first = entry(sp, w, 0, EP - FLAT)
                sp.dma_start(srci[:, b, :], src[bass.ds(first, FLAT)].rearrange("(p t) -> p t", t=TILES)).then_inc(ld_src[b], 16)

            def window(w, i, b):
                if not isinstance(w, int) or w + 1 < NW:
                    if known(w, 1):
                        wait_apart(sp, (gath[1 - b], 16 * TILES * (i + b)))
                    load_sources(w + 1, 1 - b)
                first = entry(sp, w, 0, EP - FLAT)
                if known(w, 2):
                    wait_apart(sp, (oh_ok, w - 1), (lk_ok, w - 1))
                sp.dma_start(dbc[:, b, :], dst16_dram[bass.ds(first, FLAT)].rearrange("(a e) -> a e", a=1).broadcast_to([P, FLAT])).then_inc(ld_dbc[b], 16)
                sp.dma_start(dsti[:, b, :], dst[bass.ds(first, FLAT)].rearrange("(p t) -> p t", t=TILES)).then_inc(ld_dst[b], 16)
                sp.dma_start(base[:, bass.ds(w, 1), :].rearrange("p w c -> p (w c)"), x[bass.ds(w * P, P), :]).then_inc(ld_x[b], 16)
                if known(w, 2):
                    wait_apart(sp, (agg_ok, w - 1))
                sp.dma_start(selfr[:, b, :], table[bass.ds(w * P, P), :]).then_inc(ld_self[b], 16)
                if known(w, 1):
                    extra_loads(w - 1)

            def extra_loads(w):
                if isinstance(w, int) and w == 0:
                    sp.wait_ge(parts_ok, 1)
                after = entry(sp, w, 0, EP - FLAT) + FLAT

                def load(j, k):
                    at = in_edges(after + j * P)
                    wait_apart(sp, (x_done, k + 1))
                    with nc.allow_non_contiguous_dma("an edge to a partition"):
                        sp.dma_start(xsrc[:, :], src[bass.ds(at, P)].rearrange("(p t) -> p t", t=1)).then_inc(x_src, 16)
                        sp.dma_start(xdst[:, :], dst[bass.ds(at, P)].rearrange("(p t) -> p t", t=1)).then_inc(x_dst, 16)
                    sp.dma_start(xdbc[:, :], dst16_dram[bass.ds(at, P)].rearrange("(a e) -> a e", a=1).broadcast_to([P, P])).then_inc(x_dbc, 16)

                for_extra(sp, w, load)

            load_sources(0, 0)
            two_by_two(sp, PAIRS, window, last_peeled=True)
            extra_loads(NW - 1)
            for g in range(NB):
                sp.wait_ge(out_ok, g + 1)
                sp.dma_start(nodes(out, g * BATCH, BATCH), base[:, g * BATCH:(g + 1) * BATCH, :]).then_inc(out_st, 16)
            sp.wait_ge(out_st, 16 * NB)

        @block.gpsimd
        def _(pool):
            nc.gpsimd.memset(ident[:, :], 0.0).then_inc(pool_const, 1)
            nc.gpsimd.memset(below[:, :], 1.0).then_inc(pool_const, 1)
            nc.gpsimd.memset(ones[:, :], 1.0).then_inc(pool_const, 1)
            nc.gpsimd.memset(minus_half[:, :], -0.5).then_inc(pool_const, 1)
            nc.gpsimd.memset(ones_bf[:, :], 1.0).then_inc(pool_const, 1)
            nc.gpsimd.memset(gb_parts[:, D:], 0.0).then_inc(pool_const, 1)
            nc.gpsimd.memset(dst_all[:, EPP:EPP + 1], NW * P).then_inc(pool_const, 1)
            pool.wait_ge(pool_const, 7)
            nc.gpsimd.affine_select(out=ident[:, :], in_=ident[:, :], compare_op=ALU.not_equal, fill=1.0, base=0,
                                    pattern=[[-1, P]], channel_multiplier=1).then_inc(pool_const, 1)
            nc.gpsimd.affine_select(out=below[:, :], in_=below[:, :], compare_op=ALU.is_gt, fill=0.0, base=0,
                                    pattern=[[1, P]], channel_multiplier=-1).then_inc(pool_const, 1)

            def count(dst_ap, pattern, base_, by_partition):
                nc.gpsimd.iota(dst_ap, pattern=pattern, base=base_, channel_multiplier=by_partition,
                               allow_small_or_imprecise_dtypes=True).then_inc(pool_const, 1)

            count(iota_d[:, :], [[1, P]], 0, 0)
            count(node_id[:, :], [[P, NW]], 0, 1)
            count(base_id[:, :], [[P, NW]], 0, 0)
            count(wv[0:NW, 0:1], [[0, 1]], 0, P)
            count(wv[0:NW, 1:2], [[0, 1]], P - 1, P)
            pool.wait_ge(pool_const, CONSTS)
            steps = [0]

            def then(ins):
                steps[0] += 1
                ins.then_inc(bias_step, 1)
                pool.wait_ge(bias_step, steps[0])

            def bias_parts(bias, parted, ready):
                rest = bias
                for k in range(3):
                    then(nc.gpsimd.tensor_copy(bias_b[:, k, :], rest))
                    if k < 2:
                        then(nc.gpsimd.tensor_tensor(bias_f[2], rest, bias_b[:, k, :], ALU.subtract))
                        rest = bias_f[2]
                for k in range(3):
                    then(nc.gpsimd.tensor_scalar(bias_b[:, k, :], bias_b[:, k, :], ident[:, k:k + 1], None, ALU.mult))
                then(nc.gpsimd.tensor_tensor(parted, bias_b[:, 0, :], bias_b[:, 1, :], ALU.add))
                nc.gpsimd.tensor_tensor(parted, parted, bias_b[:, 2, :], ALU.add).then_inc(ready, 1)

            def edge_order():
                pool.wait_ge(dst_ld, 32)
                by_block = dst_all[:, 0:EPP].rearrange("p (n e) -> p n e", e=BLOCK)
                nc.gpsimd.tensor_copy(blo, by_block[:, :, 0]).then_inc(blk_ok, 1)
                nc.gpsimd.tensor_copy(bhi, by_block[:, :, BLOCK - 1]).then_inc(blk_ok, 1)
                nc.gpsimd.tensor_copy(dst16, dst_all[:, 0:EPP]).then_inc(d16_ok, 1)
                nc.gpsimd.tensor_tensor(falls, dst_all[:, 0:EPP], dst_all[:, 1:EPP + 1], ALU.subtract).then_inc(falls_ok, 1)

            pool.wait_ge(gb_ld, 16)
            bias_parts(bias_f[0], gb_parts[:, 0:D], gb_ok)

            def rstd_batch(g, t, b, r, q):
                wait_apart(pool, (aggr_ok, g + 1), *([(norm_ok, g - 1)] if known(g, 2) else []))
                nc.gpsimd.tensor_scalar(rs_b[:, b, :], mv_b[:, b, :, 1], EPS, None, ALU.add).then_inc(vareps_b, 1)
                wait_apart(pool, (vareps_b, g + 1))
                nc.gpsimd.tensor_tensor(rs_b[:, b, :], rs_b[:, b, :], minus_half[:, :], ALU.pow).then_inc(rstd_b, 1)
                if isinstance(g, int) and g == 0:
                    edge_order()
                if isinstance(g, int) and g == 1:
                    pool.wait_ge(fall_ok, 1)
                    nc.gpsimd.partition_all_reduce(broken_all[:, :], broken[:, :], P, bass.bass_isa.ReduceOp.max).then_inc(broken_ok, 1)

            batches(pool, rstd_batch)
            pool.wait_ge(b2_ld, 16)
            pool.wait_ge(gb_ok, 1)
            bias_parts(bias_f[1], b2_parts[:, :], b2_ok)
            pool.wait_ge(win_ok, 1)
            pool.dma_start(win_dram, wi[0:NW, :]).then_inc(win_st, 16)
            pool.wait_ge(win_st, 16)
            pool.dma_start(win[:, :], win_dram.rearrange("(a w) c -> a (w c)", a=1)).then_inc(win_ld, 16)
            pool.wait_ge(gmax_ok, 2)
            nc.gpsimd.partition_all_reduce(gall[:, :], gmax[:, :], P, bass.bass_isa.ReduceOp.max).then_inc(gall_ok, 1)
            for b in range(2):
                pool.wait_ge(tab_st[b], 16 * (NB // 2))
            pool.wait_ge(win_ld, 16)

            def exact_gather(w, j, k):
                wait_apart(pool, (m_src, 16 * k + 16))
                pool.indirect_dma_start(out=xrow[:, :], out_offset=None, in_=table,
                                        in_offset=bass.IndirectOffsetOnAxis(ap=xsrc[:, 0:1], axis=0)).then_inc(m_row, 16)


            def window(w, i, b):
                pool.wait_ge(ld_src[b], 16 * (i + 1))
                for t in range(TILES):
                    if known(w, 2) and t % FREED == 0:
                        wait_apart(pool, (tile_done, (w - 2) * TILES + min(t + FREED, TILES)))
                    pool.indirect_dma_start(out=rows[:, b, t, :], out_offset=None, in_=table,
                                            in_offset=bass.IndirectOffsetOnAxis(ap=srci[:, b, t:t + 1], axis=0)).then_inc(gath[b], 16)

                if isinstance(w, int) and w == 0:
                    pool.wait_ge(exact_ok, 1)
                    if_exact(pool, exact_gather)

                def extra_gather(j, k):
                    wait_apart(pool, (x_src, 16 * k + 16))
                    pool.indirect_dma_start(out=xrow[:, :], out_offset=None, in_=table,
                                            in_offset=bass.IndirectOffsetOnAxis(ap=xsrc[:, 0:1], axis=0)).then_inc(x_row, 16)

                for_extra(pool, w, extra_gather)

            two_by_two(pool, PAIRS, window)

        @block.scalar
        def _(act):
            act.dma_start(dst_all[:, 0:EPP], dst.rearrange("(p e) -> p e", p=P)).then_inc(dst_ld, 16)
            act.wait_ge(pool_const, 7)
            with nc.allow_non_contiguous_dma("the target that follows each partition's last"):
                act.dma_start(dst_all[0:P - 1, EPP:EPP + 1], dst.rearrange("(p e) -> p e", p=P)[1:P, 0:1]).then_inc(dst_ld, 16)
            act.dma_start(bias_f[0], bc(gbias, D)).then_inc(gb_ld, 16)
            act.dma_start(bias_f[1], bc(b2, D)).then_inc(b2_ld, 16)
            act.dma_start(w1s[:, :, :], w1.rearrange("(c p) n -> p c n", p=P)).then_inc(w_ld, 16)
            act.dma_start(w2s[:, :, :], w2.rearrange("(c p) n -> p c n", p=P)).then_inc(w_ld, 16)
            with nc.allow_non_contiguous_dma("a bias by column of the hidden layer"):
                act.dma_start(b1s[:, :], b1.rearrange("(c p) -> p c", p=P)).then_inc(w_ld, 16)
            act.dma_start(wrs[:, :], bc(wr.rearrange("d o -> (d o)"), D)).then_inc(w_ld, 16)
            act.dma_start(brs[:, :], bc(br, 1)).then_inc(w_ld, 16)

            def row_copy(n, g, t, b, turn):
                act.wait_ge(xp_ok, n + 1)
                if t == 0 and known(g, 2):
                    act.wait_ge(tab_st[b], 16 * turn)
                    act.wait_ge(asd_ok, g - 1)
                nc.scalar.copy(po[b][:, t, :], ag_ps[(b + t) % 2][:, 0:WIDE]).then_inc(xpc_ok, 1)

            def batch_copies(g, turn, b, r, q):
                for t in range(BATCH):
                    n = BATCH * g + t
                    act.wait_ge(trb_ok, n + 1)
                    if known(n, 2):
                        act.wait_ge(xp_ok, n - 1)
                    nc.scalar.copy(xnT2[:, (b + t) % 2], tr2[(b + t) % 2]).then_inc(trc_ok, 1)
                    if t >= 1:
                        row_copy(n - 1, g, t - 1, b, turn)
                row_copy(BATCH * g + BATCH - 1, g, BATCH - 1, b, turn)

            batches(act, batch_copies)
            act.wait_ge(sdiff_ok, 1)
            nc.scalar.activation(exself[:, :, :], exself[:, :, :], ACT.Exp).then_inc(exself_ok, 1)
            act.wait_ge(win_ld, 16)
            act.wait_ge(w_ld, 16 * LOADS)

            def turn(w):
                act.wait_ge(tr_ok, w + 1)
                if known(w, 1):
                    act.wait_ge(h_ok, FC * w)
                nc.scalar.copy(xnT[:, :, :], tr2[0]).then_inc(xnT_ok, 1)

            def gelu(w):
                if known(w, 1):
                    act.wait_ge(y_ok, w)
                for m in range(FC):
                    if m % IN_BANK == 0:
                        act.wait_ge(h_ok, FC * w + m + IN_BANK)
                    nc.scalar.activation(hT[:, m, :], h_ps[:, m * P:(m + 1) * P], ACT.Gelu_apprx_tanh, bias=b1s[:, m:m + 1]).then_inc(hT_ok, 1)

            def store(w, i, b):
                act.wait_ge(y_ok, w + 1)
                if known(w, 2):
                    act.wait_ge(y_st[b], 16 * i)
                nc.scalar.copy(yb[:, b, :], y_ps[:, 0:D]).then_inc(yb_ok, 1)
                act.wait_ge(yb_ok, w + 1)
                act.dma_start(y_dram[bass.ds(w * P, P), :], yb[:, b, :]).then_inc(y_st[b], 16)

            def window(w, i, b):
                act.wait_ge(diff_ok, w + 1)
                nc.scalar.activation(rows[:, b, :, D:ROW], diff[:, :, :], ACT.Exp).then_inc(ex_ok, 1)

                def extra_exp(j, k):
                    act.wait_ge(x_diff, k + 1)
                    nc.scalar.activation(xrow[:, D:ROW], xdiff[:, :], ACT.Exp).then_inc(x_ex, 1)

                if known(w, 2):
                    gelu(w - 2)
                for_extra(act, w, extra_exp)
                if known(w, 1):
                    after_sum(w - 1)
                if known(w, 2):
                    store(w - 2, i - 1, b)
                if known(w, 1):
                    turn(w - 1)

            def after_sum(w):
                act.wait_ge(zmin_ok, w + 1)
                nc.scalar.activation(zexp[:, :], zmin[:, :], ACT.Exp).then_inc(zexp_ok, 1)
                act.wait_ge(ve_ok, w + 1)
                nc.scalar.activation(lnv[:, :], vareps[:, :], ACT.Ln).then_inc(ln_ok, 1)
                act.wait_ge(ln_ok, w + 1)
                nc.scalar.activation(rs0[:, :], lnv[:, :], ACT.Exp, scale=-0.5).then_inc(rs0_ok, 1)

            two_by_two(act, PAIRS, window)
            gelu(NW - 2)
            after_sum(NW - 1)
            store(NW - 2, PAIRS - 1, 0)
            turn(NW - 1)
            gelu(NW - 1)
            store(NW - 1, PAIRS - 1, 1)
            act.wait_ge(agg_ok, NW)
            act.wait_ge(oh_ok, NW)
            act.wait_ge(y_st[0], 16 * PAIRS)
            act.wait_ge(y_st[1], 16 * PAIRS)
            for g in range(NB):
                if g >= YIN:
                    act.wait_ge(out_ok, g - YIN + 1)
                act.dma_start(yin[g % YIN], nodes(y_dram, g * BATCH, BATCH)).then_inc(y_ld[g % YIN], 16)

        @block.tensor
        def _(pe):
            pe.sem_inc(x_done, 1)
            pe.sem_inc(m_done, 1)
            pe.wait_ge(pool_const, CONSTS)

            def project(n, t, b):
                if isinstance(n, int) and n == 0:
                    pe.wait_ge(wext_ok, 1)
                    pe.wait_ge(gb_ok, 1)
                pe.wait_ge(trc_ok, n + 1)
                if known(n, 2):
                    pe.wait_ge(xpc_ok, n - 1)
                into = ag_ps[(b + t) % 2][:, 0:WIDE]
                for c in range(DC):
                    nc.tensor.matmul(into, xnT2[:, (b + t) % 2, c, :], wext[:, c, :], start=(c == 0), stop=False)
                nc.tensor.matmul(into, ones_bf[:, :], gb_parts[:, :], start=False, stop=True).then_inc(xp_ok, 1)

            def batch_products(g, turn, b, r, q):
                pe.wait_ge(norm_ok, g + 1)
                for t in range(BATCH):
                    n = BATCH * g + t
                    if known(n, 2):
                        pe.wait_ge(trc_ok, n - 1)
                    for c in range(DC):
                        last = nc.tensor.transpose(tr2[(b + t) % 2][:, c, :], nb[b][:, t, c * P:(c + 1) * P], ident[:, :])
                    last.then_inc(trb_ok, 1)
                    if t >= 1:
                        project(n - 1, t - 1, b)
                project(BATCH * g + BATCH - 1, BATCH - 1, b)

            batches(pe, batch_products)
            pe.wait_ge(count_ok, 1)
            nc.tensor.matmul(y_ps[0:NW, 0:2], below[0:NW, 0:NW], count_f[0:NW, :], start=True, stop=True).then_inc(before_ok, 1)
            pe.wait_ge(win_ld, 16)
            pe.wait_ge(exact_ok, 1)

            def exact_turn(w, j, k):
                pe.wait_ge(m_mask, k + 1)
                for h in range(H):
                    last = nc.tensor.transpose(xl_ps[:, h * P:(h + 1) * P], xmask[:, h, :], ident[:, :])
                last.then_inc(m_tr, 1)

            if_exact(pe, exact_turn)
            pe.wait_ge(parts_ok, 3)
            pe.wait_ge(b2_ok, 1)
            pe.wait_ge(w_ld, 16 * LOADS)

            def node_parts(w):
                return parts[:, bass.ds(w, 1), :, :].rearrange("p w v k -> p (w v k)")

            def look_up(w, b):
                pe.wait_ge(oht_ok, w + 1)
                if known(w, 1):
                    pe.wait_ge(dm_ok, w)
                by_tile = oht[:, b, :].rearrange("p (e t) -> p t e", t=TILES)
                for t in range(TILES):
                    last = nc.tensor.matmul(lk_ps[:, VK * t:VK * (t + 1)], by_tile[:, t, :], node_parts(w), start=True, stop=True)
                last.then_inc(lk_ok, 1)

            def turn(w):
                pe.wait_ge(xn_ok, w + 1)
                if known(w, 1):
                    pe.wait_ge(xnT_ok, w)
                for c in range(DC):
                    last = nc.tensor.transpose(tr2[0][:, c, :], xn[:, c * P:(c + 1) * P], ident[:, :])
                last.then_inc(tr_ok, 1)

            def hidden(w):
                pe.wait_ge(xnT_ok, w + 1)
                if known(w, 1):
                    pe.wait_ge(hT_ok, FC * w)
                for m in range(FC):
                    for c in range(DC):
                        last = nc.tensor.matmul(h_ps[:, m * P:(m + 1) * P], w1s[:, c, m * P:(m + 1) * P], xnT[:, c, :],
                                                start=(c == 0), stop=(c == DC - 1))
                    last.then_inc(h_ok, 1)

            def ffn_out(w):
                if known(w, 1):
                    pe.wait_ge(yb_ok, w)
                for m in range(FC):
                    pe.wait_ge(hT_ok, FC * w + m + 1)
                    nc.tensor.matmul(y_ps[:, 0:D], hT[:, m, :], w2s[:, m, :], start=(m == 0), stop=False)
                nc.tensor.matmul(y_ps[:, 0:D], ones_bf[:, :], b2_parts[:, :], start=False, stop=True).then_inc(y_ok, 1)

            def window(w, i, b):
                pe.wait_ge(oh_ok, w + 1)
                if known(w, 2):
                    pe.wait_ge(zn_ok, w - 1)
                for t in range(TILES):
                    pe.wait_ge(scaled, w * NP + piece_of[t] + 1)
                    nc.tensor.matmul(ag_ps[b][:, 0:ROW], oh[:, b, t, :], rows[:, b, t, :], start=(t == 0), stop=False).then_inc(tile_done, 1)

                def extra_products(j, k):
                    pe.wait_ge(x_oht, k + 1)
                    nc.tensor.matmul(xl_ps[:, 0:VK], xoht[:, :], node_parts(w), start=True, stop=True).then_inc(x_lk, 1)
                    pe.wait_ge(x_sc, k + 1)
                    nc.tensor.matmul(ag_ps[b][:, 0:ROW], xoh[:, :], xrow[:, :], start=False, stop=False).then_inc(x_done, 1)

                for_extra(pe, w, extra_products)
                pe.wait_ge(self_ok, w + 1)
                nc.tensor.matmul(ag_ps[b][:, 0:ROW], ident[:, :], selfr[:, b, :], start=False, stop=True).then_inc(agg_ok, 1)
                if not isinstance(w, int) or w + 1 < NW:
                    look_up(w + 1, 1 - b)
                if known(w, 2):
                    ffn_out(w - 2)
                if known(w, 1):
                    turn(w - 1)
                    hidden(w - 1)

            look_up(0, 0)
            two_by_two(pe, PAIRS, window, last_peeled=True)
            ffn_out(NW - 2)
            turn(NW - 1)
            hidden(NW - 1)
            for r in range(ROUNDS):
                if r == 3:
                    ffn_out(NW - 1)
                pe.wait_ge(cnt_ok, r + 1)
                nc.tensor.matmul(lk_ps[:, 0:3], ones[:, :], cnt[:, :], start=True, stop=True).then_inc(tot_ok, 1)
            pe.wait_ge(tie_ok, 1)
            nc.tensor.matmul(lk_ps[:, 0:NW], below[:, :], tie, start=True, stop=True)
            nc.tensor.matmul(xl_ps[:, 0:NW], ones[:, :], tie, start=True, stop=True).then_inc(rank_ok, 1)

        @block.vector
        def _(dve):
            taken = [0]

            def then(ins):
                taken[0] += 1
                ins.then_inc(pre, 1)
                dve.wait_ge(pre, taken[0])

            def attention_columns():
                dve.wait_ge(att_ld, 16 * 3)
                for n in range(2 * DC):
                    last = nc.vector.tensor_tensor(wext_mul[n][:, :], wext[:, n % DC, 0:D], att_b[n // DC], ALU.mult)
                last.then_inc(wext_mul_ok, 1)
                dve.wait_ge(wext_mul_ok, 1)
                for n in range(2 * DC):
                    k = ROW - H + n // DC * H
                    last = nc.vector.tensor_reduce(wext[:, n % DC, k:k + H], wext_mul[n][:, :].rearrange("p (h c) -> p h c", h=H), AXX, ALU.add)
                last.then_inc(wext_ok, 1)

            def norm(g, b, q):
                dve.wait_ge(rstd_b, g + 1)
                if known(g, 2):
                    dve.wait_ge(trb_ok, BATCH * (g - 1))
                for t in range(BATCH):
                    last = nc.vector.tensor_scalar(nb[b][:, t, :], xb[q][:, t, :], mv_b[:, b, t, 0:1], rs_b[:, b, t:t + 1], ALU.subtract, ALU.mult)
                last.then_inc(norm_ok, 1)

            def keep_asd(g, b):
                dve.wait_ge(xpc_ok, BATCH * (g + 1))
                nc.vector.tensor_copy(asd[:, bass.ds(g * BATCH, BATCH), :], po[b][:, :, D:WIDE]).then_inc(asd_ok, 1)

            def batch_stats(g, turn, b, r, q):
                wait_apart(dve, (x_ld[q], 16 * (r + 1)), *([(aggr_ok, g)] if known(g, 1) else []))
                for t in range(BATCH):
                    last = nc.vector.bn_stats(st_b[:, t, :], xb[q][:, t, :])
                last.then_inc(stat_ok, 1)
                wait_apart(dve, (stat_ok, g + 1))
                for t in range(BATCH):
                    last = nc.vector.bn_aggr(mv_b[:, b, t, :], st_b[:, t, :])
                last.then_inc(aggr_ok, 1)
                if isinstance(g, int) and g == 0:
                    attention_columns()
                    norm(0, 0, 0)
                if isinstance(g, int) and g == 1:
                    dve.wait_ge(falls_ok, 1)
                    nc.vector.tensor_reduce(broken[:, :], falls, AXX, ALU.max).then_inc(fall_ok, 1)
                if known(g, 2):
                    norm(g - 1, 1 - b, (q - 1) % DEEP)
                    keep_asd(g - 2, b)
                if isinstance(g, int) and g == NB - DEEP:
                    dve.wait_ge(pool_const, CONSTS)
                    dve.wait_ge(blk_ld, 32)
                    nc.vector.tensor_scalar(hi_b, hi_b, wv[0:NW, 0:1], 0.0, ALU.is_lt, ALU.add, accum_out=wv[0:NW, 2:3])
                    then(nc.vector.tensor_scalar(lo_b, lo_b, wv[0:NW, 1:2], 0.0, ALU.is_le, ALU.add, accum_out=wv[0:NW, 3:4]))
                    dve.wait_ge(broken_ok, 1)
                    then(nc.vector.tensor_scalar(broken_all[:, :], broken_all[:, :], 0.0, None, ALU.is_gt))
                    then(nc.vector.tensor_scalar(wv[0:NW, 7:8], broken_all[0:NW, :], -1.0, 1.0, ALU.mult, ALU.add))
                    then(nc.vector.tensor_scalar(wv[0:NW, 4:5], wv[0:NW, 2:3], wv[0:NW, 7:8], None, ALU.mult))
                    then(nc.vector.scalar_tensor_tensor(out=wv[0:NW, 3:4], in0=broken_all[0:NW, :], scalar=float(NBLK), in1=wv[0:NW, 3:4], op0=ALU.mult, op1=ALU.max))
                if isinstance(g, int) and g == NB - DEEP + 1:
                    then(nc.vector.tensor_scalar(wv[0:NW, 5:6], wv[0:NW, 4:5], float(NBLK - FB), float(BLOCK), ALU.min, ALU.mult))
                    then(nc.vector.tensor_copy(wi[0:NW, 0:1], wv[0:NW, 5:6]))
                    then(nc.vector.tensor_scalar(wv[0:NW, 5:6], wv[0:NW, 5:6], -1.0 / BLOCK, float(PB - 1), ALU.mult, ALU.add))
                    then(nc.vector.tensor_tensor(wv[0:NW, 6:7], wv[0:NW, 3:4], wv[0:NW, 5:6], ALU.add))
                    then(nc.vector.tensor_scalar(i1[0:NW, 0:1], wv[0:NW, 6:7], float(-FB), None, ALU.add))
                    then(nc.vector.tensor_copy(i1[0:NW, 1:2], wv[0:NW, 6:7]))
                    then(nc.vector.tensor_scalar(i2[0:NW, :], i1[0:NW, :], PB.bit_length() - 1, None, ALU.arith_shift_right))
                    then(nc.vector.tensor_scalar(count_f[0:NW, :], i2[0:NW, :], 0.0, None, ALU.max))
                    then(nc.vector.tensor_copy(wi[0:NW, 1:2], count_f[0:NW, 0:1]))
                    nc.vector.tensor_copy(wi[0:NW, 3:4], count_f[0:NW, 1:2]).then_inc(count_ok, 1)

            batches(dve, batch_stats, last_peeled=True)
            norm(NB - 1, 1, (NB - 1) % DEEP)
            keep_asd(NB - 2, 0)
            dve.wait_ge(before_ok, 1)
            then(nc.vector.tensor_copy(wi[0:NW, 2:3], y_ps[0:NW, 0:1]))
            nc.vector.tensor_copy(wi[0:NW, 4:5], y_ps[0:NW, 1:2]).then_inc(win_ok, 1)
            keep_asd(NB - 1, 1)
            dve.wait_ge(asd_ok, NB)
            by_head = asd[:, :, 0:H].rearrange("p w h -> p h w")
            nc.vector.tensor_reduce(gmax[:, 0:H], by_head, AXX, ALU.max).then_inc(gmax_ok, 1)
            then(nc.vector.tensor_reduce(spread[:, :], by_head, AXX, ALU.min))
            nc.vector.tensor_scalar(gmax[:, H:2 * H], spread[:, :], -1.0, None, ALU.mult).then_inc(gmax_ok, 1)
            dve.wait_ge(gall_ok, 1)
            then(nc.vector.tensor_tensor(spread[:, :], gall[:, 0:H], gall[:, H:2 * H], ALU.add))
            then(nc.vector.tensor_reduce(widest[:, :], spread[:, :], AXX, ALU.max))
            then(nc.vector.tensor_copy(dm[:, :, 0:H], asd[:, :, H:2 * H]))
            then(nc.vector.tensor_copy(dm[:, :, H:2 * H], gall[:, 0:H].unsqueeze(1).broadcast_to([P, NW, H])))
            nc.vector.tensor_scalar(exact[:, :], widest[:, :], SPREAD, None, ALU.is_gt).then_inc(exact_ok, 1)
            dve.wait_ge(exact_ok, 1)
            dve.wait_ge(win_ld, 16)
            flag = dve.value_load(exact[0:1, 0:1], min_val=0, max_val=1)
            with dve.If(flag > 0):
                nc.vector.tensor_copy(dm[:, :, H:2 * H], asd[:, :, 0:H]).then_inc(m_max, 1)
                dve.wait_ge(m_max, 1)

            def exact_max(w, j, k):
                dve.wait_ge(m_dst, 16 * k + 16)
                nc.vector.tensor_scalar(xloc[:, :], xdst[:, :], base_id[:, bass.ds(w, 1)], None, ALU.subtract).then_inc(m_loc, 1)
                dve.wait_ge(m_loc, k + 1)
                nc.vector.tensor_scalar(xoh[:, :], iota_d[:, :], xloc[:, 0:1], None, ALU.is_equal).then_inc(m_oh, 1)
                dve.wait_ge(m_oh, k + 1)
                nc.vector.tensor_scalar(xpen, xoh[:, :], 1.0, 1e38, ALU.subtract, ALU.mult).then_inc(m_pen, 1)
                dve.wait_ge(m_pen, k + 1)
                dve.wait_ge(m_row, 16 * k + 16)
                nc.vector.tensor_tensor(xmask[:, :, :], xpen.unsqueeze(1).broadcast_to([P, H, P]),
                                        xrow[:, D:ROW].unsqueeze(2).broadcast_to([P, H, P]), ALU.add).then_inc(m_mask, 1)
                dve.wait_ge(m_tr, k + 1)
                nc.vector.tensor_reduce(xmax[:, :], xl_ps[:, :].rearrange("p (h e) -> p h e", h=H), AXX, ALU.max).then_inc(m_max, 1)
                dve.wait_ge(m_max, k + 2)
                mx = dm[:, bass.ds(w, 1), H:2 * H].rearrange("p w h -> p (w h)")
                nc.vector.tensor_tensor(mx, mx, xmax[:, :], ALU.max).then_inc(m_done, 1)
                dve.wait_ge(m_done, k + 2)

            if_exact(dve, exact_max)
            def flat(a):
                return a.rearrange("p w h -> p (w h)")

            then(nc.vector.tensor_tensor(sz[:, :, :], asd[:, :, 0:H], dm[:, :, 0:H], ALU.add))
            then(nc.vector.tensor_tensor(sm[:, :, :], dm[:, :, H:2 * H], dm[:, :, 0:H], ALU.add))
            then(nc.vector.scalar_tensor_tensor(out=flat(sz[:, :, :]), in0=flat(sz[:, :, :]), scalar=SLOPE, in1=flat(sz[:, :, :]), op0=ALU.mult, op1=ALU.max))
            then(nc.vector.scalar_tensor_tensor(out=flat(sm[:, :, :]), in0=flat(sm[:, :, :]), scalar=SLOPE, in1=flat(sm[:, :, :]), op0=ALU.mult, op1=ALU.max))
            nc.vector.tensor_tensor(exself[:, :, :], sz[:, :, :], sm[:, :, :], ALU.subtract).then_inc(sdiff_ok, 1)
            then(nc.vector.tensor_copy(dm[:, :, H:2 * H], sm[:, :, :]))
            nc.vector.tensor_copy(parts[:, :, :, 0], dm[:, :, :]).then_inc(parts_ok, 1)
            dve.wait_ge(parts_ok, 1)
            then(nc.vector.tensor_tensor(left[:, :, :], dm[:, :, :], parts[:, :, :, 0], ALU.subtract))
            nc.vector.tensor_copy(parts[:, :, :, 1], left[:, :, :]).then_inc(parts_ok, 1)
            dve.wait_ge(parts_ok, 2)
            then(nc.vector.tensor_tensor(left[:, :, :], left[:, :, :], parts[:, :, :, 1], ALU.subtract))
            nc.vector.tensor_copy(parts[:, :, :, 2], left[:, :, :]).then_inc(parts_ok, 1)
            dve.wait_ge(exself_ok, 1)
            dve.wait_ge(w_ld, 16 * LOADS)
            dve.wait_ge(parts_ok, 3)

            def one_hots_turned(w, i, b):
                dve.wait_ge(ld_dbc[b], 16 * (i + 1))
                nc.vector.tensor_scalar(oht[:, b, :], dbc[:, b, :], node_id[:, bass.ds(w, 1)], None, ALU.is_equal).then_inc(oht_ok, 1)
                dve.wait_ge(ld_dst[b], 16 * (i + 1))
                nc.vector.tensor_scalar(dloc[:, :], dsti[:, b, :], base_id[:, bass.ds(w, 1)], None, ALU.subtract).then_inc(loc_ok, 1)

            def one_hots(w, b):
                dve.wait_ge(loc_ok, w + 1)
                nc.vector.tensor_tensor(oh[:, b, :, :], iota_d[:, :].unsqueeze(1).broadcast_to([P, TILES, P]),
                                        dloc[:, :].unsqueeze(2).broadcast_to([P, TILES, P]), ALU.is_equal).then_inc(oh_ok, 1)

            def exponents(w, i, b):
                dve.wait_ge(lk_ok, w + 1)
                nc.vector.tensor_reduce(edge_dm[:, :, :].rearrange("p t v -> p (t v)"), lk_ps[:, 0:TILES * VK].rearrange("p (v k) -> p v k", k=3), AXX, ALU.add).then_inc(dm_ok, 1)
                dve.wait_ge(dm_ok, w + 1)
                dve.wait_ge(gath[b], 16 * TILES * (i + 1))
                nc.vector.tensor_tensor(zz[:, :, :], rows[:, b, :, D:ROW], edge_dm[:, :, 0:H], ALU.add).then_inc(zs_ok, 1)
                dve.wait_ge(zs_ok, w + 1)
                za = zz[:, :, :].rearrange("p t h -> p (t h)")
                nc.vector.scalar_tensor_tensor(out=zl[:, :, :].rearrange("p t h -> p (t h)"), in0=za, scalar=SLOPE, in1=za, op0=ALU.mult, op1=ALU.max).then_inc(zl_ok, 1)
                dve.wait_ge(zl_ok, w + 1)
                nc.vector.tensor_tensor(zc[:, :, :], zl[:, :, :], edge_dm[:, :, H:2 * H], ALU.min).then_inc(zm_ok, 1)
                dve.wait_ge(zm_ok, w + 1)
                nc.vector.tensor_tensor(diff[:, :, :], zc[:, :, :], edge_dm[:, :, H:2 * H], ALU.subtract).then_inc(diff_ok, 1)

            def weigh(w, i, b):
                dve.wait_ge(ex_ok, w + 1)
                for a, m in PIECES:
                    v = rows[:, b, a:a + m, 0:D].rearrange("p t (h c) -> p t h c", h=H)
                    e = rows[:, b, a:a + m, D:ROW].unsqueeze(3).broadcast_to([P, m, H, C])
                    nc.vector.tensor_tensor(v, v, e, ALU.mult).then_inc(scaled, 1)

            def weigh_self(w, i, b):
                dve.wait_ge(ld_self[b], 16 * (i + 1))
                e = exself[:, bass.ds(w, 1), :].rearrange("p w h -> p (w h)")
                v = selfr[:, b, 0:D].rearrange("p (h c) -> p h c", h=H)
                nc.vector.tensor_tensor(v, v, e.unsqueeze(2).broadcast_to([P, H, C]), ALU.mult).then_inc(selfx_ok, 1)
                nc.vector.tensor_copy(selfr[:, b, D:ROW], e).then_inc(self_ok, 1)

            def extra_tile(w, k):
                dve.wait_ge(x_dbc, 16 * k + 16)
                nc.vector.tensor_scalar(xoht[:, :], xdbc[:, :], node_id[:, bass.ds(w, 1)], None, ALU.is_equal).then_inc(x_oht, 1)
                dve.wait_ge(x_dst, 16 * k + 16)
                nc.vector.tensor_scalar(xloc[:, :], xdst[:, :], base_id[:, bass.ds(w, 1)], None, ALU.subtract).then_inc(x_loc, 1)
                dve.wait_ge(x_loc, k + 1)
                nc.vector.tensor_scalar(xoh[:, :], iota_d[:, :], xloc[:, 0:1], None, ALU.is_equal).then_inc(x_oh, 1)
                dve.wait_ge(x_lk, k + 1)
                nc.vector.tensor_reduce(xdm[:, :], xl_ps[:, 0:VK].rearrange("p (v k) -> p v k", k=3), AXX, ALU.add).then_inc(x_dm, 1)
                dve.wait_ge(x_dm, k + 1)
                dve.wait_ge(x_row, 16 * k + 16)
                nc.vector.tensor_tensor(xzz[:, :], xrow[:, D:ROW], xdm[:, 0:H], ALU.add).then_inc(x_zs, 1)
                dve.wait_ge(x_zs, k + 1)
                nc.vector.scalar_tensor_tensor(out=xzl[:, :], in0=xzz[:, :], scalar=SLOPE, in1=xzz[:, :], op0=ALU.mult, op1=ALU.max).then_inc(x_zl, 1)
                dve.wait_ge(x_zl, k + 1)
                nc.vector.tensor_tensor(xzc[:, :], xzl[:, :], xdm[:, H:2 * H], ALU.min).then_inc(x_zm, 1)
                dve.wait_ge(x_zm, k + 1)
                nc.vector.tensor_tensor(xdiff[:, :], xzc[:, :], xdm[:, H:2 * H], ALU.subtract).then_inc(x_diff, 1)
                dve.wait_ge(x_ex, k + 1)
                dve.wait_ge(x_oh, k + 1)
                v = xrow[:, 0:D].rearrange("p (h c) -> p h c", h=H)
                nc.vector.tensor_tensor(v, v, xrow[:, D:ROW].unsqueeze(2).broadcast_to([P, H, C]), ALU.mult).then_inc(x_sc, 1)

            def residual(w, i, b):
                dve.wait_ge(agg_ok, w + 1)
                nc.vector.reciprocal(rden[:, :], ag_ps[b][:, D:ROW]).then_inc(rden_ok, 1)
                dve.wait_ge(rden_ok, w + 1)
                nc.vector.tensor_tensor(zag[:, :].rearrange("p (h c) -> p h c", h=H), ag_ps[b][:, 0:D].rearrange("p (h c) -> p h c", h=H),
                                        rden[:, :].unsqueeze(2).broadcast_to([P, H, C]), ALU.mult).then_inc(zn_ok, 1)
                dve.wait_ge(zn_ok, w + 1)
                nc.vector.tensor_scalar(zmin[:, :], zag[:, :], 0.0, None, ALU.min).then_inc(zmin_ok, 1)
                dve.wait_ge(ld_x[b], 16 * (i + 1))
                x1 = base[:, bass.ds(w, 1), :].rearrange("p w c -> p (w c)")
                nc.vector.scalar_tensor_tensor(out=zag[:, :], in0=zag[:, :], scalar=0.0, in1=x1, op0=ALU.max, op1=ALU.add).then_inc(xa_ok, 1)
                dve.wait_ge(xa_ok, w + 1)
                dve.wait_ge(zexp_ok, w + 1)
                nc.vector.scalar_tensor_tensor(out=x1, in0=zexp[:, :], scalar=-1.0, in1=zag[:, :], op0=ALU.add, op1=ALU.add).then_inc(x1_ok, 1)
                wait_apart(dve, (x1_ok, w + 1))
                nc.vector.bn_stats(st6[:, :], x1).then_inc(st_ok, 1)
                wait_apart(dve, (st_ok, w + 1))
                nc.vector.bn_aggr(mv[:, :], st6[:, :]).then_inc(mv_ok, 1)
                dve.wait_ge(mv_ok, w + 1)
                nc.vector.tensor_scalar(vareps[:, :], mv[:, 1:2], EPS, None, ALU.add).then_inc(ve_ok, 1)

            def route(w, b):
                dve.wait_ge(rs0_ok, w + 1)
                nc.vector.scalar_tensor_tensor(out=sq[:, :], in0=rs0[:, :], scalar=rs0[:, 0:1], in1=vareps[:, :], op0=ALU.mult, op1=ALU.mult).then_inc(sq_ok, 1)
                dve.wait_ge(sq_ok, w + 1)
                nc.vector.tensor_scalar(half[:, :], sq[:, :], -0.5, 1.5, ALU.mult, ALU.add).then_inc(half_ok, 1)
                dve.wait_ge(half_ok, w + 1)
                nc.vector.tensor_tensor(rstd[:, :], rs0[:, :], half[:, :], ALU.mult).then_inc(rstd_ok, 1)
                dve.wait_ge(rstd_ok, w + 1)
                if known(w, 1):
                    dve.wait_ge(tr_ok, w)
                x1 = base[:, bass.ds(w, 1), :].rearrange("p w c -> p (w c)")
                nc.vector.tensor_scalar(xn[:, :], x1, mv[:, 0:1], rstd[:, 0:1], ALU.subtract, ALU.mult).then_inc(xn_ok, 1)
                dve.wait_ge(xn_ok, w + 1)
                nc.vector.tensor_tensor(x1, x1, xn[:, :], ALU.add).then_inc(base_ok, 1)
                nc.vector.tensor_tensor_reduce(junk[:, :], xn[:, :], wrs[:, :], 1.0, 0.0, ALU.mult, ALU.add, wcol[:, b:b + 1]).then_inc(wcol_ok, 1)
                dve.wait_ge(wcol_ok, w + 1)
                nc.vector.tensor_copy(wt[:, bass.ds(w, 1)], wcol[:, b:b + 1]).then_inc(wt_ok, 1)

            def window(w, i, b):
                more = not isinstance(w, int) or w + 1 < NW
                exponents(w, i, b)
                weigh(w, i, b)
                weigh_self(w, i, b)
                if more:
                    one_hots_turned(w + 1, i + b, 1 - b)
                for_extra(dve, w, lambda j, k: extra_tile(w, k))
                if known(w, 1):
                    residual(w - 1, i - 1 + b, 1 - b)
                if more:
                    one_hots(w + 1, 1 - b)
                if known(w, 1):
                    route(w - 1, 1 - b)

            one_hots_turned(0, 0, 0)
            one_hots(0, 0)
            two_by_two(dve, PAIRS, window, last_peeled=True)
            residual(NW - 1, PAIRS - 1, 1)
            route(NW - 1, 1)
            dve.wait_ge(wt_ok, NW)
            dve.wait_ge(base_ok, NW)
            then(nc.vector.tensor_scalar(wt[:, :], wt[:, :], brs[:, 0:1], None, ALU.add))
            bits = wt[:, :].bitcast(I32)
            then(nc.vector.tensor_scalar(sgn, bits, 31, None, ALU.arith_shift_right))
            then(nc.vector.tensor_scalar(sgn, sgn, -2 ** 31, None, ALU.bitwise_or))
            then(nc.vector.tensor_tensor(key, bits, sgn, ALU.bitwise_xor))
            then(nc.vector.tensor_scalar(sgn, key, 16, 0xffff, ALU.logical_shift_right, ALU.bitwise_and))
            then(nc.vector.tensor_copy(khi, sgn))
            then(nc.vector.tensor_scalar(sgn, key, 0xffff, None, ALU.bitwise_and))
            then(nc.vector.tensor_copy(klo, sgn))
            then(nc.vector.tensor_scalar(valid, node_id[:, :], float(N), None, ALU.is_lt))
            then(nc.vector.scalar_tensor_tensor(out=khi, in0=khi, scalar=1.0, in1=valid, op0=ALU.add, op1=ALU.mult))
            then(nc.vector.tensor_scalar(khi, khi, -1.0, None, ALU.add))
            then(nc.vector.memset(kth[:, :], float(K)))
            then(nc.vector.memset(cnt[:, :], 0.0))
            rounds = [0]

            def totals():
                rounds[0] += 1
                dve.wait_ge(tot_ok, rounds[0])

            def search(keys):
                then(nc.vector.memset(cur[:, :], 0.0))
                for place in range(7, -1, -1):
                    step = float(4 ** place)
                    then(nc.vector.tensor_scalar(thr[:, :], iota_d[:, 1:4], step, cur[:, 0:1], ALU.mult, ALU.add))
                    for j in range(3):
                        last = nc.vector.tensor_scalar(marks[j], keys, thr[:, j:j + 1], 0.0, ALU.is_ge, ALU.add, accum_out=cnt[:, j:j + 1])
                    last.then_inc(cnt_ok, 1)
                    totals()
                    then(nc.vector.tensor_scalar(got[:, :], lk_ps[:, 0:3], kth[:, 0:1], 0.0, ALU.is_ge, ALU.add, accum_out=nge[:, :]))
                    then(nc.vector.tensor_scalar(cur[:, :], nge[:, :], step, cur[:, 0:1], ALU.mult, ALU.add))

            def take_above(keys):
                then(nc.vector.tensor_scalar(above, keys, cur[:, 0:1], None, ALU.is_gt))
                nc.vector.tensor_reduce(cnt[:, 0:1], above, AXX, ALU.add).then_inc(cnt_ok, 1)
                totals()
                then(nc.vector.tensor_tensor(kth[:, :], kth[:, :], lk_ps[:, 0:1], ALU.subtract))

            search(khi)
            take_above(khi)
            then(nc.vector.tensor_tensor(coef, above, wt[:, :], ALU.mult))
            then(nc.vector.tensor_scalar(tie, khi, cur[:, 0:1], None, ALU.is_equal))
            then(nc.vector.scalar_tensor_tensor(out=klo, in0=klo, scalar=1.0, in1=tie, op0=ALU.add, op1=ALU.mult))
            then(nc.vector.tensor_scalar(klo, klo, -1.0, None, ALU.add))
            search(klo)
            take_above(klo)
            nc.vector.tensor_scalar(tie, klo, cur[:, 0:1], None, ALU.is_equal).then_inc(tie_ok, 1)
            dve.wait_ge(rank_ok, 1)
            then(nc.vector.tensor_copy(col, xl_ps[:, 0:NW]))
            then(nc.vector.tensor_tensor_scan(rank, ones[:, 0:NW], col, 0.0, ALU.mult, ALU.add))
            then(nc.vector.tensor_tensor(rank, rank, col, ALU.subtract))
            then(nc.vector.tensor_tensor(rank, rank, lk_ps[:, 0:NW], ALU.add))
            then(nc.vector.scalar_tensor_tensor(out=tie, in0=rank, scalar=kth[:, 0:1], in1=tie, op0=ALU.is_lt, op1=ALU.mult))
            then(nc.vector.tensor_tensor(tie, tie, above, ALU.add))
            then(nc.vector.tensor_tensor(tie, tie, wt[:, :], ALU.mult))
            then(nc.vector.tensor_tensor(coef, coef, tie, ALU.add))
            for g in range(NB):
                dve.wait_ge(y_ld[g % YIN], 16 * (g // YIN + 1))
                for t in range(BATCH):
                    w = g * BATCH + t
                    last = nc.vector.scalar_tensor_tensor(out=base[:, w, :], in0=yin[g % YIN][:, t, :], scalar=coef[:, w:w + 1], in1=base[:, w, :], op0=ALU.mult, op1=ALU.add)
                last.then_inc(out_ok, 1)


def kernel(**inputs):
    import numpy as np
    import concourse.bacc as bacc
    from concourse import mybir as my
    from concourse.bass_utils import run_bass_kernel_spmd as run

    arrays = {k: np.ascontiguousarray(v) for k, v in inputs.items() if k != "L0_ffn_attention_mask"}
    n, e = arrays["x"].shape[0], arrays["src"].shape[0]
    nw, _, ep = sizes(n, e)
    arrays["x"] = np.pad(arrays["x"], ((0, nw * P - n), (0, 0)))
    arrays["src"] = np.pad(arrays["src"], (0, ep - e))
    arrays["dst"] = np.pad(arrays["dst"], (0, ep - e), constant_values=nw * P)
    nc = bacc.Bacc("TRN2", target_bir_lowering=False, num_devices=1)
    ins = {k: nc.dram_tensor(f"in_{k}", a.shape, my.dt.from_np(a.dtype), kind="ExternalInput").ap() for k, a in arrays.items()}
    out = nc.dram_tensor("out", arrays["x"].shape, F32, kind="ExternalOutput").ap()
    build(nc, ins["x"], ins["src"], ins["dst"], ins["L0_gnn_W"], ins["L0_gnn_att_src"], ins["L0_gnn_att_dst"],
          ins["L0_gnn_bias"], ins["L0_ffn_wr"], ins["L0_ffn_br"], ins["L0_ffn_w1"], ins["L0_ffn_b1"],
          ins["L0_ffn_w2"], ins["L0_ffn_b2"], out, n, e)
    r = run(nc, [{f"in_{k}": a for k, a in arrays.items()}], core_ids=[0])
    return r.results[0]["out"][:n]
```

```python
from contextlib import ExitStack

import concourse.bass as bass
from concourse import mybir

F32 = mybir.dt.float32
BF16 = mybir.dt.bfloat16
I32 = mybir.dt.int32
I16 = mybir.dt.int16
ALU = mybir.AluOpType
ACT = mybir.ActivationFunctionType
AXX = mybir.AxisListType.X

P = 128
EPS = 1e-5
SLOPE = 0.2
BLOCK = 32
SPREAD = 40.0


def sizes(n, e):
    nw = -(-n // P)
    tiles = -(-e // n) + 1
    ep = -(-(e + P * (tiles + 1)) // (P * BLOCK)) * P * BLOCK
    return nw, tiles, ep


def build(nc, x, src, dst, W, att_src, att_dst, gbias, wr, br, w1, b1, w2, b2, out, N, E):
    D = W.shape[0]
    H, C = att_src.shape
    F = w1.shape[1]
    NW, TILES, EP = sizes(N, E)
    BATCH = 7
    PAIRS = NW // 2
    K = max(1, int(0.5 * N)) - 1
    ROW = D + H
    DC, FC = D // P, F // P
    NB = NW // BATCH
    DEEP = 4
    VK = 2 * H * 3
    EPP = EP // P
    BPP = EPP // BLOCK
    NBLK = EP // BLOCK
    FLAT = TILES * P
    MASKS = 5
    EDGE = 2
    LOW_BITS = 8
    DIGITS, LOW_DIGITS = (32 - LOW_BITS) // 2, LOW_BITS // 2
    FREED = 6
    COLS = 6
    MAIN = (TILES - 1) * P
    LAST = -(-E * (N - (NW - 1) * P) // (N * P)) + 1
    CONSTS = 12 + DIGITS
    LOADS = 6
    IN_BANK = 512 // P
    assert BPP % MASKS == 0 and NW % (2 * BATCH) == 0 and (NB - 2) % DEEP == 0 and NB > DEEP and DC == 2 and TILES * VK <= 512
    PIECES = []
    at = 0
    for size in (1, 2, 2, 3, 3, 3, 3, 3, 3, 3):
        if at < TILES:
            PIECES.append((at, min(size, TILES - at)))
            at += size
    NP = len(PIECES)
    piece_of = {t: n for n, (a, m) in enumerate(PIECES) for t in range(a, a + m)}

    with ExitStack() as ctx:
        def sb(name, shape, dt=F32):
            return ctx.enter_context(nc.sbuf_tensor(name, shape, dt))

        def ps(name, shape):
            return ctx.enter_context(nc.psum_tensor(name, shape, F32))

        def sem(name):
            return ctx.enter_context(nc.semaphore(name))

        def sem2(name):
            return [sem(f"{name}{b}") for b in range(2)]

        table = nc.dram_tensor("node_rows", (NW * P, ROW), F32).ap()
        y_dram = nc.dram_tensor("ffn_rows", (NW * P, D), F32).ap()
        dst16_dram = nc.dram_tensor("dst16", (EP,), I16).ap()
        win_dram = nc.dram_tensor("window_table", (NW, COLS), I32).ap()

        ident = sb("ident", [P, P])
        ones = sb("ones", [P, P])
        below = sb("below", [P, P])
        iota_d = sb("iota_d", [P, P])
        node_id = sb("node_id", [P, NW])
        base_id = sb("base_id", [P, NW + 1])
        w1s = sb("w1s", [P, DC, F])
        w2s = sb("w2s", [P, FC, D])
        b1s = sb("b1s", [P, FC])
        gbs = sb("gbs", [P, D])
        b2_parts = sb("b2_parts", [P, D], BF16)
        ones_bf = sb("ones_bf", [P, P], BF16)
        wrs = sb("wrs", [P, D])
        brs = sb("brs", [P, 1])
        base = sb("base", [P, NW, D])
        parts_flat = sb("parts", [P, NW * VK], BF16)
        parts = parts_flat[:, :].rearrange("p (w v k) -> p w v k", w=NW, k=3)
        exself = sb("exself", [P, NW, H])
        wt = sb("wt", [P, NW])
        win = sb("win", [1, COLS * NW], I32)
        rows = sb("rows", [P, 2, TILES, ROW])
        srci = sb("srci", [P, 2, TILES], I32)
        dsti = sb("dsti", [P, 2, TILES], I32)
        dbc = sb("dbc", [P, 2, FLAT], I16)
        oht = dbc[:, :, :].bitcast(BF16)
        oh = sb("oh", [P, 2, TILES, P])
        dloc = sb("dloc", [P, TILES])
        edge_dm = sb("edge_dm", [P, TILES, 2 * H])
        zz = sb("zz", [P, TILES, H])
        zl = sb("zl", [P, TILES, H])
        zc = sb("zc", [P, TILES, H])
        diff = sb("diff", [P, TILES, H])
        selfr = sb("selfr", [P, 2, ROW])
        rden = sb("rden", [P, H])
        steps_of_rows = sb("steps_of_rows", [P, 4, D])
        zag, zmin, zexp, xn = (steps_of_rows[:, k, :] for k in range(4))
        junk = zexp
        xnT = sb("xnT", [P, DC, P])
        hT = sb("hT", [P, FC, P])
        yb = sb("yb", [P, 2, D])
        st6 = sb("st6", [P, 6])
        mv = sb("mv", [P, 2, 2])
        lnv = sb("lnv", [P, 2])
        rs0 = sb("rs0", [P, 2])
        rs1 = sb("rs1", [P, 1])
        rstd = sb("rstd", [P, 1])
        vareps = sb("vareps", [P, 2])
        sq = sb("sq", [P, 1])
        half = sb("half", [P, 1])
        wcol = sb("wcol", [P, 2])
        xsrc = sb("xsrc", [P, 1], I32)
        xdst = sb("xdst", [P, 1], I32)
        xdbc = sb("xdbc", [P, P], I16)
        xrow = sb("xrow", [P, ROW])
        xoh = sb("xoh", [P, P])
        xoht = sb("xoht", [P, P], BF16)
        xloc = sb("xloc", [P, 1])
        xdm = sb("xdm", [P, 2 * H])
        xzz = sb("xzz", [P, H])
        xzl = sb("xzl", [P, H])
        xzc = sb("xzc", [P, H])
        xdiff = sb("xdiff", [P, H])

        xmax = sb("xmax", [P, H])

        BD = BATCH * D
        WIDE = ROW + H
        rows_flat = rows[:, :, :, :].rearrange("p a t c -> p (a t c)")
        base_flat = base[:, :, :].rearrange("p w c -> p (w c)")
        oh_flat = oh[:, :, :, :].rearrange("p a t c -> p (a t c)")

        def batch(flat, at, width):
            return flat[:, at:at + BATCH * width].rearrange("p (g c) -> p g c", g=BATCH)

        nb = [batch(rows_flat, b * BD, D) for b in range(2)]
        scratch = 2 * BD
        falls = rows_flat[:, scratch:scratch + EPP].bitcast(I32)
        bias_f = [rows_flat[:, scratch + EPP + k * D:scratch + EPP + (k + 1) * D] for k in range(2)]
        bias_b = rows_flat[:, scratch + EPP + 2 * D:scratch + EPP + 2 * D + 3 * D // 2].bitcast(BF16).rearrange("p (k n) -> p k n", k=3)
        mask_at = scratch + EPP + 2 * D + 3 * D // 2
        earlier = rows_flat[:, mask_at:mask_at + BPP * (NW + 1) // 2].bitcast(BF16).rearrange("p (n w) -> p n w", n=BPP)
        xb = [batch(base_flat, q * BD, D) for q in range(DEEP)]
        po = [batch(base_flat, DEEP * BD + b * BATCH * WIDE, WIDE) for b in range(2)]
        dst_all = oh_flat[:, 0:EPP + 1].bitcast(I32)
        kept = EPP + 1
        block_first = oh_flat[:, kept:kept + BPP]
        kept += BPP
        asd, dm = (oh_flat[:, kept + k * NW * 2 * H:kept + (k + 1) * NW * 2 * H].rearrange("p (w v) -> p w v", w=NW) for k in range(2))
        kept += 4 * NW * H
        sz, sm = (oh_flat[:, kept + k * NW * H:kept + (k + 1) * NW * H].rearrange("p (w v) -> p w v", w=NW) for k in range(2))
        left = oh_flat[:, 0:2 * NW * H].rearrange("p (w v) -> p w v", w=NW)
        xpen = oh_flat[:, 2 * NW * H:2 * NW * H + P]
        xmask = oh_flat[:, 2 * NW * H + P:2 * NW * H + (1 + H) * P].rearrange("p (h e) -> p h e", h=H)
        assert kept + 2 * NW * H <= 2 * TILES * P and 2 * NW * H + (1 + H) * P <= EPP
        assert DEEP * BD + 2 * BATCH * WIDE <= NW * D and mask_at + BPP * (NW + 1) // 2 <= 2 * TILES * ROW
        SEARCH = 13 * NW
        dbc_flat = dbc[:, :, :].rearrange("p a e -> p (a e)").bitcast(F32)
        w1_flat = w1s[:, :, :].rearrange("p c n -> p (c n)")
        w2_flat = w2s[:, :, :].rearrange("p m n -> p (m n)")
        hT_flat = hT[:, :, :].rearrange("p m q -> p (m q)")
        selfr_flat = selfr[:, :, :].rearrange("p a c -> p (a c)")
        steps_flat = steps_of_rows[:, :, :].rearrange("p k c -> p (k c)")
        yin = []
        free_with = []
        for step, flat, at, tiles in (("sums", rows_flat, 0, (2, 5, 7, 7, 7, 6)), ("sums", oh_flat, SEARCH, (6, 6)), ("sums", dbc_flat, 0, (8,)),
                                      ("sums", parts_flat[:, :].bitcast(F32), 0, (4,)), ("sums", selfr_flat, 0, (2,)), ("rows", steps_flat, 0, (4,)),
                                      ("hidden", w1_flat, 0, (8,)), ("ffn", w2_flat, 0, (8,)), ("ffn", hT_flat, 0, (4,))):
            for count in tiles:
                free_with.append(step)
                yin.append(flat[:, at:at + count * D].rearrange("p (g c) -> p g c", g=count))
                at += count * D
        ROOMS = len(yin)
        chunks = []
        first = 0
        while first < NW - 2:
            r = len(chunks) % ROOMS
            chunks.append((first, min(yin[r].shape[1], NW - 2 - first), r))
            first += chunks[-1][1]
        assert sum(count for _, count, _ in chunks[:ROOMS]) <= NW - 4
        wext = hT[:, :, :].rearrange("p m q -> p (m q)")[:, 0:DC * WIDE].rearrange("p (c n) -> p c n", c=DC)
        key, sgn, khi, klo, tie, above, col, rank, coef, valid, *marks = (oh_flat[:, k * NW:(k + 1) * NW] for k in range(13))
        key, sgn = key.bitcast(I32), sgn.bitcast(I32)
        dst16 = dbc[:, 0, 0:EPP]
        xnT2 = dbc[:, 1, 0:4 * D].bitcast(F32).rearrange("p (a c q) -> p a c q", a=2, c=DC)
        att_b = [zag[:, :], zmin[:, :]]
        wext_mul = [zexp, xn, yb[:, 0, :], yb[:, 1, :]]
        broken = sb("broken", [P, 1])
        broken_all = sb("broken_all", [P, 1])
        st_b = sb("st_b", [P, BATCH, 6])
        mv_b = sb("mv_b", [P, 2, BATCH, 2])
        rs_b = sb("rs_b", [P, 2, BATCH])
        minus_half = sb("minus_half", [P, BATCH])
        gmax = sb("gmax", [P, 2 * H])
        gall = sb("gall", [P, 2 * H])
        spread = sb("spread", [P, H])
        widest = sb("widest", [P, 1])
        exact = sb("exact", [P, 1], I32)
        wv = sb("wv", [P, 4, 2])
        edge_block = sb("edge_block", [P, 2], I32)
        edge_dst = sb("edge_dst", [P, 2, BLOCK], I32)
        edge_less = sb("edge_less", [P, BLOCK])
        wi = sb("wi", [P, COLS], I32)
        count_f = sb("count_f", [P, 2])
        in_order = sb("in_order", [P, 1])
        first_f = sb("first_f", [P, 1])
        length = sb("length", [P, 1])
        fewer = half
        i1 = sb("i1", [P, 2], I32)
        i2 = sb("i2", [P, 2], I32)
        thr = sb("thr", [P, 4])
        after = sb("after", [P, 4])
        powers = sb("powers", [P, DIGITS])
        level = sb("level", [P, 1], I32)
        cnt = sb("cnt", [P, 3])
        got = sb("got", [P, 3])
        nge = sb("nge", [P, 1])
        cur = sb("cur", [P, 1])
        kth = sb("kth", [P, 1])

        lk_ps = ps("lk_ps", [P, 512])
        ag_ps = [ps(f"ag_ps{b}", [P, 512]) for b in range(2)]
        tr_ps = ps("tr_ps", [P, 512])
        h_ps = ps("h_ps", [P, 1024])
        y_ps = ps("y_ps", [P, 512])
        xl_ps = ps("xl_ps", [P, 512])
        tr2 = [t[:, 0:D].rearrange("p (c q) -> p c q", c=DC) for t in (tr_ps, xl_ps)]

        def sems(names):
            return [sem(n) for n in names.split()]

        dst_ld, att_ld, b2_ld, w_ld, d16_st, edge_ld, win_st, win_ld = sems(
            "dst_ld att_ld b2_ld w_ld d16_st edge_ld win_st win_ld")
        x_ld, tab_st = [sem(f"x_ld{q}") for q in range(DEEP)], sem2("tab_st")
        (pool_const, ones_bf_ok, d16_ok, blk_ok, falls_ok, fall_ok, broken_ok, earlier_ok, blocks_ok, block_ok, b2_ok, bias_step, wext_mul_ok, wext_ok, stat_ok, aggr_ok, vareps_b, rstd_b, norm_ok, trb_ok, trc_ok, xp_ok, xpc_ok, asd_ok,
         count_ok, before_ok, win_ok, gmax_ok, gall_ok, exact_ok, sdiff_ok, exself_ok, parts_ok,
         pre) = sems(
            "pool_const ones_bf_ok d16_ok blk_ok falls_ok fall_ok broken_ok earlier_ok blocks_ok block_ok b2_ok bias_step wext_mul_ok wext_ok stat_ok aggr_ok vareps_b rstd_b norm_ok trb_ok trc_ok xp_ok xpc_ok asd_ok "
            "count_ok before_ok win_ok gmax_ok gall_ok exact_ok sdiff_ok exself_ok parts_ok pre")
        ld_src, ld_dst, ld_dbc, ld_self, ld_x, gath, gath_last, y_st = (
            sem2(n) for n in ("ld_src", "ld_dst", "ld_dbc", "ld_self", "ld_x", "gath", "gath_last", "y_st"))
        (oht_ok, loc_ok, oh_ok, lk_ok, dm_ok, zs_ok, zm_ok, zl_ok, diff_ok, ex_ok, scaled, tile_done, agg_ok, selfx_ok,
         self_ok, rden_ok, zn_ok, zb_ok, zmin_ok, zexp_ok, xa_ok, x1_ok, st_ok, mv_ok, ln_ok, rs0_ok, ve_ok, sq_ok,
         half_ok, rstd_ok, xn_ok, base_ok, wcol_ok, wt_ok, tr_ok, xnT_ok, h_ok, hT_ok, y_ok, yb_ok) = sems(
            "oht_ok loc_ok oh_ok lk_ok dm_ok zs_ok zm_ok zl_ok diff_ok ex_ok scaled tile_done agg_ok selfx_ok "
            "self_ok rden_ok zn_ok zb_ok zmin_ok zexp_ok xa_ok x1_ok st_ok mv_ok ln_ok rs0_ok ve_ok sq_ok "
            "half_ok rstd_ok xn_ok base_ok wcol_ok wt_ok tr_ok xnT_ok h_ok hT_ok y_ok yb_ok")
        (x_src, x_dst, x_dbc, x_row, x_oht, x_loc, x_oh, x_lk, x_dm, x_zs, x_zm, x_zl, x_diff, x_ex, x_exc, x_sc,
         x_go, x_done) = sems(
            "x_src x_dst x_dbc x_row x_oht x_loc x_oh x_lk x_dm x_zs x_zm x_zl x_diff x_ex x_exc x_sc x_go x_done")
        m_src, m_dst, m_go, m_row, m_loc, m_oh, m_pen, m_mask, m_tr, m_max, m_done = sems(
            "m_src m_dst m_go m_row m_loc m_oh m_pen m_mask m_tr m_max m_done")
        step_ok, cnt_ok, tot_ok, level_ok, tie_ok, rank_ok, out_ok, out_st = sems(
            "step_ok cnt_ok tot_ok level_ok tie_ok rank_ok out_ok out_st")
        y_ld = [sem(f"y_ld{k}") for k in range(ROOMS)]

        def bc(v, n):
            return v.rearrange("(a n) -> a n", a=1).broadcast_to([P, n])

        def nodes(t, first, count):
            return t[bass.ds(first * P, count * P), :].rearrange("(g p) c -> p g c", p=P)

        def two_by_two(eng, turns, body, last_peeled=False):
            for b in range(2):
                body(b, 0, b)
            with eng.Fori(1, turns - last_peeled) as i:
                for b in range(2):
                    body(2 * i + b, i, b)
            if last_peeled:
                for b in range(2):
                    body(2 * (turns - 1) + b, turns - 1, b)

        def batches(eng, body, last_peeled=False):
            for b in range(2):
                body(b, 0, b, 0, b)
            turns = (NB - 2) // DEEP - last_peeled
            if turns:
                with eng.Fori(0, turns) as i:
                    for k in range(DEEP):
                        body(DEEP * i + 2 + k, 2 * i + 1 + k // 2, k % 2, i + (2 + k) // DEEP, (2 + k) % DEEP)
            if last_peeled:
                for g in range(NB - DEEP, NB):
                    body(g, g // 2, g % 2, g // DEEP, g % DEEP)

        def known(n, least):
            return not isinstance(n, int) or n >= least

        def tiles_of(w):
            return LAST if isinstance(w, int) and w == NW - 1 else TILES

        def wait_apart(eng, *waits):
            waits = [(semaphore, value if isinstance(value, int) else eng.to_reg(value)) for semaphore, value in waits]
            eng.wait_ge(pool_const, CONSTS)
            for semaphore, value in waits:
                eng.wait_ge(semaphore, value)

        def entry(eng, w, k, most):
            return eng.value_load(win[0:1, bass.ds(COLS * w + k, 1)], min_val=0, max_val=most)

        def for_extra(eng, w, body):
            n = entry(eng, w, 1, EP // P)
            before = entry(eng, w, 2, NW * EP // P)
            with eng.If(n > 0):
                with eng.Fori(0, n) as j:
                    body(j, before + j)

        def in_edges(at):
            return nc.s_assert_within(at, 0, EP - P, skip_runtime_bounds_check_because="a window's tiles begin before its last edge")

        def if_exact(eng, body):
            flag = eng.value_load(exact[0:1, 0:1], min_val=0, max_val=1)
            with eng.If(flag > 0):
                with eng.Fori(0, NW) as w:
                    n = entry(eng, w, 3, EP // P)
                    before = entry(eng, w, 4, NW * EP // P)
                    with eng.If(n > 0):
                        with eng.Fori(0, n) as j:
                            body(w, j, before + j)

        block = ctx.enter_context(nc.Block())

        @block.sync
        def _(sp):
            def load_x(g, q):
                sp.dma_start(xb[q], nodes(x, g * BATCH, BATCH)).then_inc(x_ld[q], 16)

            load_x(0, 0)
            sp.dma_start(wext[:, :, 0:D], W.rearrange("(c p) n -> p c n", p=P)).then_inc(att_ld, 16)
            sp.dma_start(att_b[0], bc(att_src.rearrange("h c -> (h c)"), D)).then_inc(att_ld, 16)
            sp.dma_start(att_b[1], bc(att_dst.rearrange("h c -> (h c)"), D)).then_inc(att_ld, 16)
            for q in range(1, DEEP):
                load_x(q, q)

            def store_rows(g, b, at=0, count=BATCH):
                wait_apart(sp, (xpc_ok, BATCH * g + at + count))
                sp.dma_start(nodes(table, g * BATCH + at, count), po[b][:, at:at + count, 0:ROW]).then_inc(tab_st[b], 16)

            def batch_io(g, t, b, r, q):
                if not isinstance(g, int) or g + DEEP < NB:
                    wait_apart(sp, (norm_ok, BATCH * (g + 1)))
                    load_x(g + DEEP, q)
                if known(g, 1):
                    store_rows(g - 1, 1 - b)
                if isinstance(g, int) and g == 1:
                    sp.wait_ge(d16_ok, 1)
                    sp.dma_start(dst16_dram.rearrange("(p e) -> p e", p=P), dst16).then_inc(d16_st, 16)

            batches(sp, batch_io, last_peeled=True)
            sp.wait_ge(win_ok, 1)
            sp.dma_start(win_dram, wi[0:NW, :]).then_inc(win_st, 16)
            store_rows(NB - 1, 1, 0, BATCH - EDGE)
            sp.wait_ge(win_st, 16)
            sp.dma_start(win[:, :], win_dram.rearrange("(a w) c -> a (w c)", a=1)).then_inc(win_ld, 16)
            store_rows(NB - 1, 1, BATCH - EDGE, EDGE)

            def load_flat(into, edges, first, w, b, loaded):
                before = tiles_of(w) - 1
                sp.dma_start(into[:, b, 0:before], edges[bass.ds(first, before * P)].rearrange("(p t) -> p t", t=before)).then_inc(loaded, 16)
                with nc.allow_non_contiguous_dma("an edge to a partition"):
                    sp.dma_start(into[:, b, before:before + 1], edges[bass.ds(first + before * P, P)].rearrange("(p t) -> p t", t=1)).then_inc(loaded, 16)

            def load_sources(w, b):
                first = entry(sp, w, 0, EP - FLAT)
                load_flat(srci, src, first, w, b, ld_src[b])

            sp.wait_ge(win_ld, 16)
            load_sources(0, 0)
            sp.wait_ge(d16_st, 16)
            for b in range(2):
                sp.wait_ge(tab_st[b], 16 * (NB // 2 + b))
            sp.wait_ge(exact_ok, 1)

            def exact_loads(w, j, k):
                first = in_edges(entry(sp, w, 0, EP - FLAT) + j * P)
                wait_apart(sp, (m_done, k + 1))
                with nc.allow_non_contiguous_dma("an edge to a partition"):
                    sp.dma_start(xsrc[:, :], src[bass.ds(first, P)].rearrange("(p t) -> p t", t=1)).then_inc(m_src, 16)
                    sp.dma_start(xdst[:, :], dst[bass.ds(first, P)].rearrange("(p t) -> p t", t=1)).then_inc(m_dst, 16)

            if_exact(sp, exact_loads)

            def window(w, i, b):
                if not isinstance(w, int) or w + 1 < NW:
                    if known(w, 1):
                        wait_apart(sp, (gath[1 - b], 16 * (TILES - 1) * (i + b)), (gath_last[1 - b], 16 * (i + b)))
                    load_sources(w + 1, 1 - b)
                first = entry(sp, w, 0, EP - FLAT)
                if known(w, 2):
                    wait_apart(sp, (oh_ok, w - 1), (lk_ok, w - 1))
                flat = tiles_of(w) * P
                sp.dma_start(dbc[:, b, 0:flat], dst16_dram[bass.ds(first, flat)].rearrange("(a e) -> a e", a=1).broadcast_to([P, flat])).then_inc(ld_dbc[b], 16)
                load_flat(dsti, dst, first, w, b, ld_dst[b])
                sp.dma_start(base[:, bass.ds(w, 1), :].rearrange("p w c -> p (w c)"), x[bass.ds(w * P, P), :]).then_inc(ld_x[b], 16)
                if known(w, 2):
                    wait_apart(sp, (agg_ok, w - 1))
                sp.dma_start(selfr[:, b, :], table[bass.ds(w * P, P), :]).then_inc(ld_self[b], 16)
                if known(w, 1):
                    extra_loads(w - 1)

            def extra_loads(w):
                if isinstance(w, int) and w == 0:
                    sp.wait_ge(parts_ok, 1)
                after = entry(sp, w, 0, EP - FLAT) + tiles_of(w) * P

                def load(j, k):
                    at = in_edges(after + j * P)
                    wait_apart(sp, (x_done, k + 1))
                    with nc.allow_non_contiguous_dma("an edge to a partition"):
                        sp.dma_start(xsrc[:, :], src[bass.ds(at, P)].rearrange("(p t) -> p t", t=1)).then_inc(x_src, 16)
                        sp.dma_start(xdst[:, :], dst[bass.ds(at, P)].rearrange("(p t) -> p t", t=1)).then_inc(x_dst, 16)
                    sp.dma_start(xdbc[:, :], dst16_dram[bass.ds(at, P)].rearrange("(a e) -> a e", a=1).broadcast_to([P, P])).then_inc(x_dbc, 16)

                for_extra(sp, w, load)

            two_by_two(sp, PAIRS, window, last_peeled=True)
            extra_loads(NW - 1)
            for c, (first, count, _) in enumerate(chunks + [(NW - 2, 2, None)]):
                sp.wait_ge(out_ok, c + 1)
                sp.dma_start(nodes(out, first, count), base[:, first:first + count, :]).then_inc(out_st, 16)
            sp.wait_ge(out_st, 16 * (len(chunks) + 1))

        @block.gpsimd
        def _(pool):
            nc.gpsimd.memset(ident[:, :], 0.0).then_inc(pool_const, 1)
            nc.gpsimd.memset(below[:, :], 1.0).then_inc(pool_const, 1)
            nc.gpsimd.memset(ones[:, :], 1.0).then_inc(pool_const, 1)
            nc.gpsimd.memset(minus_half[:, :], -0.5).then_inc(pool_const, 1)
            nc.gpsimd.memset(dst_all[:, EPP:EPP + 1], NW * P).then_inc(pool_const, 1)
            pool.wait_ge(pool_const, 5)
            nc.gpsimd.affine_select(out=ident[:, :], in_=ident[:, :], compare_op=ALU.not_equal, fill=1.0, base=0,
                                    pattern=[[-1, P]], channel_multiplier=1).then_inc(pool_const, 1)
            nc.gpsimd.affine_select(out=below[:, :], in_=below[:, :], compare_op=ALU.is_gt, fill=0.0, base=0,
                                    pattern=[[1, P]], channel_multiplier=-1).then_inc(pool_const, 1)

            def count(dst_ap, pattern, base_, by_partition):
                nc.gpsimd.iota(dst_ap, pattern=pattern, base=base_, channel_multiplier=by_partition,
                               allow_small_or_imprecise_dtypes=True).then_inc(pool_const, 1)

            for place in range(DIGITS):
                nc.gpsimd.memset(powers[:, place:place + 1], float(4 ** place)).then_inc(pool_const, 1)
            count(iota_d[:, :], [[1, P]], 0, 0)
            count(node_id[:, :], [[P, NW]], 0, 1)
            count(base_id[:, :], [[P, NW + 1]], 0, 0)
            count(wv[0:NW, 0, 0:1], [[0, 1]], 0, P)
            count(wv[0:NW, 0, 1:2], [[0, 1]], P, P)
            pool.wait_ge(pool_const, CONSTS)
            steps = [0]

            def then(ins):
                steps[0] += 1
                ins.then_inc(bias_step, 1)
                pool.wait_ge(bias_step, steps[0])

            def bias_parts(bias, parted, ready):
                rest = bias
                for k in range(3):
                    then(nc.gpsimd.tensor_copy(bias_b[:, k, :], rest))
                    if k < 2:
                        then(nc.gpsimd.tensor_tensor(bias_f[1], rest, bias_b[:, k, :], ALU.subtract))
                        rest = bias_f[1]
                for k in range(3):
                    then(nc.gpsimd.tensor_scalar(bias_b[:, k, :], bias_b[:, k, :], ident[:, k:k + 1], None, ALU.mult))
                then(nc.gpsimd.tensor_tensor(parted, bias_b[:, 0, :], bias_b[:, 1, :], ALU.add))
                nc.gpsimd.tensor_tensor(parted, parted, bias_b[:, 2, :], ALU.add).then_inc(ready, 1)

            def edge_order():
                pool.wait_ge(dst_ld, 32)
                by_block = dst_all[:, 0:EPP].rearrange("p (n e) -> p n e", e=BLOCK)
                nc.gpsimd.tensor_copy(block_first, by_block[:, :, 0]).then_inc(blk_ok, 1)
                nc.gpsimd.tensor_tensor(falls, dst_all[:, 0:EPP], dst_all[:, 1:EPP + 1], ALU.subtract).then_inc(falls_ok, 1)

            def rstd_batch(g, t, b, r, q):
                if isinstance(g, int) and g == NB - 1:
                    pool.wait_ge(block_ok, 1)
                    for k in range(2):
                        pool.indirect_dma_start(out=edge_dst[0:NW, k, :], out_offset=None, in_=dst.rearrange("(n e) -> n e", e=BLOCK),
                                                in_offset=bass.IndirectOffsetOnAxis(ap=edge_block[0:NW, k:k + 1], axis=0)).then_inc(edge_ld, 16)
                wait_apart(pool, (aggr_ok, g + 1), *([(norm_ok, BATCH * (g - 1))] if known(g, 2) else []))
                nc.gpsimd.tensor_scalar(rs_b[:, b, :], mv_b[:, b, :, 1], EPS, None, ALU.add).then_inc(vareps_b, 1)
                wait_apart(pool, (vareps_b, g + 1))
                nc.gpsimd.tensor_tensor(rs_b[:, b, :], rs_b[:, b, :], minus_half[:, :], ALU.pow).then_inc(rstd_b, 1)
                if isinstance(g, int) and g == 1:
                    edge_order()

            batches(pool, rstd_batch, last_peeled=True)
            pool.wait_ge(fall_ok, 1)
            nc.gpsimd.partition_all_reduce(broken_all[:, :], broken[:, :], P, bass.bass_isa.ReduceOp.max).then_inc(broken_ok, 1)
            pool.wait_ge(b2_ld, 16)
            bias_parts(bias_f[0], b2_parts[:, :], b2_ok)
            pool.wait_ge(gmax_ok, 2)
            nc.gpsimd.partition_all_reduce(gall[:, :], gmax[:, :], P, bass.bass_isa.ReduceOp.max).then_inc(gall_ok, 1)
            for b in range(2):
                pool.wait_ge(tab_st[b], 16 * (NB // 2 + b))
            pool.wait_ge(win_ld, 16)

            def gather_row(k, arrived, started):
                with pool.If(k > 0):
                    pool.inc_swdge_sem([arrived], [16], mode="sub").then_inc(started, 1)
                with pool.If(k < 1):
                    pool.sem_inc(started, 1)
                pool.indirect_dma_start(out=xrow[:, :], out_offset=None, in_=table,
                                        in_offset=bass.IndirectOffsetOnAxis(ap=xsrc[:, 0:1], axis=0)).then_inc(arrived, 16)

            def exact_gather(w, j, k):
                wait_apart(pool, (m_src, 16 * k + 16))
                gather_row(k, m_row, m_go)


            def window(w, i, b):
                pool.wait_ge(ld_src[b], 32 * (i + 1))

                def gather(t, arrived):
                    pool.indirect_dma_start(out=rows[:, b, t, :], out_offset=None, in_=table,
                                            in_offset=bass.IndirectOffsetOnAxis(ap=srci[:, b, t:t + 1], axis=0)).then_inc(arrived, 16)

                last = tiles_of(w) - 1
                for t in range(last):
                    if known(w, 2) and t % FREED == 0:
                        wait_apart(pool, (tile_done, (w - 2) * TILES + min(t + FREED, TILES)))
                    gather(t, gath[b])
                if known(w, 2):
                    some = entry(pool, w, 5, 1)
                    with pool.If(some > 0):
                        gather(last, gath_last[b])
                    with pool.If(some < 1):
                        pool.inc_swdge_sem([gath_last[b]], [16])
                else:
                    gather(last, gath_last[b])
                if isinstance(w, int) and w == 0:
                    pool.wait_ge(exact_ok, 1)
                    if_exact(pool, exact_gather)

                def extra_gather(j, k):
                    wait_apart(pool, (x_src, 16 * k + 16))
                    gather_row(k, x_row, x_go)

                for_extra(pool, w, extra_gather)

            two_by_two(pool, PAIRS, window, last_peeled=True)

        @block.scalar
        def _(act):
            act.wait_ge(pool_const, 5)
            nc.scalar.copy(ones_bf[:, :], ones[:, :]).then_inc(ones_bf_ok, 1)
            act.wait_ge(att_ld, 16 * 3)
            act.dma_start(dst_all[:, 0:EPP], dst.rearrange("(p e) -> p e", p=P)).then_inc(dst_ld, 16)
            act.wait_ge(pool_const, 5)
            with nc.allow_non_contiguous_dma("the target that follows each partition's last"):
                act.dma_start(dst_all[0:P - 1, EPP:EPP + 1], dst.rearrange("(p e) -> p e", p=P)[1:P, 0:1]).then_inc(dst_ld, 16)
            act.dma_start(bias_f[0], bc(b2, D)).then_inc(b2_ld, 16)
            act.dma_start(gbs[:, :], bc(gbias, D)).then_inc(w_ld, 16)
            act.dma_start(w1s[:, :, :], w1.rearrange("(c p) n -> p c n", p=P)).then_inc(w_ld, 16)
            act.dma_start(w2s[:, :, :], w2.rearrange("(c p) n -> p c n", p=P)).then_inc(w_ld, 16)
            with nc.allow_non_contiguous_dma("a bias by column of the hidden layer"):
                act.dma_start(b1s[:, :], b1.rearrange("(c p) -> p c", p=P)).then_inc(w_ld, 16)
            act.dma_start(wrs[:, :], bc(wr.rearrange("d o -> (d o)"), D)).then_inc(w_ld, 16)
            act.dma_start(brs[:, :], bc(br, 1)).then_inc(w_ld, 16)

            def row_copy(n, g, t, b, turn):
                act.wait_ge(xp_ok, n + 1)
                if t == 0 and known(g, 2):
                    act.wait_ge(tab_st[b], 16 * turn)
                    act.wait_ge(asd_ok, g - 1)
                nc.scalar.copy(po[b][:, t, :], ag_ps[(b + t) % 2][:, 0:WIDE]).then_inc(xpc_ok, 1)

            def batch_copies(g, turn, b, r, q):
                if isinstance(g, int) and g == 1:
                    act.wait_ge(dst_ld, 32)
                    nc.scalar.copy(dst16, dst_all[:, 0:EPP]).then_inc(d16_ok, 1)
                for t in range(BATCH):
                    n = BATCH * g + t
                    act.wait_ge(trb_ok, n + 1)
                    if known(n, 2):
                        act.wait_ge(xp_ok, n - 1)
                    nc.scalar.copy(xnT2[:, (b + t) % 2], tr2[(b + t) % 2]).then_inc(trc_ok, 1)
                    if t >= 1:
                        row_copy(n - 1, g, t - 1, b, turn)
                    elif known(g, 1):
                        row_copy(n - 1, g - 1, BATCH - 1, 1 - b, turn)

            batches(act, batch_copies)
            row_copy(NW - 1, NB - 1, BATCH - 1, 1, NB // 2 - 1)
            act.wait_ge(sdiff_ok, 1)
            nc.scalar.activation(exself[:, :, :], exself[:, :, :], ACT.Exp).then_inc(exself_ok, 1)
            act.wait_ge(win_ld, 16)
            act.wait_ge(w_ld, 16 * LOADS)

            def turn(w):
                act.wait_ge(tr_ok, w + 1)
                if known(w, 1):
                    act.wait_ge(h_ok, FC * w)
                nc.scalar.copy(xnT[:, :, :], tr2[0]).then_inc(xnT_ok, 1)

            def gelu(w):
                if known(w, 1):
                    act.wait_ge(y_ok, w)
                for m in range(FC):
                    if m % IN_BANK == 0:
                        act.wait_ge(h_ok, FC * w + m + IN_BANK)
                    nc.scalar.activation(hT[:, m, :], h_ps[:, m * P:(m + 1) * P], ACT.Gelu_apprx_tanh, bias=b1s[:, m:m + 1]).then_inc(hT_ok, 1)

            def store(w, i, b):
                act.wait_ge(y_ok, w + 1)
                if known(w, 2):
                    act.wait_ge(y_st[b], 16 * i)
                nc.scalar.copy(yb[:, b, :], y_ps[:, 0:D]).then_inc(yb_ok, 1)
                if isinstance(w, int) and w >= NW - 2:
                    return
                act.wait_ge(yb_ok, w + 1)
                act.dma_start(y_dram[bass.ds(w * P, P), :], yb[:, b, :]).then_inc(y_st[b], 16)

            def exponentials(w, b):
                act.wait_ge(diff_ok, w + 1)
                nc.scalar.activation(rows[:, b, 0:tiles_of(w), D:ROW], diff[:, 0:tiles_of(w), :], ACT.Exp).then_inc(ex_ok, 1)

            def window(w, i, b):
                last = isinstance(w, int) and w == NW - 1

                def extra_exp(j, k):
                    act.wait_ge(x_diff, k + 1)
                    nc.scalar.activation(xrow[:, D:ROW], xdiff[:, :], ACT.Exp).then_inc(x_ex, 1)

                if known(w, 2) and not last:
                    gelu(w - 2)
                for_extra(act, w, extra_exp)
                if known(w, 1):
                    after_sum(w - 1, 1 - b)
                    if last:
                        after_sum(w, b)
                    elif isinstance(w, int) and w == NW - 2:
                        exponentials(w + 1, 1 - b)
                    turn(w - 1)
                    if not isinstance(w, int) or w < NW - 2:
                        exponentials(w + 1, 1 - b)
                else:
                    exponentials(w + 1, 1 - b)
                if known(w, 2) and not last:
                    store(w - 2, i - 1, b)
                if last:
                    gelu(w - 2)
                    early_y()
                    store(w - 2, i - 1, b)

            def after_sum(w, b):
                act.wait_ge(zmin_ok, w + 1)
                nc.scalar.activation(zexp[:, :], zmin[:, :], ACT.Exp).then_inc(zexp_ok, 1)
                act.wait_ge(ve_ok, w + 1)
                nc.scalar.activation(lnv[:, b:b + 1], vareps[:, b:b + 1], ACT.Ln).then_inc(ln_ok, 1)
                act.wait_ge(ln_ok, w + 1)
                nc.scalar.activation(rs0[:, b:b + 1], lnv[:, b:b + 1], ACT.Exp, scale=-0.5).then_inc(rs0_ok, 1)

            def load_y(c):
                first, count, r = chunks[c]
                if c >= ROOMS:
                    act.wait_ge(out_ok, c - ROOMS + 1)
                act.dma_start(yin[r][:, 0:count, :], nodes(y_dram, first, count)).then_inc(y_ld[r], 16)

            def load_free(step):
                for r in range(ROOMS):
                    if free_with[r] == step:
                        load_y(r)

            def early_y():
                act.wait_ge(agg_ok, NW)
                act.wait_ge(y_st[0], 16 * (PAIRS - 2))
                act.wait_ge(y_st[1], 16 * (PAIRS - 2))
                load_free("sums")

            exponentials(0, 0)
            two_by_two(act, PAIRS, window, last_peeled=True)

            act.wait_ge(wt_ok, NW)
            act.wait_ge(base_ok, NW)
            act.wait_ge(tr_ok, NW)
            load_free("rows")
            turn(NW - 1)
            gelu(NW - 2)
            store(NW - 2, PAIRS - 1, 0)
            gelu(NW - 1)
            load_free("hidden")
            store(NW - 1, PAIRS - 1, 1)
            load_free("ffn")
            act.wait_ge(y_st[0], 16 * (PAIRS - 1))
            act.wait_ge(y_st[1], 16 * (PAIRS - 1))
            for c in range(ROOMS, len(chunks)):
                load_y(c)

        @block.tensor
        def _(pe):
            pe.sem_inc(x_done, 1)
            pe.sem_inc(m_done, 1)
            pe.wait_ge(pool_const, CONSTS)
            pe.wait_ge(ones_bf_ok, 1)

            def project(n, parity):
                if isinstance(n, int) and n == 0:
                    pe.wait_ge(wext_ok, 1)
                pe.wait_ge(trc_ok, n + 1)
                if known(n, 2):
                    pe.wait_ge(xpc_ok, n - 1)
                for c in range(DC):
                    last = nc.tensor.matmul(ag_ps[parity % 2][:, 0:WIDE], xnT2[:, parity % 2, c, :], wext[:, c, :],
                                            start=(c == 0), stop=(c == DC - 1))
                last.then_inc(xp_ok, 1)

            def batch_products(g, turn, b, r, q):
                for t in range(BATCH):
                    n = BATCH * g + t
                    if isinstance(g, int) and n == BATCH * (NB - DEEP + 1) + BATCH // 2:
                        pe.wait_ge(earlier_ok, MASKS)
                        for k in range(2):
                            for m in range(BPP):
                                last = nc.tensor.matmul(y_ps[0:NW, k:k + 1], earlier[:, m, k:k + NW], ones_bf[:, 0:1], start=(m == 0), stop=(m == BPP - 1))
                        last.then_inc(blocks_ok, 1)
                    pe.wait_ge(norm_ok, n + 1)
                    if isinstance(g, int) and n == BATCH * NB - EDGE - 1:
                        pe.wait_ge(count_ok, 1)
                        nc.tensor.matmul(y_ps[0:NW, 0:2], below[0:NW, 0:NW], count_f[0:NW, :], start=True, stop=True).then_inc(before_ok, 1)
                    if known(n, 2):
                        pe.wait_ge(trc_ok, n - 1)
                    for c in range(DC):
                        last = nc.tensor.transpose(tr2[(b + t) % 2][:, c, :], nb[b][:, t, c * P:(c + 1) * P], ident[:, :])
                    last.then_inc(trb_ok, 1)
                    if known(n, 1):
                        project(n - 1, b + t - 1)

            batches(pe, batch_products, last_peeled=True)
            project(NW - 1, 1 + BATCH - 1)
            pe.wait_ge(win_ld, 16)
            pe.wait_ge(exact_ok, 1)

            def exact_turn(w, j, k):
                pe.wait_ge(m_mask, k + 1)
                for h in range(H):
                    last = nc.tensor.transpose(xl_ps[:, h * P:(h + 1) * P], xmask[:, h, :], ident[:, :])
                last.then_inc(m_tr, 1)

            if_exact(pe, exact_turn)
            pe.wait_ge(parts_ok, 3)
            pe.wait_ge(b2_ok, 1)
            pe.wait_ge(w_ld, 16 * LOADS)

            def node_parts(w):
                return parts[:, bass.ds(w, 1), :, :].rearrange("p w v k -> p (w v k)")

            def look_up(w, b):
                pe.wait_ge(oht_ok, w + 1)
                if known(w, 1):
                    pe.wait_ge(dm_ok, w)
                before = tiles_of(w) - 1
                by_tile = oht[:, b, 0:before * P].rearrange("p (e t) -> p t e", t=before)
                for t in range(before + 1):
                    last = nc.tensor.matmul(lk_ps[:, VK * t:VK * (t + 1)], by_tile[:, t, :] if t < before else oht[:, b, before * P:(before + 1) * P], node_parts(w), start=True, stop=True)
                last.then_inc(lk_ok, 1)

            def turn(w):
                pe.wait_ge(xn_ok, w + 1)
                if known(w, 1):
                    pe.wait_ge(xnT_ok, w)
                for c in range(DC):
                    last = nc.tensor.transpose(tr2[0][:, c, :], xn[:, c * P:(c + 1) * P], ident[:, :])
                last.then_inc(tr_ok, 1)

            def hidden(w, ms=range(FC)):
                if 0 in ms:
                    pe.wait_ge(xnT_ok, w + 1)
                    if known(w, 1):
                        pe.wait_ge(hT_ok, FC * w)
                for m in ms:
                    for c in range(DC):
                        last = nc.tensor.matmul(h_ps[:, m * P:(m + 1) * P], w1s[:, c, m * P:(m + 1) * P], xnT[:, c, :],
                                                start=(c == 0), stop=(c == DC - 1))
                    last.then_inc(h_ok, 1)

            def ffn_out(w, ms=range(FC)):
                if 0 in ms and known(w, 1):
                    pe.wait_ge(yb_ok, w)
                for m in ms:
                    pe.wait_ge(hT_ok, FC * w + m + 1)
                    nc.tensor.matmul(y_ps[:, 0:D], hT[:, m, :], w2s[:, m, :], start=(m == 0), stop=False)
                if FC - 1 in ms:
                    nc.tensor.matmul(y_ps[:, 0:D], ones_bf[:, :], b2_parts[:, :], start=False, stop=True).then_inc(y_ok, 1)

            def window(w, i, b):
                pe.wait_ge(oh_ok, w + 1)
                if known(w, 2):
                    pe.wait_ge(zn_ok, w - 1)
                for t in range(tiles_of(w)):
                    pe.wait_ge(scaled, w * NP + piece_of[t] + 1)
                    nc.tensor.matmul(ag_ps[b][:, 0:ROW], oh[:, b, t, :], rows[:, b, t, :], start=(t == 0), stop=False).then_inc(tile_done, 1)

                def extra_products(j, k):
                    pe.wait_ge(x_oht, k + 1)
                    nc.tensor.matmul(xl_ps[:, 0:VK], xoht[:, :], node_parts(w), start=True, stop=True).then_inc(x_lk, 1)
                    pe.wait_ge(x_sc, k + 1)
                    nc.tensor.matmul(ag_ps[b][:, 0:ROW], xoh[:, :], xrow[:, :], start=False, stop=False).then_inc(x_done, 1)

                for_extra(pe, w, extra_products)
                pe.wait_ge(self_ok, w + 1)
                nc.tensor.matmul(ag_ps[b][:, 0:ROW], ident[:, :], selfr[:, b, :], start=False, stop=True).then_inc(agg_ok, 1)
                if not isinstance(w, int) or w + 1 < NW:
                    look_up(w + 1, 1 - b)
                if isinstance(w, int) and w == NW - 1:
                    hidden(w - 2)
                    turn(w - 1)
                    return
                if known(w, 2):
                    ffn_out(w - 2, range(FC // 2))
                if known(w, 1):
                    turn(w - 1)
                if known(w, 2):
                    ffn_out(w - 2, range(FC // 2, FC))
                if known(w, 1):
                    if not isinstance(w, int) or w < NW - 2:
                        hidden(w - 1)

            look_up(0, 0)
            two_by_two(pe, PAIRS, window, last_peeled=True)
            turn(NW - 1)
            between = {}
            for r, part, w in ((1, hidden, NW - 2), (4, ffn_out, NW - 2), (6, hidden, NW - 1), (8, ffn_out, NW - 1)):
                between[r], between[r + 1] = (part, w, 0), (part, w, 1)
            between[0] = (ffn_out, NW - 3, 1)
            ffn_out(NW - 3, range(FC // 2))

            def total(r):
                pe.wait_ge(cnt_ok, r + 1)
                nc.tensor.matmul(lk_ps[:, 0:3], ones[:, :], cnt[:, :], start=True, stop=True).then_inc(tot_ok, 1)

            for r in range(DIGITS + 1):
                total(r)
                if r in between:
                    part, w, k = between[r]
                    part(w, range(k * FC // 2, (k + 1) * FC // 2))
            pe.wait_ge(level_ok, 1)
            undecided = pe.value_load(level[0:1, 0:1], min_val=0, max_val=1)
            with pe.If(undecided > 0):
                for r in range(DIGITS + 1, DIGITS + 1 + LOW_DIGITS + 1):
                    total(r)
                pe.wait_ge(tie_ok, 1)
                nc.tensor.matmul(lk_ps[:, 0:NW], below[:, :], tie, start=True, stop=True)
                nc.tensor.matmul(xl_ps[:, 0:NW], ones[:, :], tie, start=True, stop=True).then_inc(rank_ok, 1)

        @block.vector
        def _(dve):
            taken = [0]

            def then(ins):
                taken[0] += 1
                ins.then_inc(pre, 1)
                dve.wait_ge(pre, taken[0])

            def attention_columns():
                dve.wait_ge(att_ld, 16 * 3)
                for n in range(2 * DC):
                    last = nc.vector.tensor_tensor(wext_mul[n][:, :], wext[:, n % DC, 0:D], att_b[n // DC], ALU.mult)
                last.then_inc(wext_mul_ok, 1)
                dve.wait_ge(wext_mul_ok, 1)
                for n in range(2 * DC):
                    k = ROW - H + n // DC * H
                    last = nc.vector.tensor_reduce(wext[:, n % DC, k:k + H], wext_mul[n][:, :].rearrange("p (h c) -> p h c", h=H), AXX, ALU.add)
                last.then_inc(wext_ok, 1)

            def norm(g, b, q):
                dve.wait_ge(rstd_b, g + 1)
                if known(g, 2):
                    dve.wait_ge(trb_ok, BATCH * (g - 1))
                for t in range(BATCH):
                    nc.vector.tensor_scalar(nb[b][:, t, :], xb[q][:, t, :], mv_b[:, b, t, 0:1], rs_b[:, b, t:t + 1], ALU.subtract, ALU.mult).then_inc(norm_ok, 1)

            def keep_asd(g, b):
                dve.wait_ge(xpc_ok, BATCH * (g + 1))
                nc.vector.tensor_copy(asd[:, bass.ds(g * BATCH, BATCH), :], po[b][:, :, D:WIDE]).then_inc(asd_ok, 1)

            def batch_stats(g, turn, b, r, q):
                wait_apart(dve, (x_ld[q], 16 * (r + 1)), *([(aggr_ok, g)] if known(g, 1) else []))
                for t in range(BATCH):
                    last = nc.vector.bn_stats(st_b[:, t, :], xb[q][:, t, :])
                last.then_inc(stat_ok, 1)
                wait_apart(dve, (stat_ok, g + 1))
                for t in range(BATCH):
                    last = nc.vector.bn_aggr(mv_b[:, b, t, :], st_b[:, t, :])
                last.then_inc(aggr_ok, 1)
                if isinstance(g, int) and g == 0:
                    attention_columns()
                    norm(0, 0, 0)
                if known(g, 2):
                    norm(g - 1, 1 - b, (q - 1) % DEEP)
                    keep_asd(g - 2, b)
                if isinstance(g, int):
                    for m in {NB - DEEP: [0, 1, 2], NB - DEEP + 1: [3, 4]}.get(g, []):
                        mask(m)
                    if g == NB - DEEP + 2:
                        window_blocks()
                        dve.wait_ge(falls_ok, 1)
                        nc.vector.tensor_reduce(broken[:, :], falls, AXX, ALU.max).then_inc(fall_ok, 1)

            def mask(m):
                if m == 0:
                    dve.wait_ge(pool_const, CONSTS)
                    dve.wait_ge(blk_ok, 1)
                n = BPP // MASKS
                nc.vector.tensor_tensor(earlier[:, m * n:(m + 1) * n, :], block_first[:, m * n:(m + 1) * n].unsqueeze(2).broadcast_to([P, n, NW + 1]),
                                        base_id[:, :].unsqueeze(1).broadcast_to([P, n, NW + 1]), ALU.is_lt).then_inc(earlier_ok, 1)

            def window_blocks():
                then(nc.vector.tensor_scalar(fewer[:, :], node_id[:, 0:1], float(NW - 1), float((TILES - LAST) * P), ALU.is_ge, ALU.mult))
                dve.wait_ge(blocks_ok, 1)
                then(nc.vector.tensor_scalar(wv[0:NW, 1, :], y_ps[0:NW, 0:2], -1.0, 0.0, ALU.add, ALU.max))
                nc.vector.tensor_copy(edge_block[0:NW, :], wv[0:NW, 1, :]).then_inc(block_ok, 1)

            def window_edges():
                dve.wait_ge(edge_ld, 32)
                for k in range(2):
                    then(nc.vector.tensor_scalar(edge_less[0:NW, :], edge_dst[0:NW, k, :], wv[0:NW, 0, k:k + 1], 0.0, ALU.is_lt, ALU.add, accum_out=wv[0:NW, 2, k:k + 1]))
                then(nc.vector.scalar_tensor_tensor(out=wv[0:NW, 3, :], in0=wv[0:NW, 1, :], scalar=float(BLOCK), in1=wv[0:NW, 2, :], op0=ALU.mult, op1=ALU.add))
                dve.wait_ge(broken_ok, 1)
                then(nc.vector.tensor_scalar(in_order[:, :], broken_all[:, :], 0.0, None, ALU.is_le))
                then(nc.vector.tensor_scalar(broken_all[:, :], broken_all[:, :], 0.0, float(EP), ALU.is_gt, ALU.mult))
                then(nc.vector.tensor_scalar(first_f[0:NW, :], wv[0:NW, 3, 0:1], float(EP - FLAT), in_order[0:NW, 0:1], ALU.min, ALU.mult))
                then(nc.vector.tensor_tensor(length[0:NW, :], wv[0:NW, 3, 1:2], broken_all[0:NW, :], ALU.max))
                then(nc.vector.tensor_tensor(length[0:NW, :], length[0:NW, :], first_f[0:NW, :], ALU.subtract))
                nc.vector.tensor_copy(wi[0:NW, 0:1], first_f[0:NW, :])
                nc.vector.tensor_scalar(i1[0:NW, 1:2], length[0:NW, :], float(P - 1), None, ALU.add)
                then(nc.vector.tensor_tensor(length[0:NW, :], length[0:NW, :], fewer[0:NW, :], ALU.add))
                nc.vector.tensor_scalar(wi[0:NW, 5:6], length[0:NW, :], float(MAIN), None, ALU.is_gt)
                then(nc.vector.tensor_scalar(i1[0:NW, 0:1], length[0:NW, :], float(P - 1 - FLAT), None, ALU.add))
                then(nc.vector.tensor_scalar(i2[0:NW, :], i1[0:NW, :], P.bit_length() - 1, None, ALU.arith_shift_right))
                then(nc.vector.tensor_scalar(count_f[0:NW, :], i2[0:NW, :], 0.0, None, ALU.max))
                nc.vector.tensor_copy(wi[0:NW, 1:2], count_f[0:NW, 0:1])
                nc.vector.tensor_copy(wi[0:NW, 3:4], count_f[0:NW, 1:2]).then_inc(count_ok, 1)

            batches(dve, batch_stats, last_peeled=True)
            norm(NB - 1, 1, (NB - 1) % DEEP)
            window_edges()
            keep_asd(NB - 2, 0)
            dve.wait_ge(before_ok, 1)
            nc.vector.tensor_copy(wi[0:NW, 2:3], y_ps[0:NW, 0:1])
            nc.vector.tensor_copy(wi[0:NW, 4:5], y_ps[0:NW, 1:2]).then_inc(win_ok, 1)
            keep_asd(NB - 1, 1)
            dve.wait_ge(asd_ok, NB)
            by_head = asd[:, :, 0:H].rearrange("p w h -> p h w")
            nc.vector.tensor_reduce(gmax[:, 0:H], by_head, AXX, ALU.max).then_inc(gmax_ok, 1)
            then(nc.vector.tensor_reduce(spread[:, :], by_head, AXX, ALU.min))
            nc.vector.tensor_scalar(gmax[:, H:2 * H], spread[:, :], -1.0, None, ALU.mult).then_inc(gmax_ok, 1)
            dve.wait_ge(gall_ok, 1)
            then(nc.vector.tensor_tensor(spread[:, :], gall[:, 0:H], gall[:, H:2 * H], ALU.add))
            then(nc.vector.tensor_reduce(widest[:, :], spread[:, :], AXX, ALU.max))
            then(nc.vector.tensor_copy(dm[:, :, 0:H], asd[:, :, H:2 * H]))
            then(nc.vector.tensor_copy(dm[:, :, H:2 * H], gall[:, 0:H].unsqueeze(1).broadcast_to([P, NW, H])))
            nc.vector.tensor_scalar(exact[:, :], widest[:, :], SPREAD, None, ALU.is_gt).then_inc(exact_ok, 1)
            dve.wait_ge(exact_ok, 1)
            dve.wait_ge(win_ld, 16)
            flag = dve.value_load(exact[0:1, 0:1], min_val=0, max_val=1)
            with dve.If(flag > 0):
                nc.vector.tensor_copy(dm[:, :, H:2 * H], asd[:, :, 0:H]).then_inc(m_max, 1)
                dve.wait_ge(m_max, 1)

            def exact_max(w, j, k):
                dve.wait_ge(m_dst, 16 * k + 16)
                nc.vector.tensor_scalar(xloc[:, :], xdst[:, :], base_id[:, bass.ds(w, 1)], None, ALU.subtract).then_inc(m_loc, 1)
                dve.wait_ge(m_go, k + 1)
                dve.wait_ge(m_loc, k + 1)
                nc.vector.tensor_scalar(xoh[:, :], iota_d[:, :], xloc[:, 0:1], None, ALU.is_equal).then_inc(m_oh, 1)
                dve.wait_ge(m_oh, k + 1)
                nc.vector.tensor_scalar(xpen, xoh[:, :], 1.0, 1e38, ALU.subtract, ALU.mult).then_inc(m_pen, 1)
                dve.wait_ge(m_pen, k + 1)
                dve.wait_ge(m_row, 16)
                nc.vector.tensor_tensor(xmask[:, :, :], xpen.unsqueeze(1).broadcast_to([P, H, P]),
                                        xrow[:, D:ROW].unsqueeze(2).broadcast_to([P, H, P]), ALU.add).then_inc(m_mask, 1)
                dve.wait_ge(m_tr, k + 1)
                nc.vector.tensor_reduce(xmax[:, :], xl_ps[:, :].rearrange("p (h e) -> p h e", h=H), AXX, ALU.max).then_inc(m_max, 1)
                dve.wait_ge(m_max, k + 2)
                mx = dm[:, bass.ds(w, 1), H:2 * H].rearrange("p w h -> p (w h)")
                nc.vector.tensor_tensor(mx, mx, xmax[:, :], ALU.max).then_inc(m_done, 1)
                dve.wait_ge(m_done, k + 2)

            if_exact(dve, exact_max)
            def flat(a):
                return a.rearrange("p w h -> p (w h)")

            then(nc.vector.tensor_tensor(sz[:, :, :], asd[:, :, 0:H], dm[:, :, 0:H], ALU.add))
            then(nc.vector.tensor_tensor(sm[:, :, :], dm[:, :, H:2 * H], dm[:, :, 0:H], ALU.add))
            then(nc.vector.scalar_tensor_tensor(out=flat(sz[:, :, :]), in0=flat(sz[:, :, :]), scalar=SLOPE, in1=flat(sz[:, :, :]), op0=ALU.mult, op1=ALU.max))
            then(nc.vector.scalar_tensor_tensor(out=flat(sm[:, :, :]), in0=flat(sm[:, :, :]), scalar=SLOPE, in1=flat(sm[:, :, :]), op0=ALU.mult, op1=ALU.max))
            nc.vector.tensor_tensor(exself[:, :, :], sz[:, :, :], sm[:, :, :], ALU.subtract).then_inc(sdiff_ok, 1)
            then(nc.vector.tensor_copy(dm[:, :, H:2 * H], sm[:, :, :]))
            nc.vector.tensor_copy(parts[:, :, :, 0], dm[:, :, :]).then_inc(parts_ok, 1)
            dve.wait_ge(parts_ok, 1)
            then(nc.vector.tensor_tensor(left[:, :, :], dm[:, :, :], parts[:, :, :, 0], ALU.subtract))
            nc.vector.tensor_copy(parts[:, :, :, 1], left[:, :, :]).then_inc(parts_ok, 1)
            dve.wait_ge(parts_ok, 2)
            then(nc.vector.tensor_tensor(left[:, :, :], left[:, :, :], parts[:, :, :, 1], ALU.subtract))
            nc.vector.tensor_copy(parts[:, :, :, 2], left[:, :, :]).then_inc(parts_ok, 1)
            dve.wait_ge(exself_ok, 1)
            dve.wait_ge(w_ld, 16 * LOADS)
            dve.wait_ge(parts_ok, 3)

            def one_hots_turned(w, i, b):
                n = tiles_of(w)
                flat = n * P
                dve.wait_ge(ld_dbc[b], 16 * (i + 1))
                nc.vector.tensor_scalar(oht[:, b, 0:flat], dbc[:, b, 0:flat], node_id[:, bass.ds(w, 1)], None, ALU.is_equal).then_inc(oht_ok, 1)
                dve.wait_ge(ld_dst[b], 32 * (i + 1))
                nc.vector.tensor_scalar(dloc[:, 0:n], dsti[:, b, 0:n], base_id[:, bass.ds(w, 1)], None, ALU.subtract).then_inc(loc_ok, 1)

            def one_hots(w, b):
                dve.wait_ge(loc_ok, w + 1)
                n = tiles_of(w)
                nc.vector.tensor_tensor(oh[:, b, 0:n, :], iota_d[:, :].unsqueeze(1).broadcast_to([P, n, P]),
                                        dloc[:, 0:n].unsqueeze(2).broadcast_to([P, n, P]), ALU.is_equal).then_inc(oh_ok, 1)

            def exponents(w, i, b):
                dve.wait_ge(lk_ok, w + 1)
                n = tiles_of(w)

                def flat(a):
                    return a[:, 0:n, :].rearrange("p t h -> p (t h)")

                nc.vector.tensor_reduce(flat(edge_dm), lk_ps[:, 0:n * VK].rearrange("p (v k) -> p v k", k=3), AXX, ALU.add).then_inc(dm_ok, 1)
                dve.wait_ge(dm_ok, w + 1)
                dve.wait_ge(gath[b], 16 * ((TILES - 1) * i + n - 1))
                dve.wait_ge(gath_last[b], 16 * (i + 1))
                nc.vector.tensor_tensor(zz[:, 0:n, :], rows[:, b, 0:n, D:ROW], edge_dm[:, 0:n, 0:H], ALU.add).then_inc(zs_ok, 1)
                dve.wait_ge(zs_ok, w + 1)
                nc.vector.scalar_tensor_tensor(out=flat(zl), in0=flat(zz), scalar=SLOPE, in1=flat(zz), op0=ALU.mult, op1=ALU.max).then_inc(zl_ok, 1)
                dve.wait_ge(zl_ok, w + 1)
                nc.vector.tensor_tensor(zc[:, 0:n, :], zl[:, 0:n, :], edge_dm[:, 0:n, H:2 * H], ALU.min).then_inc(zm_ok, 1)
                dve.wait_ge(zm_ok, w + 1)
                nc.vector.tensor_tensor(diff[:, 0:n, :], zc[:, 0:n, :], edge_dm[:, 0:n, H:2 * H], ALU.subtract).then_inc(diff_ok, 1)

            def weigh(w, i, b):
                dve.wait_ge(ex_ok, w + 1)
                for a, most in PIECES:
                    m = min(most, tiles_of(w) - a)
                    if m <= 0:
                        break
                    v = rows[:, b, a:a + m, 0:D].rearrange("p t (h c) -> p t h c", h=H)
                    e = rows[:, b, a:a + m, D:ROW].unsqueeze(3).broadcast_to([P, m, H, C])
                    nc.vector.tensor_tensor(v, v, e, ALU.mult).then_inc(scaled, 1)

            def weigh_self(w, i, b):
                dve.wait_ge(ld_self[b], 16 * (i + 1))
                e = exself[:, bass.ds(w, 1), :].rearrange("p w h -> p (w h)")
                v = selfr[:, b, 0:D].rearrange("p (h c) -> p h c", h=H)
                nc.vector.tensor_tensor(v, v, e.unsqueeze(2).broadcast_to([P, H, C]), ALU.mult).then_inc(selfx_ok, 1)
                nc.vector.tensor_copy(selfr[:, b, D:ROW], e).then_inc(self_ok, 1)

            def extra_tile(w, k):
                dve.wait_ge(x_dbc, 16 * k + 16)
                nc.vector.tensor_scalar(xoht[:, :], xdbc[:, :], node_id[:, bass.ds(w, 1)], None, ALU.is_equal).then_inc(x_oht, 1)
                dve.wait_ge(x_dst, 16 * k + 16)
                nc.vector.tensor_scalar(xloc[:, :], xdst[:, :], base_id[:, bass.ds(w, 1)], None, ALU.subtract).then_inc(x_loc, 1)
                dve.wait_ge(x_loc, k + 1)
                nc.vector.tensor_scalar(xoh[:, :], iota_d[:, :], xloc[:, 0:1], None, ALU.is_equal).then_inc(x_oh, 1)
                dve.wait_ge(x_go, k + 1)
                dve.wait_ge(x_lk, k + 1)
                nc.vector.tensor_reduce(xdm[:, :], xl_ps[:, 0:VK].rearrange("p (v k) -> p v k", k=3), AXX, ALU.add).then_inc(x_dm, 1)
                dve.wait_ge(x_dm, k + 1)
                dve.wait_ge(x_row, 16)
                nc.vector.tensor_tensor(xzz[:, :], xrow[:, D:ROW], xdm[:, 0:H], ALU.add).then_inc(x_zs, 1)
                dve.wait_ge(x_zs, k + 1)
                nc.vector.scalar_tensor_tensor(out=xzl[:, :], in0=xzz[:, :], scalar=SLOPE, in1=xzz[:, :], op0=ALU.mult, op1=ALU.max).then_inc(x_zl, 1)
                dve.wait_ge(x_zl, k + 1)
                nc.vector.tensor_tensor(xzc[:, :], xzl[:, :], xdm[:, H:2 * H], ALU.min).then_inc(x_zm, 1)
                dve.wait_ge(x_zm, k + 1)
                nc.vector.tensor_tensor(xdiff[:, :], xzc[:, :], xdm[:, H:2 * H], ALU.subtract).then_inc(x_diff, 1)
                dve.wait_ge(x_ex, k + 1)
                dve.wait_ge(x_oh, k + 1)
                v = xrow[:, 0:D].rearrange("p (h c) -> p h c", h=H)
                nc.vector.tensor_tensor(v, v, xrow[:, D:ROW].unsqueeze(2).broadcast_to([P, H, C]), ALU.mult).then_inc(x_sc, 1)

            def residual(w, i, b):
                dve.wait_ge(agg_ok, w + 1)
                nc.vector.reciprocal(rden[:, :], ag_ps[b][:, D:ROW]).then_inc(rden_ok, 1)
                dve.wait_ge(rden_ok, w + 1)
                nc.vector.tensor_tensor(zag[:, :].rearrange("p (h c) -> p h c", h=H), ag_ps[b][:, 0:D].rearrange("p (h c) -> p h c", h=H),
                                        rden[:, :].unsqueeze(2).broadcast_to([P, H, C]), ALU.mult).then_inc(zn_ok, 1)
                dve.wait_ge(zn_ok, w + 1)
                nc.vector.tensor_tensor(zag[:, :], zag[:, :], gbs[:, :], ALU.add).then_inc(zb_ok, 1)
                dve.wait_ge(zb_ok, w + 1)
                nc.vector.tensor_scalar(zmin[:, :], zag[:, :], 0.0, None, ALU.min).then_inc(zmin_ok, 1)
                dve.wait_ge(ld_x[b], 16 * (i + 1))
                x1 = base[:, bass.ds(w, 1), :].rearrange("p w c -> p (w c)")
                nc.vector.scalar_tensor_tensor(out=zag[:, :], in0=zag[:, :], scalar=0.0, in1=x1, op0=ALU.max, op1=ALU.add).then_inc(xa_ok, 1)
                dve.wait_ge(xa_ok, w + 1)
                dve.wait_ge(zexp_ok, w + 1)
                nc.vector.scalar_tensor_tensor(out=x1, in0=zexp[:, :], scalar=-1.0, in1=zag[:, :], op0=ALU.add, op1=ALU.add).then_inc(x1_ok, 1)
                wait_apart(dve, (x1_ok, w + 1))
                nc.vector.bn_stats(st6[:, :], x1).then_inc(st_ok, 1)
                wait_apart(dve, (st_ok, w + 1))
                nc.vector.bn_aggr(mv[:, b, :], st6[:, :]).then_inc(mv_ok, 1)
                dve.wait_ge(mv_ok, w + 1)
                nc.vector.tensor_scalar(vareps[:, b:b + 1], mv[:, b, 1:2], EPS, None, ALU.add).then_inc(ve_ok, 1)

            def route(w, b):
                dve.wait_ge(rs0_ok, w + 1)
                nc.vector.scalar_tensor_tensor(out=sq[:, :], in0=rs0[:, b:b + 1], scalar=rs0[:, b:b + 1], in1=vareps[:, b:b + 1], op0=ALU.mult, op1=ALU.mult).then_inc(sq_ok, 1)
                dve.wait_ge(sq_ok, w + 1)
                nc.vector.tensor_scalar(half[:, :], sq[:, :], -0.5, 1.5, ALU.mult, ALU.add).then_inc(half_ok, 1)
                dve.wait_ge(half_ok, w + 1)
                nc.vector.tensor_tensor(rstd[:, :], rs0[:, b:b + 1], half[:, :], ALU.mult).then_inc(rstd_ok, 1)
                dve.wait_ge(rstd_ok, w + 1)
                if known(w, 1):
                    dve.wait_ge(tr_ok, w)
                x1 = base[:, bass.ds(w, 1), :].rearrange("p w c -> p (w c)")
                nc.vector.tensor_scalar(xn[:, :], x1, mv[:, b, 0:1], rstd[:, 0:1], ALU.subtract, ALU.mult).then_inc(xn_ok, 1)
                dve.wait_ge(xn_ok, w + 1)
                nc.vector.tensor_tensor(x1, x1, xn[:, :], ALU.add).then_inc(base_ok, 1)
                nc.vector.tensor_tensor_reduce(junk[:, :], xn[:, :], wrs[:, :], 1.0, 0.0, ALU.mult, ALU.add, wcol[:, b:b + 1]).then_inc(wcol_ok, 1)
                dve.wait_ge(wcol_ok, w + 1)
                nc.vector.tensor_copy(wt[:, bass.ds(w, 1)], wcol[:, b:b + 1]).then_inc(wt_ok, 1)

            def window(w, i, b):
                more = not isinstance(w, int) or w + 1 < NW
                if not isinstance(w, int) or w < NW - 1:
                    exponents(w, i, b)
                weigh(w, i, b)
                weigh_self(w, i, b)
                if more:
                    one_hots_turned(w + 1, i + b, 1 - b)
                for_extra(dve, w, lambda j, k: extra_tile(w, k))
                if known(w, 1):
                    residual(w - 1, i - 1 + b, 1 - b)
                if more:
                    one_hots(w + 1, 1 - b)
                if isinstance(w, int) and w == NW - 2:
                    exponents(NW - 1, PAIRS - 1, 1)
                if not more:
                    residual(w, i, b)
                if known(w, 1):
                    route(w - 1, 1 - b)

            one_hots_turned(0, 0, 0)
            one_hots(0, 0)
            two_by_two(dve, PAIRS, window, last_peeled=True)
            then(nc.vector.tensor_scalar(valid, node_id[:, :], float(N), None, ALU.is_lt))
            then(nc.vector.memset(kth[:, :], float(K)))
            then(nc.vector.memset(cnt[:, :], 0.0))
            route(NW - 1, 1)
            dve.wait_ge(wt_ok, NW)
            dve.wait_ge(base_ok, NW)
            then(nc.vector.tensor_scalar(wt[:, :], wt[:, :], brs[:, 0:1], None, ALU.add))
            bits = wt[:, :].bitcast(I32)
            then(nc.vector.tensor_scalar(sgn, bits, 31, None, ALU.arith_shift_right))
            then(nc.vector.tensor_scalar(sgn, sgn, -2 ** 31, None, ALU.bitwise_or))
            then(nc.vector.tensor_tensor(key, bits, sgn, ALU.bitwise_xor))
            then(nc.vector.tensor_scalar(sgn, key, LOW_BITS, 2 ** (32 - LOW_BITS) - 1, ALU.logical_shift_right, ALU.bitwise_and))
            then(nc.vector.tensor_copy(khi, sgn))
            then(nc.vector.scalar_tensor_tensor(out=khi, in0=khi, scalar=1.0, in1=valid, op0=ALU.add, op1=ALU.mult))
            then(nc.vector.tensor_scalar(khi, khi, -1.0, None, ALU.add))
            rounds = [0]

            def totals():
                rounds[0] += 1
                dve.wait_ge(tot_ok, rounds[0])

            def search(keys, digits):
                then(nc.vector.tensor_scalar(thr[:, :], iota_d[:, 0:4], float(4 ** (digits - 1)), None, ALU.mult))
                for place in range(digits - 1, -1, -1):
                    for j in range(3):
                        last = nc.vector.tensor_scalar(marks[j], keys, thr[:, j + 1:j + 2], 0.0, ALU.is_ge, ALU.add, accum_out=cnt[:, j:j + 1])
                    last.then_inc(cnt_ok, 1)
                    then(nc.vector.tensor_scalar(after[:, :], iota_d[:, 0:4], 4.0 ** (place - 1) if place else 0.0, thr[:, 0:1], ALU.mult, ALU.add))
                    totals()
                    then(nc.vector.tensor_scalar(got[:, :], lk_ps[:, 0:3], kth[:, 0:1], 0.0, ALU.is_ge, ALU.add, accum_out=nge[:, :]))
                    then(nc.vector.scalar_tensor_tensor(out=thr[:, :], in0=powers[:, place:place + 1].broadcast_to([P, 4]), scalar=nge[:, 0:1], in1=after[:, :], op0=ALU.mult, op1=ALU.add))
                then(nc.vector.tensor_copy(cur[:, :], thr[:, 0:1]))

            def take_above(keys):
                nc.vector.tensor_scalar(above, keys, cur[:, 0:1], 0.0, ALU.is_gt, ALU.add, accum_out=cnt[:, 0:1])
                nc.vector.tensor_scalar(tie, keys, cur[:, 0:1], 0.0, ALU.is_ge, ALU.add, accum_out=cnt[:, 1:2]).then_inc(cnt_ok, 1)
                totals()

            search(khi, DIGITS)
            take_above(khi)
            nc.vector.tensor_scalar(level[:, :], lk_ps[:, 1:2], float(K), None, ALU.is_gt).then_inc(level_ok, 1)
            then(nc.vector.tensor_tensor(coef, tie, wt[:, :], ALU.mult))
            dve.wait_ge(level_ok, 1)
            undecided = dve.value_load(level[0:1, 0:1], min_val=0, max_val=1)
            with dve.If(undecided > 0):
                then(nc.vector.tensor_tensor(kth[:, :], kth[:, :], lk_ps[:, 0:1], ALU.subtract))
                then(nc.vector.tensor_tensor(coef, above, wt[:, :], ALU.mult))
                then(nc.vector.tensor_tensor(tie, tie, above, ALU.subtract))
                then(nc.vector.tensor_scalar(sgn, key, 2 ** LOW_BITS - 1, None, ALU.bitwise_and))
                then(nc.vector.tensor_copy(klo, sgn))
                then(nc.vector.scalar_tensor_tensor(out=klo, in0=klo, scalar=1.0, in1=tie, op0=ALU.add, op1=ALU.mult))
                then(nc.vector.tensor_scalar(klo, klo, -1.0, None, ALU.add))
                search(klo, LOW_DIGITS)
                take_above(klo)
                then(nc.vector.tensor_tensor(kth[:, :], kth[:, :], lk_ps[:, 0:1], ALU.subtract))
                nc.vector.tensor_scalar(tie, klo, cur[:, 0:1], None, ALU.is_equal).then_inc(tie_ok, 1)
                dve.wait_ge(rank_ok, 1)
                then(nc.vector.tensor_copy(col, xl_ps[:, 0:NW]))
                then(nc.vector.tensor_tensor_scan(rank, ones[:, 0:NW], col, 0.0, ALU.mult, ALU.add))
                then(nc.vector.tensor_tensor(rank, rank, col, ALU.subtract))
                then(nc.vector.tensor_tensor(rank, rank, lk_ps[:, 0:NW], ALU.add))
                then(nc.vector.scalar_tensor_tensor(out=tie, in0=rank, scalar=kth[:, 0:1], in1=tie, op0=ALU.is_lt, op1=ALU.mult))
                then(nc.vector.tensor_tensor(tie, tie, above, ALU.add))
                then(nc.vector.tensor_tensor(tie, tie, wt[:, :], ALU.mult))
                then(nc.vector.tensor_tensor(coef, coef, tie, ALU.add))
            for c, (first, count, r) in enumerate(chunks + [(NW - 2, 2, None)]):
                if r is None:
                    dve.wait_ge(yb_ok, NW)
                else:
                    dve.wait_ge(y_ld[r], 16 * (c // ROOMS + 1))
                held = yb if r is None else yin[r]
                for t in range(count):
                    w = first + t
                    last = nc.vector.scalar_tensor_tensor(out=base[:, w, :], in0=held[:, t, :], scalar=coef[:, w:w + 1], in1=base[:, w, :], op0=ALU.mult, op1=ALU.add)
                last.then_inc(out_ok, 1)


def kernel(**inputs):
    import numpy as np
    import concourse.bacc as bacc
    from concourse import mybir as my
    from concourse.bass_utils import run_bass_kernel_spmd as run

    arrays = {k: np.ascontiguousarray(v) for k, v in inputs.items() if k != "L0_ffn_attention_mask"}
    n, e = arrays["x"].shape[0], arrays["src"].shape[0]
    nw, _, ep = sizes(n, e)
    arrays["x"] = np.pad(arrays["x"], ((0, nw * P - n), (0, 0)))
    arrays["src"] = np.pad(arrays["src"], (0, ep - e))
    arrays["dst"] = np.pad(arrays["dst"], (0, ep - e), constant_values=nw * P)
    nc = bacc.Bacc("TRN2", target_bir_lowering=False, num_devices=1)
    ins = {k: nc.dram_tensor(f"in_{k}", a.shape, my.dt.from_np(a.dtype), kind="ExternalInput").ap() for k, a in arrays.items()}
    out = nc.dram_tensor("out", arrays["x"].shape, F32, kind="ExternalOutput").ap()
    build(nc, ins["x"], ins["src"], ins["dst"], ins["L0_gnn_W"], ins["L0_gnn_att_src"], ins["L0_gnn_att_dst"],
          ins["L0_gnn_bias"], ins["L0_ffn_wr"], ins["L0_ffn_br"], ins["L0_ffn_w1"], ins["L0_ffn_b1"],
          ins["L0_ffn_w2"], ins["L0_ffn_b2"], out, n, e)
    r = run(nc, [{f"in_{k}": a for k, a in arrays.items()}], core_ids=[0])
    return r.results[0]["out"][:n]
```
